# Optimizing a Trainium2 kernel written in Bass

```python
import numpy as np
import jax
import jax.numpy as jnp

def _softmax(x, axis=-1):
    return jax.nn.softmax(x, axis=axis)

def _gelu(x):
    return jax.nn.gelu(x, approximate=True)

def _silu(x):
    return jax.nn.silu(x)

def _sigmoid(x):
    return jax.nn.sigmoid(x)

def _layernorm(x, axis=-1, eps=1e-05):
    m = jnp.mean(x, axis=axis, keepdims=True)
    v = jnp.var(x, axis=axis, keepdims=True)
    return (x - m) / jnp.sqrt(v + eps)

def _scatter_add(tgt, idx, src, axis=0):
    return tgt.at[idx].add(src)

def _segment_sum(src, seg, n):
    return jax.ops.segment_sum(src, seg, n)
kernel_name = 'mk_gnn_preln_d4_gnn_r32_31c725'

def setup_inputs(seed: int=0):
    np.random.seed(seed)
    _w = jnp.asarray

    def _rec_inputs():
        import jax
        import jax.numpy as jnp
        _gk = jax.random.key(seed)
        x = -0.000202 + 1 * jax.random.normal(jax.random.fold_in(_gk, 1), (3125, 64), jnp.float32)
        src = jax.random.randint(jax.random.fold_in(_gk, 2), (100000,), 0, 3125, jnp.int32)
        dst = jnp.minimum((3125 * jax.random.uniform(jax.random.fold_in(_gk, 3), (100000,)) ** 2.0).astype(jnp.int32), 99999)
        _o = jnp.argsort(dst, stable=True)
        src = src[_o]
        dst = dst[_o]
        edge_attr_4 = -0.0005303 + 1.00001 * jax.random.normal(jax.random.fold_in(_gk, 12), (100000, 4), jnp.float32)
        edge_type_8 = jax.random.randint(jax.random.fold_in(_gk, 14), (100000,), 0, 8, jnp.int32)
        edge_weight1 = jax.random.uniform(jax.random.fold_in(_gk, 15), (100000, 1), jnp.float32, 0.0, 0.999998)
        return (x, src, dst, edge_attr_4, edge_type_8, edge_weight1)
    x, src, dst, edge_attr_4, edge_type_8, edge_weight1 = _rec_inputs()

    def _L0_gnn_setup():
        import jax, jax.numpy as jnp
        import numpy as np
        ALPHA = 0.2
        key = jax.random.key(seed)
        k1, k2, k3, k4 = jax.random.split(key, 4)
        N, E, d_in, d_out = (3125, 50000, 64, 64)
        node_features = jax.random.normal(k1, (N, d_in), dtype=jnp.float32)
        edge_index = jax.random.randint(k2, (2, E), 0, N, dtype=jnp.int64)
        W = jax.random.normal(k3, (d_in, d_out), dtype=jnp.float32) * (1.414 * np.sqrt(2.0 / (d_in + d_out)))
        a = jax.random.normal(k4, (2 * d_out,), dtype=jnp.float32) * (1.414 * np.sqrt(2.0 / (2 * d_out + 1)))
        return {'node_features': node_features, 'edge_index': edge_index, 'W': W, 'a': a}
    _L0_gnn_all = _L0_gnn_setup()
    _L0_gnn_in = {k: v for k, v in _L0_gnn_all.items() if k in ('W', 'a')}
    del _L0_gnn_all

    def _L1_gnn_setup():
        import jax, jax.numpy as jnp
        import numpy as np
        import math
        N_NODES = 50000
        N_EDGES = 15625
        HIDDEN = 64
        N_LAYERS = 4
        DELTA = 2.5
        N_AGG = 6
        N_SCALE = 3
        EPS_BN = 1e-05

        def _batchnorm(x, gamma, beta):
            mu = jnp.mean(x, axis=0)
            var = jnp.mean(jnp.square(x - mu), axis=0)
            return (x - mu) * jax.lax.rsqrt(var + EPS_BN) * gamma + beta

        def _pna_layer(h, src, dst, WM, bM, WU, bU, g_t, b_t, Wmix, bmix, g_o, b_o):
            n = h.shape[0]
            msg = jnp.concatenate([h[src], h[dst]], axis=1) @ WM + bM
            deg = jax.ops.segment_sum(jnp.ones(src.shape[0], h.dtype), dst, num_segments=n)
            denom = jnp.maximum(deg, 1.0)[:, None]
            s = jax.ops.segment_sum(msg, dst, num_segments=n)
            mean = s / denom
            mean_sq = jax.ops.segment_sum(msg * msg, dst, num_segments=n) / denom
            var = jax.nn.relu(mean_sq - mean * mean)
            std = jnp.sqrt(var + 1e-30)
            has = (deg > 0)[:, None]
            mx = jnp.where(has, jax.ops.segment_max(msg, dst, num_segments=n), 0.0)
            mn = jnp.where(has, jax.ops.segment_min(msg, dst, num_segments=n), 0.0)
            agg = jnp.concatenate([mean, mx, mn, std, var, s], axis=1)
            logD = jnp.log(deg + 1.0)[:, None]
            amp = logD / DELTA
            att = jnp.where(logD > 0, DELTA / jnp.where(logD > 0, logD, 1.0), 0.0)
            h_neigh = jnp.concatenate([agg, agg * amp, agg * att], axis=1)
            hu = jnp.concatenate([h, h_neigh], axis=1) @ WU + bU
            hu = hu * (1.0 / math.sqrt(n))
            hbn = _batchnorm(hu, g_t, b_t)
            hm = jax.nn.leaky_relu(hbn @ Wmix + bmix, 0.01)
            out = hm + h
            return jax.nn.relu(_batchnorm(out, g_o, b_o)) + h
        key = jax.random.key(seed)
        ks = jax.random.split(key, 12)
        d = HIDDEN
        L = N_LAYERS
        din_u = (N_AGG * N_SCALE + 1) * d
        return {'node_feat': jax.random.normal(ks[0], (N_NODES, d), jnp.float32), 'edge_feat': jax.random.normal(ks[1], (N_EDGES, 4), jnp.float32), 'edge_src': jax.random.randint(ks[2], (N_EDGES,), 0, N_NODES, jnp.int32), 'edge_dst': jax.random.randint(ks[3], (N_EDGES,), 0, N_NODES, jnp.int32), 'WM': jax.random.normal(ks[4], (L, 2 * d, d), jnp.float32) / math.sqrt(2 * d), 'bM': jnp.zeros((L, d), jnp.float32), 'WU': jax.random.normal(ks[5], (L, din_u, d), jnp.float32) / math.sqrt(din_u), 'bU': jnp.zeros((L, d), jnp.float32), 'gamma_t': jnp.ones((L, d), jnp.float32), 'beta_t': jnp.zeros((L, d), jnp.float32), 'Wmix': jax.random.normal(ks[6], (L, d, d), jnp.float32) / math.sqrt(d), 'bmix': jnp.zeros((L, d), jnp.float32), 'gamma_o': jnp.ones((L, d), jnp.float32), 'beta_o': jnp.zeros((L, d), jnp.float32)}
    _L1_gnn_all = _L1_gnn_setup()
    _L1_gnn_in = {k: v for k, v in _L1_gnn_all.items() if k in ('WM', 'bM', 'WU', 'bU', 'gamma_t', 'beta_t', 'Wmix', 'bmix', 'gamma_o', 'beta_o')}
    del _L1_gnn_all

    def _L2_gnn_setup():
        import jax, jax.numpy as jnp
        import numpy as np
        N, E, R, H = (50000, 25000, 8, 4)
        F_IN, HID, OUT = (64, 64, 64)
        NEG_SLOPE = 0.2

        def _glorot(key, shape):
            fan_in, fan_out = (shape[-2], shape[-1])
            std = np.sqrt(2.0 / (fan_in + fan_out)).astype(np.float32)
            return jax.random.normal(key, shape, dtype=jnp.float32) * std

        def _rgat_conv(x, src, dst, etype, W, Q, K, b):
            n = x.shape[0]
            hc = W.shape[-1]
            xw = jnp.einsum('ni,rio->rno', x, W)
            qn = jnp.einsum('rno,roh->rnh', xw, Q)
            kn = jnp.einsum('rno,roh->rnh', xw, K)
            alpha = jax.nn.leaky_relu(qn[etype, dst] + kn[etype, src], NEG_SLOPE)
            amax = jax.ops.segment_max(alpha, dst, num_segments=n)
            amax = jnp.where(jnp.isfinite(amax), amax, 0.0)
            ex = jnp.exp(alpha - amax[dst])
            denom = jax.ops.segment_sum(ex, dst, num_segments=n)
            attn = ex / (denom[dst] + 1e-16)
            out_j = xw[etype, src].reshape(-1, H, hc // H)
            agg = jax.ops.segment_sum(attn[:, :, None] * out_j, dst, num_segments=n)
            return agg.reshape(n, hc) + b
        key = jax.random.key(seed)
        ks = jax.random.split(key, 12)
        x = jax.random.normal(ks[0], (N, F_IN), dtype=jnp.float32)
        adj_t = jax.random.randint(ks[1], (2, E), 0, N, dtype=jnp.int32)
        edge_types = jax.random.randint(ks[2], (E,), 0, R, dtype=jnp.int32)
        W1 = _glorot(ks[3], (R, F_IN, HID))
        Q1 = _glorot(ks[4], (R, HID, H))
        K1 = _glorot(ks[5], (R, HID, H))
        b1 = jnp.zeros((HID,), jnp.float32)
        W2 = _glorot(ks[6], (R, HID, OUT))
        Q2 = _glorot(ks[7], (R, OUT, H))
        K2 = _glorot(ks[8], (R, OUT, H))
        b2 = jnp.zeros((OUT,), jnp.float32)
        return dict(x=x, adj_t=adj_t, edge_types=edge_types, W1=W1, Q1=Q1, K1=K1, b1=b1, W2=W2, Q2=Q2, K2=K2, b2=b2)
    _L2_gnn_all = _L2_gnn_setup()
    _L2_gnn_in = {k: v for k, v in _L2_gnn_all.items() if k in ('W1', 'Q1', 'K1', 'b1', 'W2', 'Q2', 'K2', 'b2')}
    del _L2_gnn_all

    def _L3_gnn_setup():
        import jax, jax.numpy as jnp
        import numpy as np
        N, E, R, D_IN, D_OUT = (50000, 25000, 8, 64, 64)
        key = jax.random.key(seed)
        ks = jax.random.split(key, 8)
        feat = jax.random.normal(ks[0], (N, D_IN), dtype=jnp.float32)
        edge_src = jax.random.randint(ks[1], (E,), 0, N, dtype=jnp.int32)
        edge_dst = jax.random.randint(ks[2], (E,), 0, N, dtype=jnp.int32)
        etype = jax.random.randint(ks[3], (E,), 0, R, dtype=jnp.int32)
        attention = jax.random.uniform(ks[4], (E, 1), dtype=jnp.float32)
        weight = jax.random.normal(ks[5], (R, D_IN, D_OUT), dtype=jnp.float32) * (6.0 / (D_IN + D_OUT)) ** 0.5
        h_bias = jnp.zeros((D_OUT,), dtype=jnp.float32)
        loop_weight = jax.random.normal(ks[6], (D_IN, D_OUT), dtype=jnp.float32) * (6.0 / (D_IN + D_OUT)) ** 0.5
        return {'feat': feat, 'edge_src': edge_src, 'edge_dst': edge_dst, 'etype': etype, 'attention': attention, 'weight': weight, 'h_bias': h_bias, 'loop_weight': loop_weight}
    _L3_gnn_all = _L3_gnn_setup()
    _L3_gnn_in = {k: v for k, v in _L3_gnn_all.items() if k in ('weight', 'h_bias', 'loop_weight')}
    del _L3_gnn_all
    return {'x': x, 'src': src, 'dst': dst, 'edge_attr_4': edge_attr_4, 'edge_type_8': edge_type_8, 'edge_weight1': edge_weight1, 'L0_gnn_W': _L0_gnn_in['W'], 'L0_gnn_a': _L0_gnn_in['a'], 'L1_gnn_WM': _L1_gnn_in['WM'], 'L1_gnn_bM': _L1_gnn_in['bM'], 'L1_gnn_WU': _L1_gnn_in['WU'], 'L1_gnn_bU': _L1_gnn_in['bU'], 'L1_gnn_gamma_t': _L1_gnn_in['gamma_t'], 'L1_gnn_beta_t': _L1_gnn_in['beta_t'], 'L1_gnn_Wmix': _L1_gnn_in['Wmix'], 'L1_gnn_bmix': _L1_gnn_in['bmix'], 'L1_gnn_gamma_o': _L1_gnn_in['gamma_o'], 'L1_gnn_beta_o': _L1_gnn_in['beta_o'], 'L2_gnn_W1': _L2_gnn_in['W1'], 'L2_gnn_Q1': _L2_gnn_in['Q1'], 'L2_gnn_K1': _L2_gnn_in['K1'], 'L2_gnn_b1': _L2_gnn_in['b1'], 'L2_gnn_W2': _L2_gnn_in['W2'], 'L2_gnn_Q2': _L2_gnn_in['Q2'], 'L2_gnn_K2': _L2_gnn_in['K2'], 'L2_gnn_b2': _L2_gnn_in['b2'], 'L3_gnn_weight': _L3_gnn_in['weight'], 'L3_gnn_h_bias': _L3_gnn_in['h_bias'], 'L3_gnn_loop_weight': _L3_gnn_in['loop_weight']}

def reference(x, src, dst, edge_attr_4, edge_type_8, edge_weight1, L0_gnn_W, L0_gnn_a, L1_gnn_WM, L1_gnn_bM, L1_gnn_WU, L1_gnn_bU, L1_gnn_gamma_t, L1_gnn_beta_t, L1_gnn_Wmix, L1_gnn_bmix, L1_gnn_gamma_o, L1_gnn_beta_o, L2_gnn_W1, L2_gnn_Q1, L2_gnn_K1, L2_gnn_b1, L2_gnn_W2, L2_gnn_Q2, L2_gnn_K2, L2_gnn_b2, L3_gnn_weight, L3_gnn_h_bias, L3_gnn_loop_weight):
    import jax
    import jax.numpy as jnp

    def _L0_gnn_ref(node_features, edge_index, W, a):
        import jax, jax.numpy as jnp
        import numpy as np
        ALPHA = 0.2
        N = node_features.shape[0]
        d_out = W.shape[1]
        src, tgt = (edge_index[0], edge_index[1])
        h = node_features @ W
        s_src = h @ a[:d_out]
        s_tgt = h @ a[d_out:]
        e = jax.nn.leaky_relu(s_src[src] + s_tgt[tgt], negative_slope=ALPHA)
        m = jax.ops.segment_max(e, tgt, num_segments=N)
        e_exp = jnp.exp(e - m[tgt])
        denom = jax.ops.segment_sum(e_exp, tgt, num_segments=N)
        attention = e_exp / denom[tgt]
        h_prime = jax.ops.segment_sum(h[src] * attention[:, None], tgt, num_segments=N)
        return jax.nn.elu(h_prime)

    def _L1_gnn_ref(node_feat, edge_feat, edge_src, edge_dst, WM, bM, WU, bU, gamma_t, beta_t, Wmix, bmix, gamma_o, beta_o):
        import jax, jax.numpy as jnp
        import numpy as np
        import math
        N_NODES = 50000
        N_EDGES = 15625
        HIDDEN = 64
        N_LAYERS = 4
        DELTA = 2.5
        N_AGG = 6
        N_SCALE = 3
        EPS_BN = 1e-05

        def _batchnorm(x, gamma, beta):
            mu = jnp.mean(x, axis=0)
            var = jnp.mean(jnp.square(x - mu), axis=0)
            return (x - mu) * jax.lax.rsqrt(var + EPS_BN) * gamma + beta

        def _pna_layer(h, src, dst, WM, bM, WU, bU, g_t, b_t, Wmix, bmix, g_o, b_o):
            n = h.shape[0]
            msg = jnp.concatenate([h[src], h[dst]], axis=1) @ WM + bM
            deg = jax.ops.segment_sum(jnp.ones(src.shape[0], h.dtype), dst, num_segments=n)
            denom = jnp.maximum(deg, 1.0)[:, None]
            s = jax.ops.segment_sum(msg, dst, num_segments=n)
            mean = s / denom
            mean_sq = jax.ops.segment_sum(msg * msg, dst, num_segments=n) / denom
            var = jax.nn.relu(mean_sq - mean * mean)
            std = jnp.sqrt(var + 1e-30)
            has = (deg > 0)[:, None]
            mx = jnp.where(has, jax.ops.segment_max(msg, dst, num_segments=n), 0.0)
            mn = jnp.where(has, jax.ops.segment_min(msg, dst, num_segments=n), 0.0)
            agg = jnp.concatenate([mean, mx, mn, std, var, s], axis=1)
            logD = jnp.log(deg + 1.0)[:, None]
            amp = logD / DELTA
            att = jnp.where(logD > 0, DELTA / jnp.where(logD > 0, logD, 1.0), 0.0)
            h_neigh = jnp.concatenate([agg, agg * amp, agg * att], axis=1)
            hu = jnp.concatenate([h, h_neigh], axis=1) @ WU + bU
            hu = hu * (1.0 / math.sqrt(n))
            hbn = _batchnorm(hu, g_t, b_t)
            hm = jax.nn.leaky_relu(hbn @ Wmix + bmix, 0.01)
            out = hm + h
            return jax.nn.relu(_batchnorm(out, g_o, b_o)) + h
        del edge_feat
        h = node_feat
        for i in range(N_LAYERS):
            h = _pna_layer(h, edge_src, edge_dst, WM[i], bM[i], WU[i], bU[i], gamma_t[i], beta_t[i], Wmix[i], bmix[i], gamma_o[i], beta_o[i])
        return h

    def _L2_gnn_ref(x, adj_t, edge_types, W1, Q1, K1, b1, W2, Q2, K2, b2):
        import jax, jax.numpy as jnp
        import numpy as np
        N, E, R, H = (50000, 25000, 8, 4)
        F_IN, HID, OUT = (64, 64, 64)
        NEG_SLOPE = 0.2

        def _glorot(key, shape):
            fan_in, fan_out = (shape[-2], shape[-1])
            std = np.sqrt(2.0 / (fan_in + fan_out)).astype(np.float32)
            return jax.random.normal(key, shape, dtype=jnp.float32) * std

        def _rgat_conv(x, src, dst, etype, W, Q, K, b):
            n = x.shape[0]
            hc = W.shape[-1]
            xw = jnp.einsum('ni,rio->rno', x, W)
            qn = jnp.einsum('rno,roh->rnh', xw, Q)
            kn = jnp.einsum('rno,roh->rnh', xw, K)
            alpha = jax.nn.leaky_relu(qn[etype, dst] + kn[etype, src], NEG_SLOPE)
            amax = jax.ops.segment_max(alpha, dst, num_segments=n)
            amax = jnp.where(jnp.isfinite(amax), amax, 0.0)
            ex = jnp.exp(alpha - amax[dst])
            denom = jax.ops.segment_sum(ex, dst, num_segments=n)
            attn = ex / (denom[dst] + 1e-16)
            out_j = xw[etype, src].reshape(-1, H, hc // H)
            agg = jax.ops.segment_sum(attn[:, :, None] * out_j, dst, num_segments=n)
            return agg.reshape(n, hc) + b
        src, dst = (adj_t[0], adj_t[1])
        h = _rgat_conv(x, src, dst, edge_types, W1, Q1, K1, b1)
        h = jax.nn.relu(h)
        return _rgat_conv(h, src, dst, edge_types, W2, Q2, K2, b2)

    def _L3_gnn_ref(feat, edge_src, edge_dst, etype, attention, weight, h_bias, loop_weight):
        import jax, jax.numpy as jnp
        import numpy as np
        N, E, R, D_IN, D_OUT = (50000, 25000, 8, 64, 64)
        proj = jnp.einsum('ni,rio->rno', feat, weight)
        m = (proj[etype, edge_src] + h_bias) * attention
        agg = jax.ops.segment_sum(m, edge_dst, num_segments=feat.shape[0])
        return agg + feat @ loop_weight
    edge_index = jnp.stack([src, dst])
    h = jnp.maximum(_layernorm(x, axis=-1), 0.0)
    x = x + _L0_gnn_ref(h, edge_index, L0_gnn_W, L0_gnn_a)
    h = jnp.maximum(_layernorm(x, axis=-1), 0.0)
    x = x + _L1_gnn_ref(h, edge_attr_4, src, dst, L1_gnn_WM, L1_gnn_bM, L1_gnn_WU, L1_gnn_bU, L1_gnn_gamma_t, L1_gnn_beta_t, L1_gnn_Wmix, L1_gnn_bmix, L1_gnn_gamma_o, L1_gnn_beta_o)
    h = jnp.maximum(_layernorm(x, axis=-1), 0.0)
    x = x + _L2_gnn_ref(h, edge_index, edge_type_8, L2_gnn_W1, L2_gnn_Q1, L2_gnn_K1, L2_gnn_b1, L2_gnn_W2, L2_gnn_Q2, L2_gnn_K2, L2_gnn_b2)
    h = jnp.maximum(_layernorm(x, axis=-1), 0.0)
    x = x + _L3_gnn_ref(h, src, dst, edge_type_8, edge_weight1, L3_gnn_weight, L3_gnn_h_bias, L3_gnn_loop_weight)
    return x

_drawn_inputs = setup_inputs


def setup_inputs(seed=0):
    import zlib

    import numpy as np

    out = dict(_drawn_inputs(seed))
    spreads = {'L1_gnn_bM': (0.0, 0.1),
     'L1_gnn_bU': (0.0, 2.0),
     'L1_gnn_gamma_t': (1.0, 0.2),
     'L1_gnn_beta_t': (0.0, 0.449),
     'L1_gnn_bmix': (0.0, 0.419),
     'L1_gnn_gamma_o': (1.0, 0.2),
     'L1_gnn_beta_o': (0.0, 0.1),
     'L2_gnn_b1': (0.0, 0.8),
     'L2_gnn_b2': (0.0, 1.29),
     'L3_gnn_h_bias': (0.0, 0.1)}
    factors = {'L2_gnn_W1': 5.617,
     'L2_gnn_Q1': 8.0,
     'L2_gnn_K1': 8.0,
     'L2_gnn_W2': 4.202,
     'L2_gnn_Q2': 8.0,
     'L2_gnn_K2': 8.0}
    for name, (base, spread) in spreads.items():
        noise = np.random.default_rng([zlib.crc32(name.encode()), seed]).standard_normal(out[name].shape)
        drawn = base * np.exp(spread * noise) if base else spread * noise
        out[name] = jnp.asarray(drawn.astype(out[name].dtype))
    for name, factor in factors.items():
        out[name] = (out[name] * factor).astype(out[name].dtype)
    return out
```

```python
import concourse.bass as bass
from concourse import mybir
from contextlib import ExitStack

f32, i32, bf16 = mybir.dt.float32, mybir.dt.int32, mybir.dt.bfloat16
ALU, ACT, AX = mybir.AluOpType, mybir.ActivationFunctionType, mybir.AxisListType

P = 128
N = 3125
T = 25
NP = P * T
E = 100000
B = 28
PAIRS = 14
C = 2 * PAIRS * B
EP = P * C
F = 64
REL = 8
LAYERS = 4
FULL = N // T
BIG = 1.0e30
NO_EDGE = 1 << 20
ROUND = 12582912.0


class Steps:

    def __init__(self, eng, sem):
        self.eng, self.sem, self.n = eng, sem, 0

    def add(self, ins):
        ins.then_inc(self.sem, 1)
        self.n += 1
        return self.n

    def wait(self, n=None):
        self.eng.wait_ge(self.sem, self.n if n is None else n)

    def do(self, ins):
        self.add(ins)
        self.wait()

    def reset(self):
        if self.n:
            self.wait()
            self.eng.sem_clear(self.sem)
            self.n = 0


class Attention:

    def __init__(self, heads, rels):
        self.H, self.R = heads, rels
        self.D = F // heads
        self.D1 = self.D + 1
        self.A = heads * self.D1
        self.W = self.A + heads
        self.GW = F + heads
        self.QW = rels * heads


GAT, RGAT = Attention(1, 1), Attention(4, REL)
PNA_W = 4 * F


def gnn(nc, t):
    ctx = ExitStack()
    with ctx:
        def sb(name, shape, dt=f32):
            return ctx.enter_context(nc.sbuf_tensor(name, shape, dt))

        def sem(name):
            return ctx.enter_context(nc.semaphore(name))

        def dram(name, shape, dt=f32):
            return nc.dram_tensor(name, shape, dt).ap()

        gat_table = dram("gat_table", (NP, GAT.GW))
        pna_table = dram("pna_table", (NP, F))
        rgat_table = dram("rgat_table", (NP * REL, RGAT.GW))
        rgcn_table = dram("rgcn_table", (NP * REL, F))
        gat_q = dram("gat_q", (NP, GAT.QW))
        rgat_q = dram("rgat_q", (NP, RGAT.QW))
        gat_spread = dram("gat_spread", (EP, GAT.QW))
        rgat_spread = dram("rgat_spread", (EP, RGAT.QW))
        runs = {w: dram(f"runs{w}", (EP, w)) for w in (GAT.W, PNA_W, RGAT.W, F)}
        carry = {w: dram(f"carry{w}", (P + 1, w)) for w in (GAT.W, PNA_W, RGAT.W, F)}

        X = sb("X", [P, T, F])
        Hn = sb("Hn", [P, T, F])
        Bn = sb("Bn", [P, T, F])
        Y = sb("Y", [P, T, F])
        Z = sb("Z", [P, T, F])
        gath = sb("gath", [P, 2, B, F + 4])
        msgs = sb("msgs", [P, 2 * B * 192])
        rows = sb("rows", [P, 2 * B * PNA_W])
        qx = sb("qx", [P, 2, B, 32])
        start = sb("start", [P, C])
        cont = sb("cont", [P, C])
        srci = sb("srci", [P, C], i32)
        reli = sb("reli", [P, C], i32)
        etyf = sb("etyf", [P, C])
        wgt = sb("wgt", [P, C])
        idx_now = sb("idx_now", [P, 2, B], i32)
        cont_now = sb("cont_now", [P, B])
        negs_now = sb("negs_now", [P, B])
        ety_now = sb("ety_now", [P, B])
        onehot = sb("onehot", [P, B, REL])
        qsel = sb("qsel", [P, B, 4, REL])
        score = sb("score", [P, B, 4])
        expo = sb("expo", [P, B, 4])
        maxrun = sb("maxrun", [P, 4, 1 + B])
        decay = sb("decay", [P, 4, B])
        qlast = sb("qlast", [P, 32])
        QN = sb("QN", [P, T, 32])
        tab = sb("tab", [P, 2, REL * (F + 4)])
        XT = sb("XT", [P, 2, 512])
        ident = sb("ident", [P, P])
        upper = sb("upper", [P, P])
        realp = sb("realp", [P, P])
        act_ = sb("contT", [P, P])
        negT = sb("negT", [P, P])
        cA = sb("cA", [P, P + 1])
        cB = sb("cB", [P, P])
        cC = sb("cC", [P, P])
        cD = sb("cD", [P, P])
        cS = sb("cS", [P, PNA_W])
        deg = sb("deg", [P, T])
        has = sb("has", [P, T])
        rden = sb("rden", [P, T])
        hrden = sb("hrden", [P, T])
        amp = sb("amp", [P, T])
        att = sb("att", [P, T])
        s1 = sb("s1", [P, T])
        s2 = sb("s2", [P, T])
        s3 = sb("s3", [P, T])
        s4 = sb("s4", [P, T])
        hw1 = sb("hw1", [P, T, 4])
        hw2 = sb("hw2", [P, T, 4])
        end_i = sb("end_i", [P, T], i32)
        carry_i = sb("carry_i", [P, T], i32)
        start_i = sb("start_i", [P, T], i32)
        dst0_i = sb("dst0_i", [P, 1], i32)
        col1 = sb("col1", [P, 1])
        col2 = sb("col2", [P, 1])
        iota_q = sb("iota_q", [P, P], bf16)
        iota_i = sb("iota_i", [P, P], i32)
        iota_f = sb("iota_f", [P, P])
        fa = sb("fa", [P, F])
        fb = sb("fb", [P, F])
        fc = sb("fc", [P, F])
        wrel = sb("wrel", [F, REL * F + F])
        wk = sb("wk", [F, REL, 8])
        wT = sb("wT", [F, F])
        wm = sb("wm", [F, 2 * F])
        wu0 = sb("wu0", [F, F])
        wu = sb("wu", [P, 3, 3, F])
        wmix = sb("wmix", [F, F])
        par = sb("par", [P, 7, F])

        dsti = msgs[:, 0:C].bitcast(i32)
        prevd = msgs[:, C:2 * C].bitcast(i32)
        dstf = msgs[:, 2 * C:3 * C]
        prevf = msgs[:, 3 * C:4 * C]
        qf = msgs[:, 4 * C:5 * C]
        tf = msgs[:, 5 * C:6 * C]
        qb = rows[:, 0:C // 2].bitcast(bf16)
        tb = rows[:, C // 2:C].bitcast(bf16)
        oh_q = rows[:, C:C + B * P].bitcast(bf16).rearrange("p (h j q) -> p h j q", h=2, j=B)
        oh_t = rows[:, C + B * P:C + B * P + B * T].bitcast(bf16).rearrange("p (h j q) -> p h j q", h=2, j=B)
        zeros = rows[:, 8192:8192 + 4096]
        feats = msgs[:, 0:T * 6 * F].rearrange("p (t w) -> p t w", t=T)

        def run_rows(w):
            return rows[:, 0:2 * B * w].rearrange("p (h j w) -> p h j w", h=2, j=B)

        def node_rows(w):
            return (rows[:, 0:T * w].rearrange("p (t w) -> p t w", t=T),
                    rows[:, T * PNA_W:T * PNA_W + T * w].rearrange("p (t w) -> p t w", t=T))

        def messages(w):
            return msgs[:, 0:2 * B * w].rearrange("p (h j w) -> p h j w", h=2, j=B)

        psT = [ctx.enter_context(nc.psum_tensor(f"psT{k}", [P, 512], f32)) for k in range(2)]
        psO = [ctx.enter_context(nc.psum_tensor(f"psO{k}", [P, 512], f32)) for k in range(2)]
        psS = [ctx.enter_context(nc.psum_tensor(f"psS{k}", [P, 512], f32)) for k in range(2)]
        psR = ctx.enter_context(nc.psum_tensor("psR", [P, 512], f32))

        loads_in = sem("loads_in")
        transposed = sem("transposed")
        xt_ready = sem("xt_ready")
        product_done = sem("product_done")
        evacuated = sem("evacuated")
        tab_stored = [sem("tab_stored0"), sem("tab_stored1")]
        rows_free = sem("rows_free")
        msgs_ready = sem("msgs_ready")
        scores_ready = sem("scores_ready")
        block_done = [sem("block_done0"), sem("block_done1")]
        runs_stored = [sem("runs_stored0"), sem("runs_stored1")]
        runs_free = [sem("runs_free0"), sem("runs_free1")]
        spread_in = [sem("spread_in0"), sem("spread_in1")]
        idx_ready = sem("idx_ready")
        carry_ready = sem("carry_ready")
        carry_stored = sem("carry_stored")
        table_stored = sem("table_stored")
        node_ready = sem("node_ready")
        sum_ready = sem("sum_ready")
        sum_done = sem("sum_done")
        operands_ready = sem("operands_ready")
        act_asked = sem("act_asked")
        act_done = sem("act_done")
        gathering = sem("gathering")
        oh_ready = sem("oh_ready")
        oh_used = sem("oh_used")
        stage_sems = [loads_in, transposed, xt_ready, product_done, evacuated, *tab_stored, rows_free, msgs_ready,
                      scores_ready, *block_done, *runs_stored, *runs_free, *spread_in, idx_ready, carry_ready,
                      carry_stored, table_stored, node_ready, sum_ready, sum_done, operands_ready, act_asked, act_done, gathering,
                      oh_ready, oh_used]
        names = ("gat", "pna", "rgat1", "rgat2", "rgcn")
        rows_in = {k: [sem(f"{k}_rows_in{h}") for h in range(2)] for k in names}
        nodes_in = {k: sem(f"{k}_nodes_in") for k in names}
        spread_out = {k: sem(f"{k}_spread_out") for k in ("gat", "rgat1", "rgat2")}
        q_first_in = {k: sem(f"{k}_q_first_in") for k in ("gat", "rgat1", "rgat2")}
        arrived = sem("arrived")
        go = {k: sem(f"go_{k}") for k in ("pe", "act", "dve", "pool")}
        dve_steps, act_steps, pool_steps = sem("dve_steps"), sem("act_steps"), sem("pool_steps")

        def meet(eng, who):
            eng.sem_inc(arrived, 1)
            eng.wait_ge(go[who], 1)
            eng.sem_clear(go[who])

        def meet_sp(sp):
            sp.wait_ge(arrived, 4)
            sp.sem_clear(arrived)
            for s in stage_sems:
                sp.sem_clear(s)
            for s in go.values():
                sp.sem_inc(s, 1)

        def cols(b, h):
            return bass.ds((b * 2 + h) * B, B)

        def bc(ap, shape):
            return ap.to_broadcast(shape)

        block = ctx.enter_context(nc.Block())

        @block.sync
        def _(sp):
            def load(dst, src, signal=loads_in):
                sp.dma_start(dst, src).then_inc(signal, 16)

            def store_runs(w, h, b):
                sp.wait_ge(block_done[h], b + 1)
                sp.dma_start(runs[w].rearrange("(p c) w -> p c w", p=P)[:, cols(b, h), :],
                             run_rows(w)[:, h, :, :]).then_inc(runs_stored[h], 16)

            def edge_pass(w, spread=None, qw=0):
                sp.sem_inc(runs_free[0], 1)
                sp.sem_inc(runs_free[1], 1)
                if spread is not None:
                    sv = spread.rearrange("(p c) w -> p c w", p=P)
                    qv = qx[:, :, :, :].rearrange("p h j w -> p (h j w)")[:, 0:2 * B * qw].rearrange(
                        "p (h j w) -> p h j w", h=2, j=B)
                    for h in range(2):
                        sp.dma_start(qv[:, h], sv[:, h * B:h * B + B, :]).then_inc(spread_in[h], 16)
                with sp.Fori(0, PAIRS - 1) as b:
                    for h in range(2):
                        store_runs(w, h, b)
                        if spread is not None:
                            sp.dma_start(qv[:, h], sv[:, cols(b + 1, h), :]).then_inc(spread_in[h], 16)
                        sp.wait_ge(runs_stored[h], b * 16 + 16)
                        sp.sem_inc(runs_free[h], 1)
                for h in range(2):
                    store_runs(w, h, PAIRS - 1)
                    sp.wait_ge(runs_stored[h], PAIRS * 16)
                sp.wait_ge(carry_ready, 1)
                sp.dma_start(carry[w][0:P, :], cS[:, 0:w]).then_inc(carry_stored, 16)
                sp.wait_ge(carry_stored, 16)
                meet_sp(sp)

            def store_node_tables(table, w, bank_q=None, qw=0):
                tv = table.rearrange("(p t r) w -> p t (r w)", p=P, t=T)
                for s in range(T):
                    sp.wait_ge(evacuated, s + 1)
                    sp.dma_start(tv[:, s, :], tab[:, s % 2, 0:REL * w]).then_inc(tab_stored[s % 2], 16)
                for k in range(2):
                    sp.wait_ge(tab_stored[k], 16 * len(range(k, T, 2)))
                if bank_q is not None:
                    sp.dma_start(bank_q.rearrange("(p t) w -> p t w", p=P), QN[:, :, 0:qw]).then_inc(table_stored, 16)
                    sp.wait_ge(table_stored, 16)
                meet_sp(sp)

            def broadcast_row(k, row):
                load(par[:, k, :], row.partition_broadcast(P))

            flat = t["dst"]
            load(dsti, flat[1:1 + EP].rearrange("(p c) -> p c", p=P))
            load(prevd, flat[0:EP].rearrange("(p c) -> p c", p=P))
            load(srci[:, :], t["src"])
            load(reli[:, :], t["edge_type_8"])
            load(wgt[:, :], t["edge_weight1"])
            load(X[:, :, :], t["x"].rearrange("(p t) f -> p t f", p=P))
            load(wrel[:, 0:F], t["L0_gnn_W"])
            for k in range(2):
                load(wk[:, 0, k:k + 1], t["L0_gnn_a"][k * F:(k + 1) * F].unsqueeze(1))
            sp.wait_ge(node_ready, 1)
            zr = rgat_spread.rearrange("(p c) w -> p (c w)", p=P)
            for k in range(0, C * 32, 3584):
                sp.dma_start(zr[:, k:k + 3584], zeros[:, 0:3584]).then_inc(table_stored, 16)
            sp.dma_start(gat_spread.rearrange("(p c) w -> p (c w)", p=P), zeros[:, 0:C]).then_inc(table_stored, 16)
            sp.wait_ge(table_stored, 16 * (C * 32 // 3584 + 1))
            for n, (w, a, b) in enumerate(((GAT.W, GAT.A, GAT.W), (PNA_W, 0, 2 * F), (RGAT.W, RGAT.A, RGAT.W), (F, 0, 0))):
                if b > a:
                    sp.dma_start(carry[w][P:P + 1, a:b], cS[0:1, 0:b - a]).then_inc(carry_stored, 16)
                lo, hi = (0, a) if a else (b, w)
                sp.dma_start(carry[w][P:P + 1, lo:hi], zeros[0:1, 0:hi - lo]).then_inc(carry_stored, 16)
            sp.wait_ge(carry_stored, 16 * 7)
            meet_sp(sp)

            sp.wait_ge(node_ready, 1)
            sp.dma_start(gat_table.rearrange("(p t) w -> p t w", p=P), msgs[:, 0:T * GAT.GW].rearrange(
                "p (t w) -> p t w", t=T)).then_inc(table_stored, 16)
            sp.dma_start(gat_q.rearrange("(p t) w -> p (t w)", p=P), s4[:, :]).then_inc(table_stored, 16)
            sp.wait_ge(table_stored, 32)
            meet_sp(sp)
            meet_sp(sp)
            edge_pass(GAT.W, gat_spread, GAT.QW)
            meet_sp(sp)

            with sp.Fori(0, LAYERS) as layer:
                one = bass.ds(layer, 1)
                wmv = t["L1_gnn_WM"][one, :, :]
                load(wm[:, 0:F], wmv[:, 0:F, :].rearrange("l f n -> (l f) n"))
                load(wm[:, F:2 * F], wmv[:, F:2 * F, :].rearrange("l f n -> (l f) n"))
                wuv = t["L1_gnn_WU"][one, :, :].rearrange("l r n -> (l r) n")
                load(wu0[:, :], wuv[0:F, :])
                for g in range(3):
                    load(wu[:, :, g, :], wuv[F + g * 6 * F:F + (g + 1) * 6 * F, :].rearrange("(k p) n -> p k n", p=P))
                load(wmix[:, :], t["L1_gnn_Wmix"][one, :, :].rearrange("l f n -> (l f) n"))
                for k, nm in enumerate(("bM", "bU", "gamma_t", "beta_t", "bmix", "gamma_o", "beta_o")):
                    load(par[:, k, :], t["L1_gnn_" + nm][one, :].rearrange("l f -> (l f)").partition_broadcast(P))
                sp.wait_ge(node_ready, 1)
                sp.dma_start(pna_table.rearrange("(p t) w -> p t w", p=P), Y[:, :, :]).then_inc(table_stored, 16)
                sp.wait_ge(table_stored, 16)
                meet_sp(sp)
                edge_pass(PNA_W)
                meet_sp(sp)

            for k in ("1", "2"):
                load(wrel[:, 0:REL * F].rearrange("f (r n) -> f r n", r=REL), t["L2_gnn_W" + k].rearrange("r f n -> f r n"))
                load(wk[:, :, 0:4], t["L2_gnn_K" + k].rearrange("r f n -> f r n"))
                load(wk[:, :, 4:8], t["L2_gnn_Q" + k].rearrange("r f n -> f r n"))
                broadcast_row(0, t["L2_gnn_b" + k])
                store_node_tables(rgat_table, RGAT.GW, rgat_q, RGAT.QW)
                meet_sp(sp)
                edge_pass(RGAT.W, rgat_spread, RGAT.QW)
                meet_sp(sp)

            load(wrel[:, 0:REL * F].rearrange("f (r n) -> f r n", r=REL), t["L3_gnn_weight"].rearrange("r f n -> f r n"))
            load(wrel[:, REL * F:], t["L3_gnn_loop_weight"])
            broadcast_row(0, t["L3_gnn_h_bias"])
            store_node_tables(rgcn_table, F)
            edge_pass(F)
            sp.wait_ge(node_ready, 1)
            sp.dma_start(t["out"].rearrange("(p t) f -> p t f", p=P), X[:, :, :]).then_inc(table_stored, 16)
            sp.wait_ge(table_stored, 16)

        @block.gpsimd
        def _(pool):
            steps = Steps(pool, pool_steps)

            def edge_pass(w, table, idx, rows_of, landed, key, bound, base=0):
                with pool.Fori(0, PAIRS) as b:
                    for h in range(2):
                        pool.wait_ge(rows_free, b * 2 + h + 1)
                        pool.sem_inc(gathering, 1)
                        nc.gpsimd.tensor_copy(idx_now[:, h, :], idx[:, cols(b, h)]).then_inc(idx_ready, 1)
                        pool.wait_ge(idx_ready, b * 2 + h + 1)
                        pool.sem_inc(gathering, 1)
                        for j in range(B):
                            pool.indirect_dma_start(rows_of(h, j), None, table, bass.IndirectOffsetOnAxis(
                                ap=idx_now[:, h, j:j + 1], axis=0), bounds_check=bound, oob_is_err=False
                            ).then_inc(landed[h], 16)
                meet(pool, "pool")
                ns, ncr = node_rows(w)
                for s in range(T):
                    pool.indirect_dma_start(ns[:, s, :], None, runs[w], bass.IndirectOffsetOnAxis(
                        ap=end_i[:, s:s + 1], axis=0), bounds_check=EP - 1, oob_is_err=False).then_inc(nodes_in[key], 16)
                    pool.indirect_dma_start(ncr[:, s, :], None, carry[w], bass.IndirectOffsetOnAxis(
                        ap=carry_i[:, s:s + 1], axis=0), bounds_check=P, oob_is_err=False).then_inc(nodes_in[key], 16)

            def spread(bank, q_of, qtable, qw, key):
                for s in range(T):
                    pool.indirect_dma_start(bank, bass.IndirectOffsetOnAxis(ap=start_i[:, s:s + 1], axis=0), q_of(s),
                                            None, bounds_check=EP - 1, oob_is_err=False).then_inc(spread_out[key], 16)
                pool.indirect_dma_start(qlast[:, 0:qw], None, qtable, bass.IndirectOffsetOnAxis(
                    ap=dst0_i[:, 0:1], axis=0), bounds_check=NP - 1, oob_is_err=False).then_inc(q_first_in[key], 16)
                pool.wait_ge(spread_out[key], 16 * T)
                pool.wait_ge(q_first_in[key], 16)

            steps.do(nc.gpsimd.iota(iota_i[:, :], pattern=[[1, P]], base=0, channel_multiplier=0))
            steps.do(nc.gpsimd.memset(ident[:, :], 0.0))
            steps.do(nc.gpsimd.affine_select(out=ident[:, :], in_=ident[:, :], compare_op=ALU.not_equal, fill=1.0,
                                             base=0, pattern=[[-1, P]], channel_multiplier=1))
            steps.do(nc.gpsimd.memset(upper[:, :], 1.0))
            steps.do(nc.gpsimd.affine_select(out=upper[:, :], in_=upper[:, :], compare_op=ALU.is_gt, fill=0.0,
                                             base=0, pattern=[[1, P]], channel_multiplier=-1))
            steps.do(nc.gpsimd.memset(realp[:, :], 1.0))
            steps.do(nc.gpsimd.affine_select(out=realp[:, :], in_=realp[:, :], compare_op=ALU.is_gt, fill=0.0,
                                             base=FULL, pattern=[[0, P]], channel_multiplier=-1))
            pool.sem_inc(idx_ready, 1)
            meet(pool, "pool")
            meet(pool, "pool")
            spread(gat_spread, lambda s: s4[:, s:s + 1], gat_q, 1, "gat")
            meet(pool, "pool")
            edge_pass(GAT.W, gat_table, srci, lambda h, j: gath[:, h, j, 0:GAT.GW], rows_in["gat"], "gat", NP - 1)
            meet(pool, "pool")
            with pool.Fori(0, LAYERS) as layer:
                meet(pool, "pool")
                edge_pass(PNA_W, pna_table, srci, lambda h, j: messages(192)[:, h, j, F:2 * F], rows_in["pna"], "pna",
                          NP - 1)
                meet(pool, "pool")
            for k in ("rgat1", "rgat2"):
                meet(pool, "pool")
                spread(rgat_spread, lambda s: QN[:, s, :], rgat_q, RGAT.QW, k)
                meet(pool, "pool")
                edge_pass(RGAT.W, rgat_table, reli, lambda h, j: gath[:, h, j, :], rows_in[k], k, NP * REL - 1)
                meet(pool, "pool")
            meet(pool, "pool")
            edge_pass(F, rgcn_table, reli, lambda h, j: gath[:, h, j, 0:F], rows_in["rgcn"], "rgcn", NP * REL - 1)

        @block.tensor
        def _(pe):
            def node_products(src, rhs, n, rhs2=None, n2=0):
                for s in range(T + 1):
                    if s < T:
                        if s >= 2:
                            pe.wait_ge(xt_ready, s - 1)
                        nc.tensor.transpose(psT[s % 2][0:F, 0:P], src[:, s, :], ident[:, :]).then_inc(transposed, 1)
                    if s >= 1:
                        u = s - 1
                        pe.wait_ge(xt_ready, u + 1)
                        if u >= 2:
                            pe.wait_ge(evacuated, u - 1)
                        last = nc.tensor.matmul(psO[u % 2][:, 0:n], XT[0:F, u % 2, 0:P], rhs, start=True, stop=True)
                        if n2:
                            last = nc.tensor.matmul(psS[u % 2][:, 0:n2], XT[0:F, u % 2, 0:P], rhs2, start=True, stop=True)
                        last.then_inc(product_done, 1)

            def total(k):
                pe.wait_ge(sum_ready, k + 1)
                nc.tensor.matmul(psR[:, 0:F], realp[:, :], fa[:, :], start=True, stop=True).then_inc(sum_done, 1)

            def carry_attention(a):
                pe.wait_ge(sum_ready, 1)
                nc.tensor.transpose(psT[0][0:a.A, 0:P], cS[:, 0:a.A], ident[:, :])
                nc.tensor.transpose(psT[0][0:a.A, P:2 * P], run_rows(a.W)[:, 1, B - 1, 0:a.A],
                                    ident[:, :]).then_inc(sum_done, 1)
                pe.wait_ge(sum_ready, 2)
                nc.tensor.transpose(psO[0][:, 0:a.A], cD[0:a.A, :], ident[0:a.A, 0:a.A])
                nc.tensor.transpose(psO[0][:, P:P + a.A], cA[0:a.A, 1:P + 1], ident[0:a.A, 0:a.A]).then_inc(sum_done, 1)

            pe.wait_ge(idx_ready, 1)
            pe.wait_ge(node_ready, 1)
            nc.tensor.matmul(psO[0][:, 0:T], zeros[:, 0:P // 2].bitcast(bf16), zeros[:, 0:32].bitcast(bf16)[:, 0:T],
                             start=True, stop=False)
            with pe.Fori(0, PAIRS) as b:
                for h in range(2):
                    pe.wait_ge(oh_ready, b * 2 + h + 1)
                    for j in range(B):
                        last = nc.tensor.matmul(psO[0][:, 0:T], oh_q[:, h, j, :], oh_t[:, h, j, :], start=False,
                                                stop=False)
                    last.then_inc(oh_used, 1)
            nc.tensor.matmul(psO[0][:, 0:T], zeros[:, 0:P // 2].bitcast(bf16), zeros[:, 0:32].bitcast(bf16)[:, 0:T],
                             start=False, stop=True).then_inc(sum_done, 1)
            pe.wait_ge(sum_ready, 1)
            nc.tensor.matmul(psS[0][:, 0:1], upper[:, :], col1[:, :], start=True, stop=True).then_inc(sum_done, 1)
            pe.wait_ge(sum_ready, 2)
            nc.tensor.matmul(psS[1][:, 0:P], cB[:, :], ident[:, :], start=True, stop=True).then_inc(sum_done, 1)
            meet(pe, "pe")

            nc.tensor.transpose(psR[0:F, 0:F], wrel[:, 0:F], ident[0:F, 0:F]).then_inc(sum_done, 1)
            pe.wait_ge(sum_ready, 1)
            nc.tensor.matmul(psR[0:F, F:F + 2], wT[:, :], wk[:, 0, 0:2], start=True, stop=True).then_inc(sum_done, 1)
            pe.wait_ge(operands_ready, 1)
            node_products(Hn, wrel[:, 0:F + 2], F + 2)
            meet(pe, "pe")
            meet(pe, "pe")
            carry_attention(GAT)
            meet(pe, "pe")
            meet(pe, "pe")

            with pe.Fori(0, LAYERS) as layer:
                pe.wait_ge(operands_ready, 1)
                node_products(Hn, wm[:, :], 2 * F)
                meet(pe, "pe")
                pe.wait_ge(sum_ready, 1)
                for k in range(2):
                    last = nc.tensor.transpose(psT[k][:, 0:P], run_rows(PNA_W)[:, 1, B - 1, k * P:(k + 1) * P], ident[:, :])
                last.then_inc(sum_done, 1)
                pe.wait_ge(sum_ready, 2)
                nc.tensor.transpose(psO[0][:, 0:P], cA[:, 1:P + 1], ident[:, :])
                nc.tensor.transpose(psO[0][:, P:2 * P], cD[:, :], ident[:, :]).then_inc(sum_done, 1)
                meet(pe, "pe")
                pe.wait_ge(operands_ready, 1)
                for s in range(T + 1):
                    if s < T:
                        if s >= 2:
                            pe.wait_ge(xt_ready, s - 1)
                        for k in range(3):
                            nc.tensor.transpose(psT[s % 2][:, k * P:(k + 1) * P], feats[:, s, k * P:(k + 1) * P], ident[:, :])
                        nc.tensor.transpose(psT[s % 2][0:F, 3 * P:4 * P], Hn[:, s, :], ident[:, :]).then_inc(transposed, 1)
                    if s >= 1:
                        u = s - 1
                        pe.wait_ge(xt_ready, u + 1)
                        if u >= 2:
                            pe.wait_ge(evacuated, u - 1)
                        for k in range(3):
                            nc.tensor.matmul(psO[u % 2][:, 0:3 * F], XT[:, u % 2, k * P:(k + 1) * P],
                                             wu[:, k, :, :].rearrange("p g n -> p (g n)"), start=(k == 0), stop=False)
                        nc.tensor.matmul(psO[u % 2][:, 0:F], XT[0:F, u % 2, 3 * P:4 * P], wu0[:, :], start=False,
                                         stop=True).then_inc(product_done, 1)
                total(0)
                total(1)
                pe.wait_ge(operands_ready, 2)
                for s in range(T + 1):
                    if s < T:
                        pe.wait_ge(xt_ready, T + s - 1)
                        nc.tensor.transpose(psT[s % 2][0:F, 0:P], Y[:, s, :], ident[:, :]).then_inc(transposed, 1)
                    if s >= 1:
                        u = s - 1
                        pe.wait_ge(xt_ready, T + u + 1)
                        pe.wait_ge(evacuated, T + u - 1)
                        nc.tensor.matmul(psO[u % 2][:, 0:F], XT[0:F, u % 2, 0:P], wmix[:, :], start=True,
                                         stop=True).then_inc(product_done, 1)
                total(2)
                total(3)
                meet(pe, "pe")

            for k in range(2):
                for r in range(REL):
                    pe.wait_ge(sum_ready, 2 * r + 1)
                    nc.tensor.transpose(psR[0:F, 0:F], wrel[:, r * F:(r + 1) * F], ident[0:F, 0:F]).then_inc(sum_done, 1)
                    pe.wait_ge(sum_ready, 2 * r + 2)
                    nc.tensor.matmul(psS[0][0:F, 0:8], wT[:, :], wk[:, r, :], start=True, stop=True).then_inc(sum_done, 1)
                pe.wait_ge(operands_ready, 1)
                node_products(Hn, wrel[:, 0:REL * F], REL * F, wrel[:, REL * F:], F)
                meet(pe, "pe")
                meet(pe, "pe")
                carry_attention(RGAT)
                meet(pe, "pe")
                meet(pe, "pe")

            pe.wait_ge(operands_ready, 1)
            node_products(Hn, wrel[:, 0:REL * F], REL * F, wrel[:, REL * F:], F)
            meet(pe, "pe")
            pe.wait_ge(sum_ready, 1)
            nc.tensor.transpose(psT[0][0:F, 0:P], run_rows(F)[:, 1, B - 1, :], ident[:, :]).then_inc(sum_done, 1)
            pe.wait_ge(sum_ready, 2)
            nc.tensor.transpose(psO[0][:, 0:F], cD[0:F, :], ident[0:F, 0:F]).then_inc(sum_done, 1)
            meet(pe, "pe")

        @block.scalar
        def _(act):
            asked = [0]

            def func(out, in_, fn, scale=1.0):
                asked[0] += 1
                act.wait_ge(act_asked, asked[0])
                nc.scalar.activation(out, in_, fn, scale=scale).then_inc(act_done, 1)

            def end():
                asked[0] = 0
                meet(act, "act")

            def node_transposes(base=0):
                for s in range(T):
                    act.wait_ge(transposed, base + s + 1)
                    if base + s >= 2:
                        act.wait_ge(product_done, base + s - 1)
                    nc.scalar.copy(XT[0:F, s % 2, 0:P], psT[s % 2][0:F, 0:P]).then_inc(xt_ready, 1)

            def layer_norm():
                func(s1[:, :], s2[:, :], ACT.Sqrt)

            def edge_attention(a):
                mv = messages(a.A)
                with act.Fori(0, PAIRS) as b:
                    for h in range(2):
                        act.wait_ge(scores_ready, b * 2 + h + 1)
                        nc.scalar.activation(decay[:, 0:a.H, :], decay[:, 0:a.H, :], ACT.Exp).then_inc(msgs_ready, 1)
                        nc.scalar.activation(mv[:, h].rearrange("p j (k d) -> p j k d", k=a.H)[:, :, :, a.D],
                                             expo[:, :, 0:a.H], ACT.Exp).then_inc(msgs_ready, 1)
                func(cB[0:a.A, :], cB[0:a.A, :], ACT.Exp)
                func(cC[0:a.A, :], cC[0:a.A, :], ACT.Exp)
                end()
                func(hw1[:, :, 0:a.H], hw1[:, :, 0:a.H], ACT.Exp)
                func(hw2[:, :, 0:a.H], hw2[:, :, 0:a.H], ACT.Exp)

            func(s2[:, :], s1[:, :], ACT.Ln)
            layer_norm()
            end()
            node_transposes()
            end()
            end()
            edge_attention(GAT)
            func(Z[:, :, :], Z[:, :, :], ACT.Exp)
            layer_norm()
            end()
            with act.Fori(0, LAYERS) as layer:
                node_transposes()
                end()
                mv = messages(192)
                with act.Fori(0, PAIRS) as b:
                    for h in range(2):
                        act.wait_ge(rows_in["pna"][h], (layer * PAIRS + b + 1) * 16 * B)
                        nc.scalar.activation(mv[:, h, :, 0:F], mv[:, h, :, F:2 * F], ACT.Copy,
                                             scale=-1.0).then_inc(msgs_ready, 1)
                        nc.scalar.activation(mv[:, h, :, 2 * F:], mv[:, h, :, F:2 * F], ACT.Square).then_inc(msgs_ready, 1)
                end()
                func(feats[:, :, 3 * F:4 * F], Y[:, :, :], ACT.Sqrt)
                for s in range(T):
                    act.wait_ge(transposed, s + 1)
                    if s >= 2:
                        act.wait_ge(product_done, s - 1)
                    nc.scalar.copy(XT[:, s % 2, 0:3 * P], psT[s % 2][:, 0:3 * P])
                    nc.scalar.copy(XT[0:F, s % 2, 3 * P:], psT[s % 2][0:F, 3 * P:]).then_inc(xt_ready, 1)
                func(fb[:, :], fc[:, :], ACT.Sqrt)
                node_transposes(T)
                func(fb[:, :], fc[:, :], ACT.Sqrt)
                end()
            for k in range(2):
                if k == 0:
                    layer_norm()
                node_transposes()
                end()
                end()
                edge_attention(RGAT)
                if k:
                    layer_norm()
                end()
            node_transposes()
            end()
            end()

        @block.vector
        def _(dve):
            st = Steps(dve, dve_steps)
            V = nc.vector
            asked = [0]
            sums = [0]

            def tt(out, a, b, op):
                st.do(V.tensor_tensor(out, a, b, op))

            def ts(out, a, x, op, y=None, op1=None):
                if y is None:
                    st.do(V.tensor_scalar(out, a, x, None, op))
                else:
                    st.do(V.tensor_scalar(out, a, x, y, op, op1))

            def copy(out, a):
                st.do(V.tensor_copy(out, a))

            def ask(wait=True):
                asked[0] += 1
                dve.sem_inc(act_asked, 1)
                if wait:
                    dve.wait_ge(act_done, asked[0])

            def ask_pe():
                sums[0] += 1
                dve.sem_inc(sum_ready, 1)

            def end():
                st.reset()
                asked[0] = sums[0] = 0
                meet(dve, "dve")

            def over_t(x, w=F):
                return bc(x.unsqueeze(2), [P, T, w])

            def over_f(x):
                return bc(x.unsqueeze(1), [P, T, F])

            def layer_norm():
                st.do(V.tensor_reduce(s3[:, :], X[:, :, :], AX.X, ALU.add))
                ts(s3[:, :], s3[:, :], 1.0 / F, ALU.mult)
                tt(Hn[:, :, :], X[:, :, :], over_t(s3[:, :]), ALU.subtract)
                tt(Z[:, :, :], Hn[:, :, :], Hn[:, :, :], ALU.mult)
                st.do(V.tensor_reduce(s2[:, :], Z[:, :, :], AX.X, ALU.add))
                ts(s2[:, :], s2[:, :], 1.0 / F, ALU.mult, 1e-5, ALU.add)
                ask()
                st.do(V.reciprocal(s3[:, :], s1[:, :]))
                tt(Hn[:, :, :], Hn[:, :, :], over_t(s3[:, :]), ALU.mult)
                ts(Hn[:, :, :], Hn[:, :, :], 0.0, ALU.max)

            def batch_norm(buf, gamma, beta):
                def mean(of):
                    st.do(V.tensor_reduce(fa[:, :], of.rearrange("p t f -> p f t"), AX.X, ALU.add))
                    ask_pe()
                    dve.wait_ge(sum_done, sums[0])

                mean(buf)
                ts(fb[:, :], psR[:, 0:F], 1.0 / N, ALU.mult)
                tt(buf, buf, over_f(fb[:, :]), ALU.subtract)
                tt(Z[:, :, :], buf, buf, ALU.mult)
                mean(Z[:, :, :])
                ts(fc[:, :], psR[:, 0:F], 1.0 / N, ALU.mult, 1e-5, ALU.add)
                ask()
                st.do(V.reciprocal(fb[:, :], fb[:, :]))
                tt(fb[:, :], fb[:, :], gamma, ALU.mult)
                tt(buf, buf, over_f(fb[:, :]), ALU.mult)
                tt(buf, buf, over_f(beta), ALU.add)

            def block_masks(b, h):
                st.add(V.tensor_copy(cont_now[:, :], cont[:, cols(b, h)]))
                st.add(V.tensor_scalar(negs_now[:, :], start[:, cols(b, h)], -BIG, None, ALU.mult))

            def finish_block(h):
                st.wait()
                dve.sem_inc(rows_free, 1)
                dve.sem_inc(block_done[h], 1)
                st.reset()

            def scan(out, data0, data1, initial, op0, op1):
                st.do(V.tensor_tensor_scan(out, data0, data1, initial, op0, op1))

            def edge_attention(a, landed):
                rv, mv = run_rows(a.W), messages(a.A)
                qv = qx[:, :, :, :].rearrange("p h j w -> p (h j w)")[:, 0:2 * B * a.QW].rearrange(
                    "p (h j w) -> p h j w", h=2, j=B)
                st.do(V.memset(rv[:, 1, B - 1, :], 0.0))
                st.do(V.memset(maxrun[:, :, :], -BIG))
                st.reset()
                dve.sem_inc(rows_free, 2)
                with dve.Fori(0, PAIRS) as b:
                    for h in range(2):
                        block_masks(b, h)
                        if a.R > 1:
                            st.add(V.tensor_copy(ety_now[:, :], etyf[:, cols(b, h)]))
                        st.wait()
                        dve.wait_ge(spread_in[h], b * 16 + 16)
                        if a.R == 1:
                            scan(qv[:, h, :, 0], cont_now[:, :], qv[:, h, :, 0], qlast[:, 0:1], ALU.mult, ALU.add)
                            q = qv[:, h]
                        else:
                            for j in range(B):
                                before = qv[:, h, j - 1, :] if j else qlast[:, :]
                                st.do(V.scalar_tensor_tensor(qv[:, h, j, :], before, cont_now[:, j:j + 1], qv[:, h, j, :],
                                                             ALU.mult, ALU.add))
                            tt(onehot[:, :, :], bc(iota_f[:, 0:REL].unsqueeze(1), [P, B, REL]),
                               bc(ety_now[:, :].unsqueeze(2), [P, B, REL]), ALU.is_equal)
                            tt(qsel[:, :, :, :], qv[:, h].rearrange("p j (k r) -> p j k r", k=a.H),
                               bc(onehot[:, :, :].unsqueeze(2), [P, B, a.H, REL]), ALU.mult)
                            st.do(V.tensor_reduce(expo[:, :, :], qsel[:, :, :, :], AX.X, ALU.add))
                            q = expo[:, :, 0:a.H]
                        copy(qlast[:, 0:a.QW], qv[:, h, B - 1, :])
                        dve.wait_ge(landed[h], (b + 1) * 16 * B)
                        tt(score[:, :, 0:a.H], q, gath[:, h, :, F:F + a.H], ALU.add)
                        st.do(V.scalar_tensor_tensor(score[:, :, 0:a.H], score[:, :, 0:a.H], 0.2, score[:, :, 0:a.H],
                                                     ALU.mult, ALU.max))
                        for k in range(a.H):
                            st.add(V.tensor_tensor_scan(maxrun[:, k, 1:], negs_now[:, :], score[:, :, k],
                                                        maxrun[:, k, 0:1], ALU.add, ALU.max))
                        st.wait()
                        tt(decay[:, 0:a.H, :], maxrun[:, 0:a.H, 0:B], maxrun[:, 0:a.H, 1:], ALU.subtract)
                        ts(decay[:, 0:a.H, :], decay[:, 0:a.H, :], 0.0, ALU.min)
                        tt(expo[:, :, 0:a.H], score[:, :, 0:a.H], maxrun[:, 0:a.H, 1:].rearrange("p k j -> p j k"),
                           ALU.subtract)
                        dve.sem_inc(scores_ready, 1)
                        dve.wait_ge(runs_free[h], b + 1)
                        copy(rv[:, h, :, a.A:], maxrun[:, 0:a.H, 1:].rearrange("p k j -> p j k"))
                        copy(maxrun[:, 0:a.H, 0:1], maxrun[:, 0:a.H, B:])
                        dve.wait_ge(msgs_ready, (b * 2 + h) * 2 + 2)
                        tt(decay[:, 0:a.H, :], decay[:, 0:a.H, :], bc(cont_now[:, :].unsqueeze(1), [P, a.H, B]), ALU.mult)
                        m4 = mv[:, h].rearrange("p j (k d) -> p j k d", k=a.H)
                        tt(m4[:, :, :, 0:a.D], gath[:, h, :, 0:F].rearrange("p j (k d) -> p j k d", k=a.H),
                           bc(m4[:, :, :, a.D:], [P, B, a.H, a.D]), ALU.mult)
                        for j in range(B):
                            before = rv[:, h, j - 1, :] if j else rv[:, 1 - h, B - 1, :]
                            for k in range(a.H):
                                c = slice(k * a.D1, (k + 1) * a.D1)
                                if j:
                                    st.wait(st.n + 1 - a.H)
                                st.add(V.scalar_tensor_tensor(rv[:, h, j, c], before[:, c], decay[:, k, j:j + 1],
                                                              mv[:, h, j, c], ALU.mult, ALU.add))
                        finish_block(h)
                last = rv[:, 1, B - 1, :]
                copy(cS[:, 0:a.A].rearrange("p (k d) -> p k d", k=a.H), bc(last[:, a.A:].unsqueeze(2), [P, a.H, a.D1]))
                ask_pe()
                st.do(V.memset(cA[:, 0:1], -BIG))
                dve.wait_ge(sum_done, 1)
                maxT, lastT = psT[0][0:a.A, 0:P], psT[0][0:a.A, P:2 * P]
                scan(cA[0:a.A, 1:], negT[0:a.A, :], maxT, -BIG, ALU.add, ALU.max)
                tt(cB[0:a.A, :], cA[0:a.A, 0:P], cA[0:a.A, 1:], ALU.subtract)
                ts(cB[0:a.A, :], cB[0:a.A, :], 0.0, ALU.min)
                ask()
                tt(cC[0:a.A, :], maxT, cA[0:a.A, 1:], ALU.subtract)
                ask()
                tt(cB[0:a.A, :], cB[0:a.A, :], act_[0:a.A, :], ALU.mult)
                tt(cC[0:a.A, :], lastT, cC[0:a.A, :], ALU.mult)
                scan(cD[0:a.A, :], cB[0:a.A, :], cC[0:a.A, :], 0.0, ALU.mult, ALU.add)
                ask_pe()
                dve.wait_ge(sum_done, 2)
                copy(cS[:, 0:a.A], psO[0][:, 0:a.A])
                copy(cS[:, a.A:a.W], psO[0][:, P:P + a.A].rearrange("p (k d) -> p k d", k=a.H)[:, :, 0])
                dve.sem_inc(carry_ready, 1)
                end()

            def nodes_attention(a, key):
                ns, ncr = node_rows(a.W)
                dve.wait_ge(nodes_in[key], 16 * 2 * T)
                m1, m2 = ns[:, :, a.A:], ncr[:, :, a.A:]
                tt(hw2[:, :, 0:a.H], m1, m2, ALU.max)
                tt(hw1[:, :, 0:a.H], m1, hw2[:, :, 0:a.H], ALU.subtract)
                ask()
                tt(hw2[:, :, 0:a.H], m2, hw2[:, :, 0:a.H], ALU.subtract)
                ask()
                n4 = ns[:, :, 0:a.A].rearrange("p t (k d) -> p t k d", k=a.H)
                c4 = ncr[:, :, 0:a.A].rearrange("p t (k d) -> p t k d", k=a.H)
                shape = [P, T, a.H, a.D1]
                tt(n4, n4, bc(hw1[:, :, 0:a.H].unsqueeze(3), shape), ALU.mult)
                tt(c4, c4, bc(hw2[:, :, 0:a.H].unsqueeze(3), shape), ALU.mult)
                tt(n4, n4, c4, ALU.add)
                if a.R > 1:
                    ts(n4[:, :, :, a.D], n4[:, :, :, a.D], 1e-16, ALU.add)
                st.do(V.reciprocal(hw1[:, :, 0:a.H], n4[:, :, :, a.D]))
                tt(hw1[:, :, 0:a.H], hw1[:, :, 0:a.H], over_t(has[:, :], a.H), ALU.mult)
                tt(Z[:, :, :].rearrange("p t (k d) -> p t k d", k=a.H), n4[:, :, :, 0:a.D],
                   bc(hw1[:, :, 0:a.H].unsqueeze(3), [P, T, a.H, a.D]), ALU.mult)

            st.do(V.memset(zeros[:, :], 0.0))
            st.do(V.memset(cS[:, :], -BIG))
            dve.sem_inc(node_ready, 2)
            dve.wait_ge(idx_ready, 1)
            copy(iota_q[:, :], iota_i[:, :])
            copy(iota_f[:, :], iota_i[:, :])
            dve.wait_ge(loads_in, 16 * 9)
            copy(dstf, dsti)
            copy(dst0_i[:, :], dsti[:, 0:1])
            copy(prevf, prevd)
            tt(start[:, :], dstf, prevf, ALU.not_equal)
            ts(cont[:, :], start[:, :], -1.0, ALU.mult, 1.0, ALU.add)
            copy(etyf[:, :], reli[:, :])
            copy(prevf, srci[:, :])
            st.do(V.scalar_tensor_tensor(prevf, prevf, float(REL), etyf[:, :], ALU.mult, ALU.add))
            copy(reli[:, :], prevf)
            ts(qf, dstf, 0.5, ALU.add, 1.0 / T, ALU.mult)
            ts(qf, qf, -0.5, ALU.add)
            ts(qf, qf, ROUND, ALU.add)
            ts(qf, qf, -ROUND, ALU.add)
            st.do(V.scalar_tensor_tensor(tf, qf, -float(T), dstf, ALU.mult, ALU.add))
            copy(qb, qf)
            copy(tb, tf)
            st.reset()
            dve.sem_inc(oh_used, 2)
            with dve.Fori(0, PAIRS) as b:
                for h in range(2):
                    st.add(V.tensor_copy(cont_now[:, :], qb[:, cols(b, h)]))
                    st.add(V.tensor_copy(negs_now[:, :], tb[:, cols(b, h)]))
                    st.wait()
                    dve.wait_ge(oh_used, b * 2 + h + 1)
                    st.add(V.tensor_tensor(oh_q[:, h], bc(iota_q[:, :].unsqueeze(1), [P, B, P]),
                                           bc(cont_now[:, :].unsqueeze(2), [P, B, P]), ALU.is_equal))
                    st.add(V.tensor_tensor(oh_t[:, h], bc(iota_q[:, 0:T].unsqueeze(1), [P, B, T]),
                                           bc(negs_now[:, :].unsqueeze(2), [P, B, T]), ALU.is_equal))
                    st.wait()
                    dve.sem_inc(oh_ready, 1)
                    st.reset()
            dve.wait_ge(sum_done, 1)
            copy(deg[:, :], psO[0][:, 0:T])
            ts(has[:, :], deg[:, :], 0.0, ALU.is_gt)
            st.do(V.memset(s1[:, :], 1.0))
            scan(s2[:, :], s1[:, :], deg[:, :], 0.0, ALU.mult, ALU.add)
            copy(col1[:, :], s2[:, T - 1:T])
            ask_pe()
            dve.wait_ge(sum_done, 2)
            copy(col2[:, :], psS[0][:, 0:1])
            ts(s2[:, :], s2[:, :], col2[:, 0:1], ALU.add)
            tt(s1[:, :], s2[:, :], deg[:, :], ALU.subtract)
            ts(s2[:, :], s2[:, :], -1.0, ALU.add)
            ts(s2[:, :], s2[:, :], 0.0, ALU.max)
            copy(end_i[:, :], s2[:, :])
            ts(s3[:, :], has[:, :], -float(NO_EDGE), ALU.mult, float(NO_EDGE), ALU.add)
            tt(s3[:, :], s3[:, :], s1[:, :], ALU.add)
            copy(start_i[:, :], s3[:, :])
            for x in (s1, s2):
                ts(x[:, :], x[:, :], 0.5, ALU.add, 1.0 / C, ALU.mult)
                ts(x[:, :], x[:, :], -0.5, ALU.add)
                ts(x[:, :], x[:, :], ROUND, ALU.add)
                ts(x[:, :], x[:, :], -ROUND, ALU.add)
            tt(s3[:, :], s1[:, :], s2[:, :], ALU.is_lt)
            ts(s2[:, :], s2[:, :], -1.0 - P, ALU.add)
            tt(s2[:, :], s2[:, :], s3[:, :], ALU.mult)
            ts(s2[:, :], s2[:, :], float(P), ALU.add)
            copy(carry_i[:, :], s2[:, :])
            st.do(V.tensor_reduce(col1[:, :], start[:, :], AX.X, ALU.max))
            ts(col1[:, :], col1[:, :], -1.0, ALU.mult, 1.0, ALU.add)
            copy(cB[:, :], bc(col1[:, :], [P, P]))
            ask_pe()
            dve.wait_ge(sum_done, 3)
            copy(act_[:, :], psS[1][:, 0:P])
            ts(negT[:, :], act_[:, :], -1.0, ALU.add, BIG, ALU.mult)
            ts(s3[:, :], deg[:, :], 1.0, ALU.max)
            st.do(V.reciprocal(rden[:, :], s3[:, :]))
            tt(hrden[:, :], rden[:, :], has[:, :], ALU.mult)
            ts(s1[:, :], deg[:, :], 1.0, ALU.add)
            ask()
            ts(amp[:, :], s2[:, :], 1.0 / 2.5, ALU.mult)
            ts(s3[:, :], has[:, :], -1.0, ALU.mult, 1.0, ALU.add)
            tt(s3[:, :], s3[:, :], s2[:, :], ALU.add)
            st.do(V.reciprocal(s3[:, :], s3[:, :]))
            ts(s3[:, :], s3[:, :], 2.5, ALU.mult)
            tt(att[:, :], s3[:, :], has[:, :], ALU.mult)
            layer_norm()
            end()

            dve.wait_ge(sum_done, 1)
            copy(wT[:, :], psR[0:F, 0:F])
            ask_pe()
            dve.wait_ge(sum_done, 2)
            copy(wrel[:, F:F + 2], psR[0:F, F:F + 2])
            dve.sem_inc(operands_ready, 1)
            gt = msgs[:, 0:T * GAT.GW].rearrange("p (t w) -> p t w", t=T)
            for s in range(T):
                dve.wait_ge(product_done, s + 1)
                st.add(V.tensor_copy(gt[:, s, :], psO[s % 2][:, 0:GAT.GW]))
                st.do(V.tensor_copy(s4[:, s:s + 1], psO[s % 2][:, GAT.GW:GAT.GW + 1]))
                dve.sem_inc(evacuated, 1)
            dve.sem_inc(node_ready, 1)
            end()
            end()
            edge_attention(GAT, rows_in["gat"])
            nodes_attention(GAT, "gat")
            ts(Y[:, :, :], Z[:, :, :], 0.0, ALU.max)
            ts(Z[:, :, :], Z[:, :, :], 0.0, ALU.min)
            ask()
            ts(Z[:, :, :], Z[:, :, :], -1.0, ALU.add)
            tt(Y[:, :, :], Y[:, :, :], Z[:, :, :], ALU.add)
            tt(X[:, :, :], X[:, :, :], Y[:, :, :], ALU.add)
            layer_norm()
            end()

            with dve.Fori(0, LAYERS) as layer:
                dve.wait_ge(loads_in, 16 * 14)
                dve.sem_inc(operands_ready, 1)
                for s in range(T):
                    dve.wait_ge(product_done, s + 1)
                    st.add(V.tensor_copy(Y[:, s, :], psO[s % 2][:, 0:F]))
                    st.do(V.tensor_tensor(Bn[:, s, :], psO[s % 2][:, F:2 * F], par[:, 0, :], ALU.add))
                    dve.sem_inc(evacuated, 1)
                dve.sem_inc(node_ready, 1)
                end()
                rv, mv = run_rows(PNA_W), messages(192)
                st.do(V.memset(rv[:, 1, B - 1, 0:2 * F], -BIG))
                st.do(V.memset(rv[:, 1, B - 1, 2 * F:], 0.0))
                st.reset()
                dve.sem_inc(rows_free, 2)
                with dve.Fori(0, PAIRS) as b:
                    for h in range(2):
                        block_masks(b, h)
                        st.wait()
                        dve.wait_ge(msgs_ready, (b * 2 + h) * 2 + 2)
                        dve.wait_ge(runs_free[h], b + 1)
                        for j in range(B):
                            before = rv[:, h, j - 1, :] if j else rv[:, 1 - h, B - 1, :]
                            if j:
                                st.wait(st.n - 1)
                            st.add(V.scalar_tensor_tensor(rv[:, h, j, 0:2 * F], before[:, 0:2 * F], negs_now[:, j:j + 1],
                                                          mv[:, h, j, 0:2 * F], ALU.add, ALU.max))
                            if j:
                                st.wait(st.n - 1)
                            st.add(V.scalar_tensor_tensor(rv[:, h, j, 2 * F:], before[:, 2 * F:], cont_now[:, j:j + 1],
                                                          mv[:, h, j, F:], ALU.mult, ALU.add))
                        finish_block(h)
                ask_pe()
                dve.wait_ge(sum_done, 1)
                scan(cA[:, 1:], negT[:, :], psT[0][:, 0:P], -BIG, ALU.add, ALU.max)
                scan(cD[:, :], act_[:, :], psT[1][:, 0:P], 0.0, ALU.mult, ALU.add)
                ask_pe()
                dve.wait_ge(sum_done, 2)
                copy(cS[:, :], psO[0][:, 0:2 * P])
                dve.sem_inc(carry_ready, 1)
                end()

                ns, ncr = node_rows(PNA_W)
                dve.wait_ge(nodes_in["pna"], (layer + 1) * 16 * 2 * T)
                tt(ns[:, :, 0:2 * F], ns[:, :, 0:2 * F], ncr[:, :, 0:2 * F], ALU.max)
                tt(ns[:, :, 2 * F:], ns[:, :, 2 * F:], ncr[:, :, 2 * F:], ALU.add)
                nmax, amax, asum, asq = (ns[:, :, k * F:(k + 1) * F] for k in range(4))
                mean, mx, mn, std, var, s_ = (feats[:, :, k * F:(k + 1) * F] for k in range(6))
                tt(mx, amax, Bn[:, :, :], ALU.add)
                tt(mx, mx, over_t(has[:, :]), ALU.mult)
                tt(mn, Bn[:, :, :], nmax, ALU.subtract)
                tt(mn, mn, over_t(has[:, :]), ALU.mult)
                tt(Z[:, :, :], asum, over_t(hrden[:, :]), ALU.mult)
                tt(Z[:, :, :], Z[:, :, :], Z[:, :, :], ALU.mult)
                tt(Y[:, :, :], asq, over_t(hrden[:, :]), ALU.mult)
                tt(Y[:, :, :], Y[:, :, :], Z[:, :, :], ALU.subtract)
                ts(var, Y[:, :, :], 0.0, ALU.max)
                ts(Y[:, :, :], var, 1e-30, ALU.add)
                ask(False)
                tt(Z[:, :, :], Bn[:, :, :], over_t(deg[:, :]), ALU.mult)
                tt(Z[:, :, :], Z[:, :, :], asum, ALU.add)
                tt(s_, Z[:, :, :], over_t(has[:, :]), ALU.mult)
                tt(mean, s_, over_t(rden[:, :]), ALU.mult)
                dve.wait_ge(act_done, 1)
                dve.sem_inc(operands_ready, 1)
                for s in range(T):
                    ps = psO[s % 2]
                    dve.wait_ge(product_done, s + 1)
                    st.do(V.scalar_tensor_tensor(Y[:, s, :], ps[:, F:2 * F], amp[:, s:s + 1], par[:, 1, :], ALU.mult, ALU.add))
                    st.do(V.scalar_tensor_tensor(Y[:, s, :], ps[:, 2 * F:3 * F], att[:, s:s + 1], Y[:, s, :], ALU.mult, ALU.add))
                    tt(Y[:, s, :], ps[:, 0:F], Y[:, s, :], ALU.add)
                    dve.sem_inc(evacuated, 1)
                ts(Y[:, :, :], Y[:, :, :], 1.0 / float(N) ** 0.5, ALU.mult)
                batch_norm(Y[:, :, :], par[:, 2, :], par[:, 3, :])
                dve.sem_inc(operands_ready, 1)
                for s in range(T):
                    dve.wait_ge(product_done, T + s + 1)
                    tt(Bn[:, s, :], psO[s % 2][:, 0:F], par[:, 4, :], ALU.add)
                    dve.sem_inc(evacuated, 1)
                st.do(V.scalar_tensor_tensor(Bn[:, :, :], Bn[:, :, :], 0.01, Bn[:, :, :], ALU.mult, ALU.max))
                tt(Y[:, :, :], Bn[:, :, :], Hn[:, :, :], ALU.add)
                batch_norm(Y[:, :, :], par[:, 5, :], par[:, 6, :])
                st.do(V.scalar_tensor_tensor(Hn[:, :, :], Y[:, :, :], 0.0, Hn[:, :, :], ALU.max, ALU.add))
                end()

            for k, key in enumerate(("rgat1", "rgat2")):
                if k == 0:
                    tt(X[:, :, :], X[:, :, :], Hn[:, :, :], ALU.add)
                    layer_norm()
                dve.wait_ge(loads_in, 16 * 4)
                for r in range(REL):
                    ask_pe()
                    dve.wait_ge(sum_done, 2 * r + 1)
                    copy(wT[:, :], psR[0:F, 0:F])
                    ask_pe()
                    dve.wait_ge(sum_done, 2 * r + 2)
                    copy(wrel[:, REL * F + 4 * r:REL * F + 4 * r + 4], psS[0][0:F, 0:4])
                    copy(wrel[:, REL * F + 32:REL * F + 64].rearrange("f (k r) -> f k r", r=REL)[:, :, r],
                         psS[0][0:F, 4:8])
                dve.sem_inc(operands_ready, 1)
                for s in range(T):
                    tv = tab[:, s % 2, :].rearrange("p (r w) -> p r w", r=REL)
                    dve.wait_ge(product_done, s + 1)
                    if s >= 2:
                        dve.wait_ge(tab_stored[s % 2], 16 * (s // 2))
                    st.add(V.tensor_copy(tv[:, :, 0:F], psO[s % 2][:, :].rearrange("p (r w) -> p r w", r=REL)))
                    st.add(V.tensor_copy(tv[:, :, F:], psS[s % 2][:, 0:32].rearrange("p (r w) -> p r w", r=REL)))
                    st.add(V.tensor_copy(QN[:, s, :], psS[s % 2][:, 32:64]))
                    st.wait()
                    dve.sem_inc(evacuated, 1)
                end()
                end()
                edge_attention(RGAT, rows_in[key])
                nodes_attention(RGAT, key)
                tt(Z[:, :, :], Z[:, :, :], over_f(par[:, 0, :]), ALU.add)
                if k == 0:
                    ts(Hn[:, :, :], Z[:, :, :], 0.0, ALU.max)
                else:
                    tt(X[:, :, :], X[:, :, :], Z[:, :, :], ALU.add)
                    layer_norm()
                end()

            dve.wait_ge(loads_in, 16 * 3)
            dve.sem_inc(operands_ready, 1)
            for s in range(T):
                tv = tab[:, s % 2, 0:REL * F].rearrange("p (r w) -> p r w", r=REL)
                dve.wait_ge(product_done, s + 1)
                if s >= 2:
                    dve.wait_ge(tab_stored[s % 2], 16 * (s // 2))
                st.add(V.tensor_tensor(tv, psO[s % 2][:, :].rearrange("p (r w) -> p r w", r=REL),
                                       bc(par[:, 0, :].unsqueeze(1), [P, REL, F]), ALU.add))
                st.add(V.tensor_copy(Bn[:, s, :], psS[s % 2][:, 0:F]))
                st.wait()
                dve.sem_inc(evacuated, 1)
            end()
            rv, mv = run_rows(F), messages(F)
            st.do(V.memset(rv[:, 1, B - 1, :], 0.0))
            st.reset()
            dve.sem_inc(rows_free, 2)
            with dve.Fori(0, PAIRS) as b:
                for h in range(2):
                    st.add(V.tensor_copy(cont_now[:, :], cont[:, cols(b, h)]))
                    st.add(V.tensor_copy(ety_now[:, :], wgt[:, cols(b, h)]))
                    st.wait()
                    dve.wait_ge(rows_in["rgcn"][h], (b + 1) * 16 * B)
                    tt(mv[:, h], gath[:, h, :, 0:F], bc(ety_now[:, :].unsqueeze(2), [P, B, F]), ALU.mult)
                    dve.wait_ge(runs_free[h], b + 1)
                    for j in range(B):
                        before = rv[:, h, j - 1, :] if j else rv[:, 1 - h, B - 1, :]
                        st.do(V.scalar_tensor_tensor(rv[:, h, j, :], before, cont_now[:, j:j + 1], mv[:, h, j, :],
                                                     ALU.mult, ALU.add))
                    finish_block(h)
            ask_pe()
            dve.wait_ge(sum_done, 1)
            scan(cD[0:F, :], act_[0:F, :], psT[0][0:F, 0:P], 0.0, ALU.mult, ALU.add)
            ask_pe()
            dve.wait_ge(sum_done, 2)
            copy(cS[:, 0:F], psO[0][:, 0:F])
            dve.sem_inc(carry_ready, 1)
            end()
            ns, ncr = node_rows(F)
            dve.wait_ge(nodes_in["rgcn"], 16 * 2 * T)
            tt(Z[:, :, :], ns, ncr, ALU.add)
            tt(Z[:, :, :], Z[:, :, :], over_t(has[:, :]), ALU.mult)
            tt(Z[:, :, :], Z[:, :, :], Bn[:, :, :], ALU.add)
            tt(X[:, :, :], X[:, :, :], Z[:, :, :], ALU.add)
            dve.sem_inc(node_ready, 1)


_WEIGHTS = ("L0_gnn_W", "L0_gnn_a", "L1_gnn_WM", "L1_gnn_bM", "L1_gnn_WU", "L1_gnn_bU", "L1_gnn_gamma_t",
            "L1_gnn_beta_t", "L1_gnn_Wmix", "L1_gnn_bmix", "L1_gnn_gamma_o", "L1_gnn_beta_o", "L2_gnn_W1",
            "L2_gnn_Q1", "L2_gnn_K1", "L2_gnn_b1", "L2_gnn_W2", "L2_gnn_Q2", "L2_gnn_K2", "L2_gnn_b2",
            "L3_gnn_weight", "L3_gnn_h_bias", "L3_gnn_loop_weight")


def kernel(**inputs):
    import numpy as np
    import concourse.bacc as bacc
    from concourse import mybir as mb
    from concourse.bass_utils import run_bass_kernel_spmd

    def padded(a, n, fill=0):
        a = np.asarray(a)
        return np.concatenate([a, np.full((n - a.shape[0],) + a.shape[1:], fill, a.dtype)])

    arrays = {
        "x": padded(inputs["x"], NP),
        "src": padded(inputs["src"], EP).reshape(P, C),
        "dst": np.concatenate([np.full((1,), -1, np.int32), padded(inputs["dst"], EP, N)]),
        "edge_type_8": padded(inputs["edge_type_8"], EP).reshape(P, C),
        "edge_weight1": padded(inputs["edge_weight1"], EP).reshape(P, C),
    }
    for name in _WEIGHTS:
        arrays[name] = np.ascontiguousarray(inputs[name])
    nc = bacc.Bacc("TRN2", target_bir_lowering=False, num_devices=1)
    t = {k: nc.dram_tensor(f"in_{k}", a.shape, mb.dt.from_np(a.dtype), kind="ExternalInput").ap()
         for k, a in arrays.items()}
    t["out"] = nc.dram_tensor("out_x", (NP, F), mb.dt.float32, kind="ExternalOutput").ap()
    gnn(nc, t)
    r = run_bass_kernel_spmd(nc, [{f"in_{k}": a for k, a in arrays.items()}], core_ids=[0])
    return r.results[0]["out_x"][0:N]
```

```python
import concourse.bass as bass
from concourse import mybir
from contextlib import ExitStack

f32, i32, bf16 = mybir.dt.float32, mybir.dt.int32, mybir.dt.bfloat16
ALU, ACT, AX = mybir.AluOpType, mybir.ActivationFunctionType, mybir.AxisListType

P = 128
N = 3125
T = 25
NP = P * T
E = 100000
C = 784
BIGB, SMALLB = 28, 14
EP = P * C
F = 64
REL = 8
LAYERS = 4
FULL = N // T
BIG = 1.0e30
G = 4
GROUPS = [range(k, min(k + G, T)) for k in range(0, T, G)]
FIFTH = T // 5
PICK = 3
OWN = SMALLB - PICK
RING = 5
NO_EDGE = 1 << 20
ROUND = 12582912.0


class Steps:

    def __init__(self, eng, sem):
        self.eng, self.sem, self.n = eng, sem, 0

    def add(self, ins):
        ins.then_inc(self.sem, 1)
        self.n += 1
        return self.n

    def wait(self, n=None):
        self.eng.wait_ge(self.sem, self.n if n is None else n)

    def do(self, ins):
        self.add(ins)
        self.wait()

    def reset(self):
        if self.n:
            self.wait()
            self.eng.sem_clear(self.sem)
            self.n = 0


class Attention:

    def __init__(self, heads, rels):
        self.H, self.R = heads, rels
        self.D = F // heads
        self.D1 = self.D + 1
        self.A = heads * self.D1
        self.W = self.A + heads
        self.GW = F + heads
        self.QW = rels * heads


GAT, RGAT = Attention(1, 1), Attention(4, REL)
PNA_W = 4 * F
PNA_M = 3 * F


def pairs(b):
    return C // (2 * b)


def gnn(nc, t):
    ctx = ExitStack()
    with ctx:
        def sb(name, shape, dt=f32):
            return ctx.enter_context(nc.sbuf_tensor(name, shape, dt))

        def sem(name):
            return ctx.enter_context(nc.semaphore(name))

        def dram(name, shape, dt=f32):
            return nc.dram_tensor(name, shape, dt).ap()

        gat_table = dram("gat_table", (NP, GAT.GW))
        pna_table = dram("pna_table", (NP, F))
        rgat_table = dram("rgat_table", (NP * REL, RGAT.GW))
        rgcn_table = dram("rgcn_table", (NP * REL, F))
        gat_q = dram("gat_q", (NP, GAT.QW))
        rgat_q = dram("rgat_q", (NP, RGAT.QW))
        gat_spread = dram("gat_spread", (EP, GAT.QW))
        rgat_spread = dram("rgat_spread", (EP, RGAT.QW))
        end_table = dram("end_table", (NP, 1), i32)
        runs = {w: dram(f"runs{w}", (EP + 1, w)) for w in (GAT.W, PNA_W, RGAT.W, F)}

        X = sb("X", [P, T, F])
        Hn = sb("Hn", [P, T, F])
        Bn = sb("Bn", [P, T, F])
        Y = sb("Y", [P, T, F])
        Z = sb("Z", [P, T, F])
        gath = sb("gath", [P, 2, BIGB, F + 4])
        Bd = gath[:, :, :, :].rearrange("p h j w -> p (h j w)")[:, 0:T * F].rearrange("p (t f) -> p t f", t=T)
        msgs = sb("msgs", [P, T * 6 * F])
        rows = sb("rows", [P, 2 * SMALLB * PNA_W])
        nodes = sb("nodes", [P, T * PNA_W])
        qx = sb("qx", [P, 2 * BIGB * 32])
        start = sb("start", [P, C])
        cont = sb("cont", [P, C])
        srci = sb("srci", [P, C], i32)
        reli = sb("reli", [P, C], i32)
        etyf = sb("etyf", [P, C])
        wgt = sb("wgt", [P, C])
        idx_now = sb("idx_now", [P, 2, BIGB], i32)
        cont_now = sb("cont_now", [P, BIGB])
        negs_now = sb("negs_now", [P, BIGB])
        extra_now = sb("extra_now", [P, BIGB])
        q_now = sb("q_now", [P, BIGB], bf16)
        t_now = sb("t_now", [P, BIGB], bf16)
        onehot = sb("onehot", [P, BIGB, REL])
        qsel = sb("qsel", [P, BIGB, 4, REL])
        score = sb("score", [P, BIGB, 4])
        expo = sb("expo", [P, BIGB, 4])
        maxrun = sb("maxrun", [P, 4, 1 + BIGB])
        decay = sb("decay", [P, 4, BIGB])
        qlast = sb("qlast", [P, 32])
        QN = sb("QN", [P, T, 32])
        tab = sb("tab", [P, 2, REL * (F + 4)])
        XT = sb("XT", [P, 2, 512])
        ident = sb("ident", [P, P])
        upper = sb("upper", [P, P])
        realp = sb("realp", [P, P])
        contT = sb("contT", [P, P])
        negT = sb("negT", [P, P])
        cA = sb("cA", [P, P + 1])
        cB = sb("cB", [P, P])
        cC = sb("cC", [P, P])
        cD = sb("cD", [P, P + 1])
        before_c = sb("before_c", [P, PNA_W])
        fixed = sb("fixed", [P, PNA_W])
        fw = sb("fw", [P, 3, 4])
        deg = sb("deg", [P, T])
        has = sb("has", [P, T])
        hasnot = sb("hasnot", [P, T])
        rden = sb("rden", [P, T])
        amp = sb("amp", [P, T])
        att = sb("att", [P, T])
        s1 = sb("s1", [P, T])
        s2 = sb("s2", [P, T])
        s3 = sb("s3", [P, T])
        s4 = sb("s4", [P, T])
        hw1 = sb("hw1", [P, T, 4])
        end_i = sb("end_i", [P, T], i32)
        start_i = sb("start_i", [P, T], i32)
        dst0_i = sb("dst0_i", [P, 1], i32)
        end0_i = sb("end0_i", [P, 1], i32)
        fix_i = sb("fix_i", [P, 1], i32)
        col1 = sb("col1", [P, 1])
        col2 = sb("col2", [P, 1])
        col3 = sb("col3", [P, 1])
        tiny = sb("tiny", [P, 1])
        iota_i = sb("iota_i", [P, P], i32)
        iota_f = sb("iota_f", [P, P])
        part_i = sb("part_i", [P, 1], i32)
        first_node = sb("first_node", [P, 1])
        fa = sb("fa", [P, F])
        fb = sb("fb", [P, F])
        fc = sb("fc", [P, F])
        wrel = [sb(f"wrel{k}", [F, REL * F + F]) for k in range(3)]
        wgat = sb("wgat", [F, F + 2])
        agat = sb("agat", [F, 2])
        wk = sb("wk", [F, 2, REL, 8])
        wT = sb("wT", [F, F])
        wm = sb("wm", [F, LAYERS, 2, F])
        bm = sb("bm", [P, LAYERS * F])
        wm_now = sb("wm_now", [F, 2, F])
        bm_now = sb("bm_now", [P, F])
        wu0 = sb("wu0", [F, F])
        wu = sb("wu", [P, 3, 3, F])
        wmix = sb("wmix", [F, F])
        par = sb("par", [P, 6, F])
        brow = sb("brow", [P, 3, F])

        dsti = nodes[:, 0:C].bitcast(i32)
        prevd = nodes[:, C:2 * C].bitcast(i32)
        dstf = nodes[:, 2 * C:3 * C]
        prevf = nodes[:, 3 * C:4 * C]
        qf = nodes[:, 4 * C:5 * C]
        tf = nodes[:, 5 * C:6 * C]
        HQ, HT = BIGB * P, BIGB * T
        oh_q = msgs[:, 0:HQ].bitcast(bf16).rearrange("p (h q j) -> p h q j", h=2, j=BIGB)
        oh_t = msgs[:, HQ:HQ + HT].bitcast(bf16).rearrange("p (h q j) -> p h q j", h=2, j=BIGB)
        at = HQ + HT
        iota_e = msgs[:, at:at + HQ // 2].bitcast(bf16).rearrange("p (q j) -> p q j", j=BIGB)
        at += HQ // 2
        qb = msgs[:, at:at + C // 2].bitcast(bf16)
        tb = msgs[:, at + C // 2:at + C].bitcast(bf16)
        at += C
        gat_rows = msgs[:, at:at + T * GAT.GW].rearrange("p (t w) -> p t w", t=T)
        ZN = C * RGAT.QW // 7
        zeros = rows[:, 0:ZN]
        feats = msgs[:, :].rearrange("p (t w) -> p t w", t=T)

        def run_rows(w, b):
            return rows[:, 0:2 * b * w].rearrange("p (h j w) -> p h j w", h=2, j=b)

        def node_rows(w):
            return nodes[:, 0:T * w].rearrange("p (t w) -> p t w", t=T)

        def messages(w, b):
            return msgs[:, 0:2 * b * w].rearrange("p (h j w) -> p h j w", h=2, j=b)

        def dst_scores(qw):
            return qx[:, 0:2 * BIGB * qw].rearrange("p (h j w) -> p h j w", h=2, j=BIGB)

        spare = gath[:, :, :, :].rearrange("p h j w -> p (h j w)")
        PAIR = 2 * PICK * P
        near_src = spare[:, T * F:T * F + PAIR].bitcast(i32)
        near = spare[:, T * F + PAIR:T * F + PAIR + PAIR // 2].bitcast(bf16)
        tab_flat = tab[:, :, :].rearrange("p k w -> p (k w)")
        ring = [(qx if k < 3 else tab_flat)[:, k % 3 * PAIR // 2:(k % 3 + 1) * PAIR // 2].bitcast(bf16)
                for k in range(RING)]
        part_hm = Z[:, :, :].rearrange("p t f -> p (t f)").bitcast(bf16).rearrange("p (z t f) -> p z t f", z=2, t=T)
        part_l = QN[:, :, :].rearrange("p t f -> p (t f)").bitcast(bf16).rearrange("p (t f) -> p t f", t=T)
        parts = [part_hm[:, 0], part_hm[:, 1], part_l]
        qsel_flat = qsel[:, :, :, :].rearrange("p j k r -> p (j k r)")
        nothing = qsel_flat[:, 0:PICK * F].bitcast(bf16)
        landing = [x[:, 0:OWN * F].rearrange("p (j f) -> p j f", j=OWN)
                   for x in (qsel_flat[:, PICK * F:], XT[:, :, :].rearrange("p k n -> p (k n)"))]

        psT = [ctx.enter_context(nc.psum_tensor(f"psT{k}", [P, 512], f32)) for k in range(2)]
        psO = [ctx.enter_context(nc.psum_tensor(f"psO{k}", [P, 512], f32)) for k in range(2)]
        psS = [ctx.enter_context(nc.psum_tensor(f"psS{k}", [P, 512], f32)) for k in range(2)]
        psR = ctx.enter_context(nc.psum_tensor("psR", [P, 512], f32))
        psH = ctx.enter_context(nc.psum_tensor("psH", [P, 512], f32))
        picked = psH[:, 0:2 * PICK * F].rearrange("p (h x) -> p h x", h=2)

        x_in = sem("x_in")
        loads_in = sem("loads_in")
        weights_in = sem("weights_in")
        zeros_stand = sem("zeros_stand")
        consts_stand = sem("consts_stand")
        transposed = sem("transposed")
        xt_ready = sem("xt_ready")
        product_done = sem("product_done")
        evacuated = sem("evacuated")
        base_ready = sem("base_ready")
        tab_stored = [sem("tab_stored0"), sem("tab_stored1")]
        rows_free = sem("rows_free")
        msgs_ready = sem("msgs_ready")
        scores_ready = sem("scores_ready")
        block_done = [sem("block_done0"), sem("block_done1")]
        runs_stored = [sem("runs_stored0"), sem("runs_stored1")]
        runs_free = [sem("runs_free0"), sem("runs_free1")]
        spread_in = [sem("spread_in0"), sem("spread_in1")]
        idx_ready = sem("idx_ready")
        table_ready = sem("table_ready")
        table_stored = sem("table_stored")
        starts_ready = sem("starts_ready")
        ends_stored = sem("ends_stored")
        fixed_ready = sem("fixed_ready")
        result_ready = sem("result_ready")
        sum_ready = sem("sum_ready")
        sum_done = sem("sum_done")
        operands_ready = sem("operands_ready")
        act_asked = sem("act_asked")
        act_done = sem("act_done")
        gathering = sem("gathering")
        oh_ready = sem("oh_ready")
        oh_used = sem("oh_used")
        stage_sems = [x_in, loads_in, weights_in, zeros_stand, consts_stand, transposed, xt_ready, product_done, evacuated,
                      base_ready, *tab_stored, rows_free, msgs_ready, scores_ready, *block_done, *runs_stored,
                      *runs_free, *spread_in, idx_ready, table_ready, table_stored, starts_ready, ends_stored,
                      fixed_ready, result_ready, sum_ready, sum_done, operands_ready, act_asked, act_done, gathering,
                      oh_ready, oh_used]
        near_in = sem("near_in")
        near_ready = sem("near_ready")
        onehot_ready = sem("onehot_ready")
        onehot_used = sem("onehot_used")
        parts_ready = sem("parts_ready")
        picked_done = sem("picked_done")
        picked_free = sem("picked_free")
        msgs_free = sem("msgs_free")
        stage_sems += [near_in, near_ready, onehot_ready, onehot_used, parts_ready, picked_done, picked_free, msgs_free]
        zero_rows = sem("zero_rows")
        zero_filled = sem("zero_filled")
        final_stored = sem("final_stored")
        names = ("gat", "pna", "rgat0", "rgat1", "rgcn")
        rows_in = {k: [sem(f"{k}_rows_in{h}") for h in range(2)] for k in names}
        nodes_in = {k: [sem(f"{k}_nodes_in{g}") for g in range(5 if k == "pna" else 1)] for k in names}
        fix_in = {k: sem(f"{k}_fix_in") for k in names}
        fix_out = {k: sem(f"{k}_fix_out") for k in names}
        spread_out = {k: sem(f"{k}_spread_out") for k in ("gat", "rgat0", "rgat1")}
        q_first_in = {k: sem(f"{k}_q_first_in") for k in ("gat", "rgat0", "rgat1")}
        end0_in = sem("end0_in")
        arrived = sem("arrived")
        go = {k: sem(f"go_{k}") for k in ("pe", "act", "dve", "pool")}
        dve_steps, pool_steps = sem("dve_steps"), sem("pool_steps")

        def meet(eng, who):
            eng.sem_inc(arrived, 1)
            eng.wait_ge(go[who], 1)
            eng.sem_clear(go[who])

        def meet_sp(sp):
            sp.wait_ge(arrived, 4)
            sp.sem_clear(arrived)
            for s in stage_sems:
                sp.sem_clear(s)
            for s in go.values():
                sp.sem_inc(s, 1)

        def cols(b, h, n):
            return bass.ds((b * 2 + h) * n, n)

        def bc(ap, shape):
            return ap.to_broadcast(shape)

        block = ctx.enter_context(nc.Block())

        @block.sync
        def _(sp):
            def load(dst, src, signal=loads_in):
                sp.dma_start(dst, src).then_inc(signal, 16)

            def edge_pass(w, n, spread=None, qw=0, key=None):
                if spread is not None:
                    sv, qv = spread.rearrange("(p c) w -> p c w", p=P), dst_scores(qw)
                    sp.wait_ge(spread_out[key], 16 * T)
                    for h in range(2):
                        sp.dma_start(qv[:, h], sv[:, h * n:h * n + n, :]).then_inc(spread_in[h], 16)
                for h in range(2):
                    sp.sem_inc(runs_free[h], 1)
                rv = runs[w][0:EP, :].rearrange("(p c) w -> p c w", p=P)
                with sp.Fori(0, pairs(n) - 1) as b:
                    for h in range(2):
                        sp.wait_ge(block_done[h], b + 1)
                        sp.dma_start(rv[:, cols(b, h, n), :], run_rows(w, n)[:, h]).then_inc(runs_stored[h], 16)
                        if spread is not None:
                            sp.dma_start(qv[:, h], sv[:, cols(b + 1, h, n), :]).then_inc(spread_in[h], 16)
                        sp.wait_ge(runs_stored[h], b * 16 + 16)
                        sp.sem_inc(runs_free[h], 1)
                for h in range(2):
                    sp.wait_ge(block_done[h], pairs(n))
                    sp.dma_start(rv[:, C - (2 - h) * n:C - (1 - h) * n, :], run_rows(w, n)[:, h]).then_inc(
                        runs_stored[h], 16)

            def store_node_tables(table, w, bank_q=None, qw=0):
                tv = table.rearrange("(p t r) w -> p t (r w)", p=P, t=T)
                for s in range(T):
                    sp.wait_ge(evacuated, s + 1)
                    sp.dma_start(tv[:, s, :], tab[:, s % 2, 0:REL * w]).then_inc(tab_stored[s % 2], 16)
                if bank_q is not None:
                    sp.dma_start(bank_q.rearrange("(p t) w -> p t w", p=P), QN[:, :, 0:qw]).then_inc(table_stored, 16)

            load(X[:, :, :], t["x"].rearrange("(p t) f -> p t f", p=P), x_in)
            load(wgat[:, 0:F], t["L0_gnn_W"], x_in)
            for k in range(2):
                load(agat[:, k:k + 1], t["L0_gnn_a"][k * F:(k + 1) * F].unsqueeze(1), x_in)
            load(srci[:, :], t["src"], x_in)
            flat = t["dst"]
            load(dsti, flat[1:1 + EP].rearrange("(p c) -> p c", p=P))
            load(prevd, flat[0:EP].rearrange("(p c) -> p c", p=P))
            load(reli[:, :], t["edge_type_8"])
            load(wgt[:, :], t["edge_weight1"])
            sp.wait_ge(zeros_stand, 1)
            sp.dma_start(gat_spread.rearrange("(p c) w -> p (c w)", p=P), zeros[:, 0:C]).then_inc(zero_rows, 16)
            for w in runs:
                sp.dma_start(runs[w][EP:EP + 1, :], zeros[0:1, 0:w]).then_inc(zero_rows, 16)
            sp.wait_ge(table_ready, 1)
            sp.dma_start(gat_table.rearrange("(p t) w -> p t w", p=P), gat_rows).then_inc(table_stored, 16)
            sp.dma_start(gat_q.rearrange("(p t) w -> p (t w)", p=P), s4[:, :]).then_inc(table_stored, 16)
            zr = rgat_spread.rearrange("(p c) w -> p (c w)", p=P)
            for k in range(0, C * 32, ZN):
                sp.dma_start(zr[:, k:k + ZN], zeros).then_inc(zero_filled, 16)
            for l in range(LAYERS):
                load(wm[:, l], t["L1_gnn_WM"][l].rearrange("(k f) n -> f k n", k=2), weights_in)
            load(bm[:, :], t["L1_gnn_bM"].rearrange("l f -> (l f)").partition_broadcast(P), weights_in)
            for k in range(2):
                n = str(k + 1)
                load(wrel[k][:, 0:REL * F].rearrange("f (r n) -> f r n", r=REL),
                     t["L2_gnn_W" + n].rearrange("r f n -> f r n"), weights_in)
                load(wk[:, k, :, 0:4], t["L2_gnn_K" + n].rearrange("r f n -> f r n"), weights_in)
                load(wk[:, k, :, 4:8], t["L2_gnn_Q" + n].rearrange("r f n -> f r n"), weights_in)
                load(brow[:, k, :], t["L2_gnn_b" + n].partition_broadcast(P), weights_in)
            load(wrel[2][:, 0:REL * F].rearrange("f (r n) -> f r n", r=REL),
                 t["L3_gnn_weight"].rearrange("r f n -> f r n"), weights_in)
            load(wrel[2][:, REL * F:], t["L3_gnn_loop_weight"], weights_in)
            load(brow[:, 2, :], t["L3_gnn_h_bias"].partition_broadcast(P), weights_in)
            sp.wait_ge(starts_ready, 1)
            sp.dma_start(end_table.rearrange("(p t) w -> p (t w)", p=P), end_i[:, :]).then_inc(ends_stored, 16)
            edge_pass(GAT.W, BIGB, gat_spread, GAT.QW, "gat")
            sp.wait_ge(zero_filled, 16 * 7)
            meet_sp(sp)

            with sp.Fori(0, LAYERS) as layer:
                one = bass.ds(layer, 1)
                wuv = t["L1_gnn_WU"][one, :, :].rearrange("l r n -> (l r) n")
                load(wu0[:, :], wuv[0:F, :])
                for g in range(3):
                    load(wu[:, :, g, :], wuv[F + g * 6 * F:F + (g + 1) * 6 * F, :].rearrange("(k p) n -> p k n", p=P))
                load(wmix[:, :], t["L1_gnn_Wmix"][one, :, :].rearrange("l f n -> (l f) n"))
                for k, nm in enumerate(("bU", "gamma_t", "beta_t", "bmix", "gamma_o", "beta_o")):
                    load(par[:, k, :], t["L1_gnn_" + nm][one, :].rearrange("l f -> (l f)").partition_broadcast(P))
                sp.wait_ge(table_ready, 1)
                sp.dma_start(pna_table.rearrange("(p t) w -> p t w", p=P), Y[:, :, :]).then_inc(table_stored, 16)
                edge_pass(PNA_W, SMALLB)
                meet_sp(sp)

            for k in range(2):
                store_node_tables(rgat_table, RGAT.GW, rgat_q, RGAT.QW)
                edge_pass(RGAT.W, BIGB, rgat_spread, RGAT.QW, f"rgat{k}")
                meet_sp(sp)

            store_node_tables(rgcn_table, F)
            edge_pass(F, SMALLB)
            sp.wait_ge(result_ready, 1)
            sp.dma_start(t["out"].rearrange("(p t) f -> p t f", p=P), X[:, :, :]).then_inc(final_stored, 16)
            sp.wait_ge(final_stored, 16)

        @block.gpsimd
        def _(pool):
            steps = Steps(pool, pool_steps)

            def fetch(dst, table, idx, signal, bound):
                pool.indirect_dma_start(dst, None, table, bass.IndirectOffsetOnAxis(ap=idx, axis=0),
                                        bounds_check=bound, oob_is_err=False).then_inc(signal, 16)

            def put(table, src, idx, signal, bound):
                pool.indirect_dma_start(table, bass.IndirectOffsetOnAxis(ap=idx, axis=0), src, None,
                                        bounds_check=bound, oob_is_err=False).then_inc(signal, 16)

            def block_rows(table, idx, rows_of, landed, bound, n, own, b, h):
                nc.gpsimd.tensor_copy(idx_now[:, h, 0:own], idx[:, bass.ds((b * 2 + h) * n, own)]).then_inc(idx_ready, 1)
                pool.wait_ge(idx_ready, b * 2 + h + 1)
                pool.sem_inc(gathering, 1)
                for j in range(own):
                    fetch(rows_of(h, j), table, idx_now[:, h, j:j + 1], landed[h], bound)

            def first_pair(*a):
                for h in range(2):
                    block_rows(*a, 0, h)

            def other_pairs(*a):
                with pool.Fori(1, pairs(a[-2])) as b:
                    for h in range(2):
                        pool.wait_ge(rows_free, b * 2 + h - 1)
                        pool.sem_inc(gathering, 1)
                        block_rows(*a, b, h)

            def fix_and_nodes(w, n, key):
                for h in range(2):
                    pool.wait_ge(runs_stored[h], 16 * pairs(n))
                fetch(fixed[:, 0:w], runs[w], fix_i[:, 0:1], fix_in[key], EP - 1)
                pool.wait_ge(fixed_ready, 1)
                put(runs[w], fixed[:, 0:w], fix_i[:, 0:1], fix_out[key], EP - 1)
                return node_rows(w)

            def fetch_nodes(w, key):
                ns = node_rows(w)
                sems = nodes_in[key]
                for s in range(T):
                    fetch(ns[:, s, :], runs[w], end_i[:, s:s + 1], sems[s * len(sems) // T], EP)

            steps.do(nc.gpsimd.iota(iota_i[:, :], pattern=[[1, P]], base=0, channel_multiplier=0))
            steps.do(nc.gpsimd.iota(part_i[:, :], pattern=[[1, 1]], base=0, channel_multiplier=1))
            steps.do(nc.gpsimd.memset(ident[:, :], 0.0))
            steps.do(nc.gpsimd.affine_select(out=ident[:, :], in_=ident[:, :], compare_op=ALU.not_equal, fill=1.0,
                                             base=0, pattern=[[-1, P]], channel_multiplier=1))
            steps.do(nc.gpsimd.memset(upper[:, :], 1.0))
            steps.do(nc.gpsimd.affine_select(out=upper[:, :], in_=upper[:, :], compare_op=ALU.is_gt, fill=0.0,
                                             base=0, pattern=[[1, P]], channel_multiplier=-1))
            steps.do(nc.gpsimd.memset(realp[:, :], 1.0))
            steps.do(nc.gpsimd.affine_select(out=realp[:, :], in_=realp[:, :], compare_op=ALU.is_gt, fill=0.0,
                                             base=FULL, pattern=[[0, P]], channel_multiplier=-1))
            pool.sem_inc(consts_stand, 1)
            pool.wait_ge(x_in, 16 * 5)
            pool.wait_ge(table_stored, 32)
            a = (gat_table, srci, lambda h, j: gath[:, h, j, 0:GAT.GW], rows_in["gat"], NP - 1, BIGB, BIGB)
            first_pair(*a)
            pool.wait_ge(starts_ready, 1)
            pool.wait_ge(zero_rows, 16 * (1 + len(runs)))
            for s in range(T):
                put(gat_spread, s4[:, s:s + 1], start_i[:, s:s + 1], spread_out["gat"], EP - 1)
            fetch(qlast[:, 0:1], gat_q, dst0_i[:, 0:1], q_first_in["gat"], NP - 1)
            pool.wait_ge(ends_stored, 16)
            fetch(end0_i[:, :], end_table, dst0_i[:, 0:1], end0_in, NP - 1)
            other_pairs(*a)
            fix_and_nodes(GAT.W, BIGB, "gat")
            pool.wait_ge(fix_out["gat"], 16)
            fetch_nodes(GAT.W, "gat")
            meet(pool, "pool")

            with pool.Fori(0, LAYERS) as layer:
                pool.wait_ge(table_stored, 16)
                a = (pna_table, srci, lambda h, j: landing[h][:, j, :], rows_in["pna"], NP - 1, SMALLB, OWN)
                first_pair(*a)
                other_pairs(*a)
                fix_and_nodes(PNA_W, SMALLB, "pna")
                pool.wait_ge(fix_out["pna"], layer * 16 + 16)
                pool.sem_inc(gathering, 1)
                fetch_nodes(PNA_W, "pna")
                meet(pool, "pool")

            for k in range(2):
                key = f"rgat{k}"
                for s in range(T):
                    pool.wait_ge(evacuated, s + 1)
                    put(rgat_spread, QN[:, s, :], start_i[:, s:s + 1], spread_out[key], EP - 1)
                for h in range(2):
                    pool.wait_ge(tab_stored[h], 16 * len(range(h, T, 2)))
                pool.wait_ge(table_stored, 16)
                fetch(qlast[:, :], rgat_q, dst0_i[:, 0:1], q_first_in[key], NP - 1)
                a = (rgat_table, reli, lambda h, j: gath[:, h, j, :], rows_in[key], NP * REL - 1, BIGB, BIGB)
                first_pair(*a)
                other_pairs(*a)
                fix_and_nodes(RGAT.W, BIGB, key)
                pool.wait_ge(fix_out[key], 16)
                fetch_nodes(RGAT.W, key)
                meet(pool, "pool")

            for h in range(2):
                pool.wait_ge(tab_stored[h], 16 * len(range(h, T, 2)))
            a = (rgcn_table, reli, lambda h, j: gath[:, h, j, 0:F], rows_in["rgcn"], NP * REL - 1, SMALLB, SMALLB)
            first_pair(*a)
            other_pairs(*a)
            fix_and_nodes(F, SMALLB, "rgcn")
            pool.wait_ge(fix_out["rgcn"], 16)
            fetch_nodes(F, "rgcn")

        @block.tensor
        def _(pe):
            def transposes(src, k, slots):
                if k >= 2:
                    pe.wait_ge(xt_ready, k - 1)
                for i, s in enumerate(slots):
                    last = nc.tensor.transpose(psT[k % 2][0:F, i * P:(i + 1) * P], src[:, s, :], ident[:, :])
                last.then_inc(transposed, 1)

            def group_products(src, rhs, n, k0):
                for g in range(len(GROUPS) + 1):
                    if g < len(GROUPS):
                        transposes(src, k0 + g, GROUPS[g])
                    if g >= 1:
                        k = k0 + g - 1
                        pe.wait_ge(xt_ready, k + 1)
                        if k >= 2:
                            pe.wait_ge(evacuated, k - 1)
                        for i, s in enumerate(GROUPS[g - 1]):
                            last = nc.tensor.matmul(psO[k % 2][:, i * n:(i + 1) * n], XT[0:F, k % 2, i * P:(i + 1) * P],
                                                    rhs, start=True, stop=True)
                        last.then_inc(product_done, 1)

            def relation_products(w):
                pe.wait_ge(operands_ready, 1)
                transposes(Hn, 0, GROUPS[0])
                for g, slots in enumerate(GROUPS):
                    if g + 1 < len(GROUPS):
                        transposes(Hn, g + 1, GROUPS[g + 1])
                    pe.wait_ge(xt_ready, g + 1)
                    for i, s in enumerate(slots):
                        if s >= 2:
                            pe.wait_ge(evacuated, s - 1)
                        lhs = XT[0:F, g % 2, i * P:(i + 1) * P]
                        nc.tensor.matmul(psO[s % 2][:, 0:REL * F], lhs, w[:, 0:REL * F], start=True, stop=True)
                        nc.tensor.matmul(psS[s % 2][:, 0:F], lhs, w[:, REL * F:], start=True, stop=True).then_inc(
                            product_done, 1)

            def total(k):
                pe.wait_ge(sum_ready, k)
                nc.tensor.matmul(psR[:, 0:F], realp[:, :], fa[:, :], start=True, stop=True).then_inc(sum_done, 1)

            def carry_attention(a, k):
                last = run_rows(a.W, BIGB)[:, 1, BIGB - 1, 0:a.A]
                pe.wait_ge(sum_ready, k + 1)
                nc.tensor.transpose(psT[0][0:a.A, 0:P], before_c[:, 0:a.A], ident[:, :])
                nc.tensor.transpose(psT[0][0:a.A, P:2 * P], last, ident[:, :]).then_inc(sum_done, 1)
                pe.wait_ge(sum_ready, k + 2)
                nc.tensor.transpose(psO[0][:, 0:a.A], cD[0:a.A, 0:P], ident[0:a.A, 0:a.A])
                nc.tensor.transpose(psO[0][:, P:P + a.A], cA[0:a.A, 0:P], ident[0:a.A, 0:a.A]).then_inc(sum_done, 1)

            pe.wait_ge(consts_stand, 1)
            pe.wait_ge(x_in, 16 * 5)
            nc.tensor.transpose(psR[0:F, 0:F], wgat[:, 0:F], ident[0:F, 0:F]).then_inc(sum_done, 1)
            pe.wait_ge(sum_ready, 1)
            nc.tensor.matmul(psR[0:F, F:F + 2], wT[:, :], agat[:, :], start=True, stop=True).then_inc(sum_done, 1)
            pe.wait_ge(operands_ready, 1)
            group_products(Hn, wgat[:, :], F + 2, 0)
            zl, zr = zeros[:, 0:P // 2].bitcast(bf16), zeros[:, 0:32].bitcast(bf16)[:, 0:T]
            nc.tensor.matmul(psH[:, 0:T], zl, zr, start=True, stop=False)
            with pe.Fori(0, pairs(BIGB)) as b:
                for h in range(2):
                    pe.wait_ge(oh_ready, b * 2 + h + 1)
                    for j in range(BIGB):
                        last = nc.tensor.matmul(psH[:, 0:T], oh_q[:, h, :, j], oh_t[:, h, :, j], start=False, stop=False)
                    last.then_inc(oh_used, 1)
            nc.tensor.matmul(psH[:, 0:T], zl, zr, start=False, stop=True).then_inc(sum_done, 1)
            pe.wait_ge(sum_ready, 2)
            nc.tensor.matmul(psS[0][:, 0:1], upper[:, :], col1[:, :], start=True, stop=True).then_inc(sum_done, 1)
            pe.wait_ge(sum_ready, 3)
            nc.tensor.matmul(psS[1][:, 0:P], cB[:, :], ident[:, :], start=True, stop=True).then_inc(sum_done, 1)
            for k in range(2):
                for r in range(REL):
                    pe.wait_ge(sum_ready, 4 + 2 * (k * REL + r))
                    nc.tensor.transpose(psR[0:F, 0:F], wrel[k][:, r * F:(r + 1) * F], ident[0:F, 0:F]).then_inc(sum_done, 1)
                    pe.wait_ge(sum_ready, 5 + 2 * (k * REL + r))
                    nc.tensor.matmul(psS[0][0:F, 0:8], wT[:, :], wk[:, k, r, :], start=True, stop=True).then_inc(sum_done, 1)
            carry_attention(GAT, 3 + 4 * REL)
            meet(pe, "pe")

            NG = len(GROUPS)
            with pe.Fori(0, LAYERS) as layer:
                pe.wait_ge(operands_ready, 1)
                group_products(Hn, wm_now[:, :, :].rearrange("f k n -> f (k n)"), 2 * F, 0)
                pe.wait_ge(parts_ready, 1)
                with pe.Fori(0, pairs(SMALLB)) as b:
                    pe.wait_ge(picked_free, b + 1)
                    nc.tensor.matmul(psH[:, 0:2 * PICK * F], nothing[:, 0:P], nothing, start=True, stop=False)
                    for s in range(T):
                        pe.wait_ge(onehot_ready, b * T + s + 1)
                        for c in range(2 * PICK):
                            for part in parts:
                                last = nc.tensor.matmul(psH[:, c * F:(c + 1) * F], ring[s % RING][:, c * P:(c + 1) * P],
                                                        part[:, s, :], start=False, stop=False)
                        last.then_inc(onehot_used, 1)
                    nc.tensor.matmul(psH[:, 0:2 * PICK * F], nothing[:, 0:P], nothing, start=False,
                                     stop=True).then_inc(picked_done, 1)
                pe.wait_ge(sum_ready, 1)
                last = run_rows(PNA_W, SMALLB)[:, 1, SMALLB - 1, :]
                nc.tensor.transpose(psT[0][:, 0:P], last[:, 0:P], ident[:, :])
                nc.tensor.transpose(psT[1][:, 0:P], last[:, P:2 * P], ident[:, :]).then_inc(sum_done, 1)
                pe.wait_ge(sum_ready, 2)
                nc.tensor.transpose(psO[0][:, 0:P], cA[:, 0:P], ident[:, :])
                nc.tensor.transpose(psO[0][:, P:2 * P], cD[:, 0:P], ident[:, :]).then_inc(sum_done, 1)
                for s in range(T + 1):
                    if s < T:
                        k = NG + s
                        if s % FIFTH == 0:
                            pe.wait_ge(act_done, s // FIFTH + 1)
                        pe.wait_ge(xt_ready, k - 1)
                        for i in range(3):
                            nc.tensor.transpose(psT[k % 2][:, i * P:(i + 1) * P], feats[:, s, i * P:(i + 1) * P], ident[:, :])
                        nc.tensor.transpose(psT[k % 2][0:F, 3 * P:4 * P], Hn[:, s, :], ident[:, :]).then_inc(transposed, 1)
                    if s >= 1:
                        k = NG + s - 1
                        pe.wait_ge(xt_ready, k + 1)
                        pe.wait_ge(evacuated, k - 1)
                        for i in range(3):
                            nc.tensor.matmul(psO[k % 2][:, 0:3 * F], XT[:, k % 2, i * P:(i + 1) * P],
                                             wu[:, i, :, :].rearrange("p g n -> p (g n)"), start=(i == 0), stop=False)
                        nc.tensor.matmul(psO[k % 2][:, 0:F], XT[0:F, k % 2, 3 * P:4 * P], wu0[:, :], start=False,
                                         stop=True).then_inc(product_done, 1)
                total(3)
                total(4)
                pe.wait_ge(operands_ready, 2)
                group_products(Y, wmix[:, :], F, NG + T)
                total(5)
                total(6)
                meet(pe, "pe")

            for k in range(2):
                relation_products(wrel[k])
                carry_attention(RGAT, 0)
                meet(pe, "pe")

            relation_products(wrel[2])
            pe.wait_ge(sum_ready, 1)
            nc.tensor.transpose(psT[0][0:F, 0:P], run_rows(F, SMALLB)[:, 1, SMALLB - 1, :], ident[:, :]).then_inc(sum_done, 1)
            pe.wait_ge(sum_ready, 2)
            nc.tensor.transpose(psO[0][:, 0:F], cD[0:F, 0:P], ident[0:F, 0:F]).then_inc(sum_done, 1)

        @block.scalar
        def _(act):
            asked = [0]

            def func(out, in_, fn, **kw):
                asked[0] += 1
                act.wait_ge(act_asked, asked[0])
                nc.scalar.activation(out, in_, fn, **kw).then_inc(act_done, 1)

            def end():
                asked[0] = 0
                meet(act, "act")

            def group_copies(k0, per_slot=False):
                for g, slots in enumerate(GROUPS):
                    k, n = k0 + g, len(slots) * P
                    act.wait_ge(transposed, k + 1)
                    if k >= 2:
                        act.wait_ge(product_done, G * (g - 1) if per_slot else k - 1)
                    nc.scalar.copy(XT[0:F, k % 2, 0:n], psT[k % 2][0:F, 0:n]).then_inc(xt_ready, 1)

            def layer_norm():
                func(s1[:, :], s2[:, :], ACT.Sqrt)

            def edge_attention(a):
                mv = messages(a.A, BIGB)
                with act.Fori(0, pairs(BIGB)) as b:
                    for h in range(2):
                        act.wait_ge(scores_ready, b * 2 + h + 1)
                        nc.scalar.activation(decay[:, 0:a.H, :], decay[:, 0:a.H, :], ACT.Exp).then_inc(msgs_ready, 1)
                        nc.scalar.activation(mv[:, h].rearrange("p j (k d) -> p j k d", k=a.H)[:, :, :, a.D],
                                             expo[:, :, 0:a.H], ACT.Exp).then_inc(msgs_ready, 1)
                func(cB[0:a.A, :], cB[0:a.A, :], ACT.Exp)
                func(cC[0:a.A, :], cC[0:a.A, :], ACT.Exp)
                func(fw[:, 0:2, 0:a.H], fw[:, 0:2, 0:a.H], ACT.Exp)

            layer_norm()
            group_copies(0)
            func(s2[:, :], s1[:, :], ACT.Ln)
            edge_attention(GAT)
            func(Z[:, :, :], Z[:, :, :], ACT.Exp)
            layer_norm()
            end()
            NG = len(GROUPS)
            with act.Fori(0, LAYERS) as layer:
                group_copies(0)
                mv = messages(PNA_M, SMALLB)

                def next_near(b):
                    act.wait_ge(near_in, b * 16 + 16)
                    nc.scalar.activation(near, near_src, ACT.Identity, bias=first_node[:, 0:1]).then_inc(near_ready, 1)
                    act.wait_ge(near_ready, b + 1)
                    act.sem_inc(gathering, 1)
                    load_near(b + 1)

                def load_near(b):
                    src = t["src_near"][bass.ds(b, 1), :].rearrange("b e -> (b e)").partition_broadcast(P)
                    act.dma_start(near_src, src).then_inc(near_in, 16)

                def messages_of(rows_, b, h, some):
                    nc.scalar.activation(mv[:, h, some, 0:F], rows_, ACT.Copy, scale=-1.0).then_inc(msgs_ready, 1)
                    nc.scalar.activation(mv[:, h, some, F:2 * F], rows_, ACT.Copy).then_inc(msgs_ready, 1)
                    nc.scalar.activation(mv[:, h, some, 2 * F:], rows_, ACT.Square).then_inc(msgs_ready, 1)

                def gathered_messages(b, h):
                    act.wait_ge(msgs_free, b * 2 + h + 1)
                    act.sem_inc(gathering, 1)
                    now = slice(h * SMALLB, (h + 1) * SMALLB)
                    nc.scalar.activation(cont_now[:, now], cont[:, cols(b, h, SMALLB)], ACT.Copy).then_inc(msgs_ready, 1)
                    nc.scalar.activation(negs_now[:, now], start[:, cols(b, h, SMALLB)], ACT.Copy,
                                         scale=-BIG).then_inc(msgs_ready, 1)
                    act.wait_ge(rows_in["pna"][h], (layer * pairs(SMALLB) + b + 1) * 16 * OWN)
                    messages_of(landing[h], b, h, slice(0, OWN))
                    act.wait_ge(msgs_ready, (b * 2 + h) * 8 + 5 + 3 * h)
                    act.sem_inc(rows_free, 1)

                def picked_messages(b, h):
                    messages_of(picked[:, h].rearrange("p (j f) -> p j f", j=PICK), b, h, slice(OWN, SMALLB))

                def pair_messages(b, more):
                    gathered_messages(b, 0)
                    if more:
                        act.wait_ge(onehot_ready, b * T + T)
                        next_near(b + 1)
                    act.wait_ge(picked_done, b + 1)
                    picked_messages(b, 0)
                    act.wait_ge(msgs_free, b * 2 + 2)
                    picked_messages(b, 1)
                    act.wait_ge(msgs_ready, b * 16 + 11)
                    act.sem_inc(picked_free, 1)
                    gathered_messages(b, 1)

                load_near(0)
                next_near(0)
                act.sem_inc(picked_free, 1)
                last = pairs(SMALLB) - 1
                with act.Fori(0, last) as b:
                    pair_messages(b, True)
                pair_messages(last, False)
                act.wait_ge(near_in, 16 * (last + 2))
                for s in range(T + 1):
                    if s < T:
                        k = NG + s
                        if s % FIFTH == 0:
                            some = slice(s, s + FIFTH)
                            func(feats[:, some, 3 * F:4 * F], feats[:, some, 4 * F:5 * F], ACT.Sqrt, bias=tiny[:, 0:1])
                        act.wait_ge(transposed, k + 1)
                        act.wait_ge(product_done, k - 1)
                        nc.scalar.copy(XT[:, k % 2, 0:3 * P], psT[k % 2][:, 0:3 * P])
                        nc.scalar.copy(XT[0:F, k % 2, 3 * P:], psT[k % 2][0:F, 3 * P:]).then_inc(xt_ready, 1)
                    if s >= 1:
                        act.wait_ge(product_done, NG + s)
                        nc.scalar.copy(Y[:, s - 1, :], psO[(NG + s - 1) % 2][:, 0:F]).then_inc(base_ready, 1)
                func(fb[:, :], fc[:, :], ACT.Sqrt)
                group_copies(NG + T)
                func(fb[:, :], fc[:, :], ACT.Sqrt)
                end()
            for k in range(2):
                if k == 0:
                    layer_norm()
                group_copies(0, per_slot=True)
                edge_attention(RGAT)
                if k:
                    layer_norm()
                end()
            group_copies(0, per_slot=True)

        @block.vector
        def _(dve):
            st = Steps(dve, dve_steps)
            V = nc.vector
            asked, sums = [0], [0]

            def tt(out, a, b, op):
                st.do(V.tensor_tensor(out, a, b, op))

            def ts(out, a, x, op, y=None, op1=None):
                if y is None:
                    st.do(V.tensor_scalar(out, a, x, None, op))
                else:
                    st.do(V.tensor_scalar(out, a, x, y, op, op1))

            def copy(out, a):
                st.do(V.tensor_copy(out, a))

            def ask(wait=True):
                asked[0] += 1
                dve.sem_inc(act_asked, 1)
                if wait:
                    dve.wait_ge(act_done, asked[0])

            def ask_pe(wait=True):
                sums[0] += 1
                dve.sem_inc(sum_ready, 1)
                if wait:
                    dve.wait_ge(sum_done, sums[0])

            def end():
                st.reset()
                asked[0] = sums[0] = 0
                meet(dve, "dve")

            def over_t(x, w=F):
                return bc(x.unsqueeze(2), [P, x.shape[1], w])

            def over_f(x):
                return bc(x.unsqueeze(1), [P, T, F])

            def layer_norm():
                st.do(V.tensor_reduce(s3[:, :], X[:, :, :], AX.X, ALU.add))
                ts(s3[:, :], s3[:, :], 1.0 / F, ALU.mult)
                tt(Hn[:, :, :], X[:, :, :], over_t(s3[:, :]), ALU.subtract)
                tt(Z[:, :, :], Hn[:, :, :], Hn[:, :, :], ALU.mult)
                st.do(V.tensor_reduce(s2[:, :], Z[:, :, :], AX.X, ALU.add))
                ts(s2[:, :], s2[:, :], 1.0 / F, ALU.mult, 1e-5, ALU.add)
                ask()
                st.do(V.reciprocal(s3[:, :], s1[:, :]))
                tt(Hn[:, :, :], Hn[:, :, :], over_t(s3[:, :]), ALU.mult)
                ts(Hn[:, :, :], Hn[:, :, :], 0.0, ALU.max)

            def batch_norm(buf, gamma, beta):
                def sum_of(of):
                    st.do(V.tensor_reduce(fa[:, :], of.rearrange("p t f -> p f t"), AX.X, ALU.add))
                    ask_pe()

                sum_of(buf)
                ts(fb[:, :], psR[:, 0:F], 1.0 / N, ALU.mult)
                tt(buf, buf, over_f(fb[:, :]), ALU.subtract)
                tt(Z[:, :, :], buf, buf, ALU.mult)
                sum_of(Z[:, :, :])
                ts(fc[:, :], psR[:, 0:F], 1.0 / N, ALU.mult, 1e-5, ALU.add)
                ask()
                st.do(V.reciprocal(fb[:, :], fb[:, :]))
                tt(fb[:, :], fb[:, :], gamma, ALU.mult)
                tt(buf, buf, over_f(fb[:, :]), ALU.mult)
                tt(buf, buf, over_f(beta), ALU.add)

            def block_masks(b, h, n, extra=None):
                st.add(V.tensor_copy(cont_now[:, 0:n], cont[:, cols(b, h, n)]))
                st.add(V.tensor_scalar(negs_now[:, 0:n], start[:, cols(b, h, n)], -BIG, None, ALU.mult))
                if extra is not None:
                    st.add(V.tensor_copy(extra_now[:, 0:n], extra[:, cols(b, h, n)]))
                st.wait()

            def finish_block(h, used):
                st.wait()
                dve.sem_inc(used, 1)
                dve.sem_inc(block_done[h], 1)
                st.reset()

            def scan(out, data0, data1, initial, op0, op1):
                return V.tensor_tensor_scan(out, data0, data1, initial, op0, op1)

            def evacuate(k0, n, take):
                for g, slots in enumerate(GROUPS):
                    k = k0 + g
                    dve.wait_ge(product_done, k + 1)
                    take(slice(slots[0], slots[-1] + 1), psO[k % 2][:, 0:len(slots) * n].rearrange(
                        "p (s n) -> p s n", n=n))
                    st.wait()
                    dve.sem_inc(evacuated, 1)

            def edge_attention(a, key):
                n = BIGB
                landed = rows_in[key]
                rv, mv, qv = run_rows(a.W, n), messages(a.A, n), dst_scores(a.QW)
                st.do(V.memset(rv[:, 1, n - 1, :], 0.0))
                st.do(V.memset(maxrun[:, :, :], -BIG))
                dve.wait_ge(q_first_in[key], 16)
                st.reset()
                with dve.Fori(0, pairs(n)) as b:
                    for h in range(2):
                        block_masks(b, h, n, etyf if a.R > 1 else None)
                        dve.wait_ge(spread_in[h], b * 16 + 16)
                        for c in range(a.QW):
                            st.add(scan(qv[:, h, :, c], cont_now[:, :], qv[:, h, :, c], qlast[:, c:c + 1], ALU.mult, ALU.add))
                        st.wait()
                        if a.R == 1:
                            q = qv[:, h]
                        else:
                            tt(onehot[:, :, :], bc(iota_f[:, 0:REL].unsqueeze(1), [P, n, REL]),
                               bc(extra_now[:, :].unsqueeze(2), [P, n, REL]), ALU.is_equal)
                            tt(qsel[:, :, :, :], qv[:, h].rearrange("p j (k r) -> p j k r", k=a.H),
                               bc(onehot[:, :, :].unsqueeze(2), [P, n, a.H, REL]), ALU.mult)
                            st.do(V.tensor_reduce(expo[:, :, :], qsel[:, :, :, :], AX.X, ALU.add))
                            q = expo[:, :, 0:a.H]
                        copy(qlast[:, 0:a.QW], qv[:, h, n - 1, :])
                        dve.wait_ge(landed[h], (b + 1) * 16 * n)
                        tt(score[:, :, 0:a.H], q, gath[:, h, :, F:F + a.H], ALU.add)
                        st.do(V.scalar_tensor_tensor(score[:, :, 0:a.H], score[:, :, 0:a.H], 0.2, score[:, :, 0:a.H],
                                                     ALU.mult, ALU.max))
                        for k in range(a.H):
                            st.add(scan(maxrun[:, k, 1:], negs_now[:, :], score[:, :, k], maxrun[:, k, 0:1],
                                        ALU.add, ALU.max))
                        st.wait()
                        st.add(V.tensor_tensor(expo[:, :, 0:a.H], score[:, :, 0:a.H],
                                               maxrun[:, 0:a.H, 1:].rearrange("p k j -> p j k"), ALU.subtract))
                        tt(decay[:, 0:a.H, :], maxrun[:, 0:a.H, 0:n], maxrun[:, 0:a.H, 1:], ALU.subtract)
                        ts(decay[:, 0:a.H, :], decay[:, 0:a.H, :], 0.0, ALU.min)
                        dve.sem_inc(scores_ready, 1)
                        dve.wait_ge(runs_free[h], b + 1)
                        st.add(V.tensor_copy(rv[:, h, :, a.A:], maxrun[:, 0:a.H, 1:].rearrange("p k j -> p j k")))
                        copy(maxrun[:, 0:a.H, 0:1], maxrun[:, 0:a.H, n:])
                        dve.wait_ge(msgs_ready, (b * 2 + h) * 2 + 2)
                        m4 = mv[:, h].rearrange("p j (k d) -> p j k d", k=a.H)
                        st.add(V.tensor_tensor(decay[:, 0:a.H, :], decay[:, 0:a.H, :],
                                               bc(cont_now[:, :].unsqueeze(1), [P, a.H, n]), ALU.mult))
                        tt(m4[:, :, :, 0:a.D], gath[:, h, :, 0:F].rearrange("p j (k d) -> p j k d", k=a.H),
                           bc(m4[:, :, :, a.D:], [P, n, a.H, a.D]), ALU.mult)
                        if a.H == 1:
                            for j in range(n):
                                before = rv[:, h, j - 1, :] if j else rv[:, 1 - h, n - 1, :]
                                st.do(V.scalar_tensor_tensor(rv[:, h, j, 0:a.A], before[:, 0:a.A], decay[:, 0, j:j + 1],
                                                             mv[:, h, j, :], ALU.mult, ALU.add))
                        else:
                            for c in range(a.A):
                                st.add(scan(rv[:, h, :, c], decay[:, c // a.D1, :], mv[:, h, :, c],
                                            rv[:, 1 - h, n - 1, c:c + 1], ALU.mult, ALU.add))
                        finish_block(h, rows_free)
                last = rv[:, 1, n - 1, :]
                copy(before_c[:, 0:a.A].rearrange("p (k d) -> p k d", k=a.H),
                     bc(last[:, a.A:].unsqueeze(2), [P, a.H, a.D1]))
                st.add(V.memset(cA[:, 0:1], -BIG))
                st.do(V.memset(cD[:, 0:1], 0.0))
                ask_pe()
                maxT, lastT = psT[0][0:a.A, 0:P], psT[0][0:a.A, P:2 * P]
                st.do(scan(cA[0:a.A, 1:], negT[0:a.A, :], maxT, -BIG, ALU.add, ALU.max))
                tt(cB[0:a.A, :], cA[0:a.A, 0:P], cA[0:a.A, 1:], ALU.subtract)
                ts(cB[0:a.A, :], cB[0:a.A, :], 0.0, ALU.min)
                ask(False)
                tt(cC[0:a.A, :], maxT, cA[0:a.A, 1:], ALU.subtract)
                ask()
                st.add(V.tensor_tensor(cB[0:a.A, :], cB[0:a.A, :], contT[0:a.A, :], ALU.mult))
                tt(cC[0:a.A, :], lastT, cC[0:a.A, :], ALU.mult)
                st.do(scan(cD[0:a.A, 1:], cB[0:a.A, :], cC[0:a.A, :], 0.0, ALU.mult, ALU.add))
                ask_pe()
                st.add(V.tensor_copy(before_c[:, 0:a.A], psO[0][:, 0:a.A]))
                copy(before_c[:, a.A:a.W], psO[0][:, P:P + a.A].rearrange("p (k d) -> p k d", k=a.H)[:, :, 0])
                dve.wait_ge(fix_in[key], 16)
                mf, mb = fixed[:, a.A:a.W], before_c[:, a.A:a.W]
                tt(fw[:, 2, 0:a.H], mf, mb, ALU.max)
                st.add(V.tensor_tensor(fw[:, 0, 0:a.H], mf, fw[:, 2, 0:a.H], ALU.subtract))
                tt(fw[:, 1, 0:a.H], mb, fw[:, 2, 0:a.H], ALU.subtract)
                ask()
                f3 = fixed[:, 0:a.A].rearrange("p (k d) -> p k d", k=a.H)
                b3 = before_c[:, 0:a.A].rearrange("p (k d) -> p k d", k=a.H)
                st.add(V.tensor_tensor(f3, f3, bc(fw[:, 0, 0:a.H].unsqueeze(2), [P, a.H, a.D1]), ALU.mult))
                tt(b3, b3, bc(fw[:, 1, 0:a.H].unsqueeze(2), [P, a.H, a.D1]), ALU.mult)
                tt(f3, f3, b3, ALU.add)
                dve.sem_inc(fixed_ready, 1)
                dve.wait_ge(nodes_in[key][0], 16 * T)
                n4 = node_rows(a.W)[:, :, 0:a.A].rearrange("p t (k d) -> p t k d", k=a.H)
                if a.R > 1:
                    ts(n4[:, :, :, a.D], n4[:, :, :, a.D], 1e-16, ALU.add)
                tt(hw1[:, :, 0:a.H], n4[:, :, :, a.D], over_t(hasnot[:, :], a.H), ALU.add)
                st.do(V.reciprocal(hw1[:, :, 0:a.H], hw1[:, :, 0:a.H]))
                tt(Z[:, :, :].rearrange("p t (k d) -> p t k d", k=a.H), n4[:, :, :, 0:a.D],
                   bc(hw1[:, :, 0:a.H].unsqueeze(3), [P, T, a.H, a.D]), ALU.mult)

            st.add(V.memset(zeros, 0.0))
            st.add(V.memset(fixed[:, :], 0.0))
            st.do(V.memset(tiny[:, :], 1e-30))
            dve.sem_inc(zeros_stand, 1)
            dve.wait_ge(x_in, 16 * 5)
            layer_norm()
            dve.wait_ge(sum_done, 1)
            copy(wT[:, :], psR[0:F, 0:F])
            sums[0] = 1
            ask_pe()
            copy(wgat[:, F:F + 2], psR[0:F, F:F + 2])
            dve.sem_inc(operands_ready, 1)

            def take_gat(sl, ps):
                st.add(V.tensor_copy(gat_rows[:, sl, :], ps[:, :, 0:GAT.GW]))
                st.add(V.tensor_copy(s4[:, sl], ps[:, :, GAT.GW]))

            evacuate(0, F + 2, take_gat)
            dve.sem_inc(table_ready, 1)
            dve.wait_ge(consts_stand, 1)
            copy(iota_f[:, :], iota_i[:, :])
            copy(iota_e, bc(iota_i[:, :].unsqueeze(2), [P, P, BIGB]))
            dve.wait_ge(loads_in, 16 * 4)
            copy(dstf, dsti)
            copy(dst0_i[:, :], dsti[:, 0:1])
            copy(prevf, prevd)
            tt(start[:, :], dstf, prevf, ALU.not_equal)
            ts(cont[:, :], start[:, :], -1.0, ALU.mult, 1.0, ALU.add)
            copy(etyf[:, :], reli[:, :])
            copy(prevf, srci[:, :])
            st.do(V.scalar_tensor_tensor(prevf, prevf, float(REL), etyf[:, :], ALU.mult, ALU.add))
            copy(reli[:, :], prevf)

            def floor_of(x, step):
                ts(x, x, 0.5, ALU.add, 1.0 / step, ALU.mult)
                ts(x, x, -0.5, ALU.add)
                ts(x, x, ROUND, ALU.add)
                ts(x, x, -ROUND, ALU.add)

            copy(qf, dstf)
            floor_of(qf, T)
            st.do(V.scalar_tensor_tensor(tf, qf, -float(T), dstf, ALU.mult, ALU.add))
            copy(qb, qf)
            copy(tb, tf)
            st.reset()
            dve.sem_inc(oh_used, 2)
            with dve.Fori(0, pairs(BIGB)) as b:
                for h in range(2):
                    st.add(V.tensor_copy(q_now[:, :], qb[:, cols(b, h, BIGB)]))
                    st.add(V.tensor_copy(t_now[:, :], tb[:, cols(b, h, BIGB)]))
                    st.wait()
                    dve.wait_ge(oh_used, b * 2 + h + 1)
                    st.add(V.tensor_tensor(oh_q[:, h], iota_e, bc(q_now[:, :].unsqueeze(1), [P, P, BIGB]), ALU.is_equal))
                    st.add(V.tensor_tensor(oh_t[:, h], iota_e[:, 0:T, :], bc(t_now[:, :].unsqueeze(1), [P, T, BIGB]),
                                           ALU.is_equal))
                    st.wait()
                    dve.sem_inc(oh_ready, 1)
                    st.reset()
            dve.wait_ge(sum_done, 3)
            sums[0] = 3 - 1
            copy(deg[:, :], psH[:, 0:T])
            ts(has[:, :], deg[:, :], 0.0, ALU.is_gt)
            ts(hasnot[:, :], has[:, :], -1.0, ALU.mult, 1.0, ALU.add)
            st.do(V.memset(s1[:, :], 1.0))
            st.do(scan(s2[:, :], s1[:, :], deg[:, :], 0.0, ALU.mult, ALU.add))
            copy(col1[:, :], s2[:, T - 1:T])
            dve.sem_inc(sum_ready, 1)
            dve.wait_ge(sum_done, 4)
            copy(col2[:, :], psS[0][:, 0:1])
            ts(s2[:, :], s2[:, :], col2[:, 0:1], ALU.add)
            tt(s1[:, :], s2[:, :], deg[:, :], ALU.subtract)
            ts(s2[:, :], s2[:, :], -1.0, ALU.add)
            st.do(V.scalar_tensor_tensor(s1[:, :], hasnot[:, :], float(NO_EDGE), s1[:, :], ALU.mult, ALU.add))
            copy(start_i[:, :], s1[:, :])
            tt(s2[:, :], s2[:, :], has[:, :], ALU.mult)
            st.do(V.scalar_tensor_tensor(s2[:, :], hasnot[:, :], float(EP), s2[:, :], ALU.mult, ALU.add))
            copy(end_i[:, :], s2[:, :])
            dve.sem_inc(starts_ready, 1)
            st.do(V.tensor_reduce(col1[:, :], start[:, :], AX.X, ALU.max))
            ts(col1[:, :], col1[:, :], -1.0, ALU.mult, 1.0, ALU.add)
            copy(cB[:, :], bc(col1[:, :], [P, P]))
            dve.sem_inc(sum_ready, 1)
            dve.wait_ge(sum_done, 5)
            copy(contT[:, :], psS[1][:, 0:P])
            ts(negT[:, :], contT[:, :], -1.0, ALU.add, BIG, ALU.mult)
            ts(s3[:, :], deg[:, :], 1.0, ALU.max)
            st.do(V.reciprocal(rden[:, :], s3[:, :]))
            ts(s1[:, :], deg[:, :], 1.0, ALU.add)
            ask()
            ts(amp[:, :], s2[:, :], 1.0 / 2.5, ALU.mult)
            tt(s3[:, :], hasnot[:, :], s2[:, :], ALU.add)
            st.do(V.reciprocal(s3[:, :], s3[:, :]))
            ts(s3[:, :], s3[:, :], 2.5, ALU.mult)
            tt(att[:, :], s3[:, :], has[:, :], ALU.mult)
            dve.wait_ge(end0_in, 16)
            copy(col1[:, :], end0_i[:, :])
            copy(col2[:, :], col1[:, :])
            floor_of(col2[:, :], C)
            copy(col3[:, :], part_i[:, :])
            ts(first_node[:, :], col3[:, :], -float(T), ALU.mult)
            tt(col2[:, :], col2[:, :], col3[:, :], ALU.is_equal)
            tt(col2[:, :], col2[:, :], cont[:, 0:1], ALU.mult)
            ts(col3[:, :], col2[:, :], -float(NO_EDGE), ALU.mult, float(NO_EDGE), ALU.add)
            tt(col3[:, :], col3[:, :], col1[:, :], ALU.add)
            copy(fix_i[:, :], col3[:, :])
            dve.wait_ge(weights_in, 16 * (5 + 8 + 3))
            sums[0] = 5
            for k in range(2):
                for r in range(REL):
                    dve.sem_inc(sum_ready, 1)
                    dve.wait_ge(sum_done, 6 + 2 * (k * REL + r))
                    copy(wT[:, :], psR[0:F, 0:F])
                    dve.sem_inc(sum_ready, 1)
                    dve.wait_ge(sum_done, 7 + 2 * (k * REL + r))
                    st.add(V.tensor_copy(wrel[k][:, REL * F + 4 * r:REL * F + 4 * r + 4], psS[0][0:F, 0:4]))
                    copy(wrel[k][:, REL * F + 32:].rearrange("f (k r) -> f k r", r=REL)[:, :, r], psS[0][0:F, 4:8])
            sums[0] = 5 + 4 * REL
            dve.wait_ge(zero_filled, 16 * 7)
            edge_attention(GAT, "gat")
            ts(Y[:, :, :], Z[:, :, :], 0.0, ALU.max)
            ts(Z[:, :, :], Z[:, :, :], 0.0, ALU.min)
            ask()
            st.do(V.scalar_tensor_tensor(Y[:, :, :], Z[:, :, :], -1.0, Y[:, :, :], ALU.add, ALU.add))
            tt(X[:, :, :], X[:, :, :], Y[:, :, :], ALU.add)
            layer_norm()
            end()

            NG = len(GROUPS)
            with dve.Fori(0, LAYERS) as layer:
                st.add(V.tensor_copy(bm_now[:, :], bm[:, bass.ds(layer * F, F)]))
                copy(wm_now[:, :, :], wm[:, bass.ds(layer, 1), :, :].rearrange("f l k n -> f (l k) n"))
                dve.sem_inc(operands_ready, 1)

                def take_pna(sl, ps):
                    n = sl.stop - sl.start
                    st.add(V.tensor_copy(Y[:, sl, :], ps[:, :, 0:F]))
                    tt(Bn[:, sl, :], ps[:, :, F:2 * F], bc(bm_now[:, :].unsqueeze(1), [P, n, F]), ALU.add)

                evacuate(0, 2 * F, take_pna)
                dve.sem_inc(table_ready, 1)
                rest = nodes[:, 0:T * F].rearrange("p (t f) -> p t f", t=T)
                st.add(V.memset(nothing, 0.0))
                copy(parts[0], Y[:, :, :])
                tt(rest, Y[:, :, :], parts[0], ALU.subtract)
                copy(parts[1], rest)
                tt(rest, rest, parts[1], ALU.subtract)
                copy(parts[2], rest)
                dve.sem_inc(parts_ready, 1)
                dve.sem_inc(onehot_used, RING)
                dve.sem_inc(msgs_free, 2)

                def one_hot(b, s):
                    dve.wait_ge(onehot_used, b * T + s + 1)
                    V.tensor_scalar(ring[s % RING], near, float(s), None, ALU.is_equal).then_inc(onehot_ready, 1)

                dve.wait_ge(near_ready, 1)
                for s in range(T):
                    one_hot(0, s)
                tt(Bn[:, :, :], Bn[:, :, :], over_t(has[:, :]), ALU.mult)
                tt(Bd[:, :, :], Bn[:, :, :], over_t(deg[:, :]), ALU.mult)
                n = SMALLB
                rv, mv = run_rows(PNA_W, n), messages(PNA_M, n)
                st.do(V.memset(rv[:, 1, n - 1, 0:2 * F], -BIG))
                st.do(V.memset(rv[:, 1, n - 1, 2 * F:], 0.0))
                st.reset()

                def block_pair(b, one_hots):
                    if one_hots:
                        dve.wait_ge(near_ready, b + 2)
                    s = 0
                    for h in range(2):
                        dve.wait_ge(msgs_ready, (b * 2 + h) * 8 + 8)
                        dve.sem_inc(gathering, 1)
                        dve.wait_ge(runs_free[h], b + 1)
                        for j in range(n):
                            before = rv[:, h, j - 1, :] if j else rv[:, 1 - h, n - 1, :]
                            if j:
                                st.wait(st.n - 1)
                            st.add(V.scalar_tensor_tensor(rv[:, h, j, 0:2 * F], before[:, 0:2 * F],
                                                          negs_now[:, h * n + j:h * n + j + 1], mv[:, h, j, 0:2 * F], ALU.add, ALU.max))
                            if j:
                                st.wait(st.n - 1)
                            st.add(V.scalar_tensor_tensor(rv[:, h, j, 2 * F:], before[:, 2 * F:],
                                                          cont_now[:, h * n + j:h * n + j + 1], mv[:, h, j, F:], ALU.mult, ALU.add))
                            for _ in range((2 if j < 5 and not h else 1) if one_hots and s < T else 0):
                                one_hot(b + 1, s)
                                s += 1
                        finish_block(h, msgs_free)

                with dve.Fori(0, pairs(n) - 1) as b:
                    block_pair(b, True)
                block_pair(pairs(n) - 1, False)
                st.add(V.memset(cA[:, 0:1], -BIG))
                st.do(V.memset(cD[:, 0:1], 0.0))
                ask_pe()
                st.add(scan(cA[:, 1:], negT[:, :], psT[0][:, 0:P], -BIG, ALU.add, ALU.max))
                st.do(scan(cD[:, 1:], contT[:, :], psT[1][:, 0:P], 0.0, ALU.mult, ALU.add))
                ask_pe()
                dve.wait_ge(fix_in["pna"], layer * 16 + 16)
                st.add(V.tensor_tensor(fixed[:, 0:2 * F], psO[0][:, 0:P], fixed[:, 0:2 * F], ALU.max))
                tt(fixed[:, 2 * F:], psO[0][:, P:2 * P], fixed[:, 2 * F:], ALU.add)
                dve.sem_inc(fixed_ready, 1)
                dve.wait_ge(loads_in, 16 * 11)
                ts(par[:, 0, :], par[:, 0, :], 1.0 / float(N) ** 0.5, ALU.mult)

                def aggregates(g):
                    sl = slice(g * FIFTH, (g + 1) * FIFTH)
                    nmax, amax, asum, asq = (node_rows(PNA_W)[:, sl, k * F:(k + 1) * F] for k in range(4))
                    mean, mx, mn, _, var, s_ = (feats[:, sl, k * F:(k + 1) * F] for k in range(6))
                    dve.wait_ge(nodes_in["pna"][g], (layer + 1) * 16 * FIFTH)
                    st.add(V.tensor_tensor(Z[:, sl, :], asum, over_t(rden[:, sl]), ALU.mult))
                    st.add(V.tensor_tensor(var, asq, over_t(rden[:, sl]), ALU.mult))
                    tt(s_, asum, Bd[:, sl, :], ALU.add)
                    tt(Z[:, sl, :], Z[:, sl, :], Z[:, sl, :], ALU.mult)
                    st.add(V.tensor_tensor(mx, amax, Bn[:, sl, :], ALU.add))
                    tt(var, var, Z[:, sl, :], ALU.subtract)
                    st.add(V.tensor_tensor(mn, Bn[:, sl, :], nmax, ALU.subtract))
                    st.add(V.tensor_scalar(var, var, 0.0, None, ALU.max))
                    tt(mean, s_, over_t(rden[:, sl]), ALU.mult)
                    ask(False)

                aggregates(0)
                for g in range(5):
                    if g < 4:
                        aggregates(g + 1)
                    for s in range(g * FIFTH, (g + 1) * FIFTH):
                        ps = psO[(NG + s) % 2]
                        dve.wait_ge(base_ready, s + 1)
                        st.do(V.scalar_tensor_tensor(Y[:, s, :], ps[:, F:2 * F], amp[:, s:s + 1], Y[:, s, :],
                                                     ALU.mult, ALU.add))
                        st.do(V.scalar_tensor_tensor(Y[:, s, :], ps[:, 2 * F:3 * F], att[:, s:s + 1], Y[:, s, :],
                                                     ALU.mult, ALU.add))
                        dve.sem_inc(evacuated, 1)
                st.do(V.scalar_tensor_tensor(Y[:, :, :], Y[:, :, :], 1.0 / float(N) ** 0.5, over_f(par[:, 0, :]),
                                             ALU.mult, ALU.add))
                batch_norm(Y[:, :, :], par[:, 1, :], par[:, 2, :])
                dve.sem_inc(operands_ready, 1)

                def take_mix(sl, ps):
                    st.add(V.tensor_tensor(Bn[:, sl, :], ps, bc(par[:, 3, :].unsqueeze(1), [P, sl.stop - sl.start, F]),
                                           ALU.add))

                evacuate(NG + T, F, take_mix)
                st.do(V.scalar_tensor_tensor(Bn[:, :, :], Bn[:, :, :], 0.01, Bn[:, :, :], ALU.mult, ALU.max))
                tt(Y[:, :, :], Bn[:, :, :], Hn[:, :, :], ALU.add)
                batch_norm(Y[:, :, :], par[:, 4, :], par[:, 5, :])
                st.do(V.scalar_tensor_tensor(Hn[:, :, :], Y[:, :, :], 0.0, Hn[:, :, :], ALU.max, ALU.add))
                end()

            def evacuate_relations(w, take):
                for s in range(T):
                    tv = tab[:, s % 2, 0:REL * w].rearrange("p (r w) -> p r w", r=REL)
                    dve.wait_ge(product_done, s + 1)
                    if s >= 2:
                        dve.wait_ge(tab_stored[s % 2], 16 * (s // 2))
                    take(s, tv, psO[s % 2][:, :].rearrange("p (r w) -> p r w", r=REL), psS[s % 2])
                    st.wait()
                    dve.sem_inc(evacuated, 1)

            def take_rgat(s, tv, ps, small):
                st.add(V.tensor_copy(tv[:, :, 0:F], ps))
                st.add(V.tensor_copy(tv[:, :, F:], small[:, 0:32].rearrange("p (r w) -> p r w", r=REL)))
                st.add(V.tensor_copy(QN[:, s, :], small[:, 32:64]))

            for k in range(2):
                if k == 0:
                    tt(X[:, :, :], X[:, :, :], Hn[:, :, :], ALU.add)
                    layer_norm()
                dve.sem_inc(operands_ready, 1)
                evacuate_relations(RGAT.GW, take_rgat)
                edge_attention(RGAT, f"rgat{k}")
                tt(Z[:, :, :], Z[:, :, :], over_f(brow[:, k, :]), ALU.add)
                if k == 0:
                    ts(Hn[:, :, :], Z[:, :, :], 0.0, ALU.max)
                else:
                    tt(X[:, :, :], X[:, :, :], Z[:, :, :], ALU.add)
                    layer_norm()
                end()

            def take_rgcn(s, tv, ps, small):
                st.add(V.tensor_tensor(tv, ps, bc(brow[:, 2, :].unsqueeze(1), [P, REL, F]), ALU.add))
                st.add(V.tensor_copy(Bn[:, s, :], small[:, 0:F]))

            dve.sem_inc(operands_ready, 1)
            evacuate_relations(F, take_rgcn)
            n = SMALLB
            rv, mv = run_rows(F, n), messages(F, n)
            st.do(V.memset(rv[:, 1, n - 1, :], 0.0))
            st.reset()
            with dve.Fori(0, pairs(n)) as b:
                for h in range(2):
                    block_masks(b, h, n, wgt)
                    dve.wait_ge(rows_in["rgcn"][h], (b + 1) * 16 * n)
                    tt(mv[:, h], gath[:, h, 0:n, 0:F], bc(extra_now[:, 0:n].unsqueeze(2), [P, n, F]), ALU.mult)
                    dve.wait_ge(runs_free[h], b + 1)
                    for j in range(n):
                        before = rv[:, h, j - 1, :] if j else rv[:, 1 - h, n - 1, :]
                        st.do(V.scalar_tensor_tensor(rv[:, h, j, :], before, cont_now[:, j:j + 1], mv[:, h, j, :],
                                                     ALU.mult, ALU.add))
                    finish_block(h, rows_free)
            st.do(V.memset(cD[:, 0:1], 0.0))
            ask_pe()
            st.do(scan(cD[0:F, 1:], contT[0:F, :], psT[0][0:F, 0:P], 0.0, ALU.mult, ALU.add))
            ask_pe()
            dve.wait_ge(fix_in["rgcn"], 16)
            tt(fixed[:, 0:F], psO[0][:, 0:F], fixed[:, 0:F], ALU.add)
            dve.sem_inc(fixed_ready, 1)
            dve.wait_ge(nodes_in["rgcn"][0], 16 * T)
            tt(Z[:, :, :], node_rows(F), Bn[:, :, :], ALU.add)
            tt(X[:, :, :], X[:, :, :], Z[:, :, :], ALU.add)
            dve.sem_inc(result_ready, 1)


_WEIGHTS = ("L0_gnn_W", "L0_gnn_a", "L1_gnn_WM", "L1_gnn_bM", "L1_gnn_WU", "L1_gnn_bU", "L1_gnn_gamma_t",
            "L1_gnn_beta_t", "L1_gnn_Wmix", "L1_gnn_bmix", "L1_gnn_gamma_o", "L1_gnn_beta_o", "L2_gnn_W1",
            "L2_gnn_Q1", "L2_gnn_K1", "L2_gnn_b1", "L2_gnn_W2", "L2_gnn_Q2", "L2_gnn_K2", "L2_gnn_b2",
            "L3_gnn_weight", "L3_gnn_h_bias", "L3_gnn_loop_weight")


def kernel(**inputs):
    import numpy as np
    import concourse.bacc as bacc
    from concourse import mybir as mb
    from concourse.bass_utils import run_bass_kernel_spmd

    def padded(a, n, fill=0):
        a = np.asarray(a)
        return np.concatenate([a, np.full((n - a.shape[0],) + a.shape[1:], fill, a.dtype)])

    def near_sources(src):
        a = src.reshape(P, pairs(SMALLB), 2, SMALLB)[:, :, :, OWN:]
        return padded(a.transpose(1, 2, 3, 0).reshape(pairs(SMALLB), 2 * PICK * P), pairs(SMALLB) + 1)

    arrays = {
        "x": padded(inputs["x"], NP),
        "src": padded(inputs["src"], EP).reshape(P, C),
        "src_near": near_sources(padded(inputs["src"], EP)),
        "dst": np.concatenate([np.full((1,), -1, np.int32), padded(inputs["dst"], EP, N)]),
        "edge_type_8": padded(inputs["edge_type_8"], EP).reshape(P, C),
        "edge_weight1": padded(inputs["edge_weight1"], EP).reshape(P, C),
    }
    for name in _WEIGHTS:
        arrays[name] = np.ascontiguousarray(inputs[name])
    nc = bacc.Bacc("TRN2", target_bir_lowering=False, num_devices=1)
    t = {k: nc.dram_tensor(f"in_{k}", a.shape, mb.dt.from_np(a.dtype), kind="ExternalInput").ap()
         for k, a in arrays.items()}
    t["out"] = nc.dram_tensor("out_x", (NP, F), mb.dt.float32, kind="ExternalOutput").ap()
    gnn(nc, t)
    r = run_bass_kernel_spmd(nc, [{f"in_{k}": a for k, a in arrays.items()}], core_ids=[0])
    return r.results[0]["out_x"][0:N]
```

```python
import concourse.bass as bass
from concourse import mybir
from contextlib import ExitStack

f32, i32, bf16 = mybir.dt.float32, mybir.dt.int32, mybir.dt.bfloat16
ALU, ACT, AX = mybir.AluOpType, mybir.ActivationFunctionType, mybir.AxisListType

P = 128
N = 3125
T = 25
NP = P * T
E = 100000
C = 784
BIGB, SMALLB = 28, 14
EP = P * C
F = 64
REL = 8
LAYERS = 4
FULL = N // T
BIG = 1.0e30
G = 4
GROUPS = [range(k, min(k + G, T)) for k in range(0, T, G)]
BIG_GROUPS = [range(k, min(k + 2 * G, T)) for k in range(0, T, 2 * G)]
FIFTH = T // 5
PICK = 3
OWN = SMALLB - PICK
GPICK = 7
RING = 5
NO_EDGE = 1 << 20
ROUND = 12582912.0


class Steps:

    def __init__(self, eng, sem):
        self.eng, self.sem, self.n = eng, sem, 0

    def add(self, ins):
        ins.then_inc(self.sem, 1)
        self.n += 1
        return self.n

    def wait(self, n=None):
        self.eng.wait_ge(self.sem, self.n if n is None else n)

    def do(self, ins):
        self.add(ins)
        self.wait()

    def reset(self):
        if self.n:
            self.wait()
            self.eng.sem_clear(self.sem)
            self.n = 0


class Attention:

    def __init__(self, heads, rels):
        self.H, self.R = heads, rels
        self.D = F // heads
        self.D1 = self.D + 1
        self.A = heads * self.D1
        self.W = self.A + heads
        self.GW = F + heads
        self.QW = rels * heads


GAT, RGAT = Attention(1, 1), Attention(4, REL)
PNA_W = 4 * F
PNA_M = 3 * F


def pairs(b):
    return C // (2 * b)


def gnn(nc, t):
    ctx = ExitStack()
    with ctx:
        def sb(name, shape, dt=f32):
            return ctx.enter_context(nc.sbuf_tensor(name, shape, dt))

        def sem(name):
            return ctx.enter_context(nc.semaphore(name))

        def dram(name, shape, dt=f32):
            return nc.dram_tensor(name, shape, dt).ap()

        gat_table = dram("gat_table", (NP, GAT.GW))
        pna_table = dram("pna_table", (NP, F))
        rgat_table = dram("rgat_table", (NP * REL, RGAT.GW))
        rgcn_table = dram("rgcn_table", (NP * REL, F))
        gat_q = dram("gat_q", (NP, GAT.QW))
        rgat_q = dram("rgat_q", (NP, RGAT.QW))
        gat_spread = dram("gat_spread", (EP, GAT.QW))
        rgat_spread = dram("rgat_spread", (EP, RGAT.QW))
        end_table = dram("end_table", (NP, 1), i32)
        runs = {w: dram(f"runs{w}", (EP + 1, w)) for w in (GAT.W, PNA_W, RGAT.W, F)}

        X = sb("X", [P, T, F])
        Hn = sb("Hn", [P, T, F])
        Bn = sb("Bn", [P, T, F])
        Y = sb("Y", [P, T, F])
        Z = sb("Z", [P, T, F])
        gath = sb("gath", [P, 2, BIGB, F + 4])
        Bd = gath[:, :, :, :].rearrange("p h j w -> p (h j w)")[:, 0:T * F].rearrange("p (t f) -> p t f", t=T)
        msgs = sb("msgs", [P, T * 6 * F])
        rows = sb("rows", [P, 2 * SMALLB * PNA_W])
        nodes = sb("nodes", [P, T * PNA_W])
        qx = sb("qx", [P, 2 * BIGB * 32])
        start = sb("start", [P, C])
        cont = sb("cont", [P, C])
        srci = sb("srci", [P, C], i32)
        reli = sb("reli", [P, C], i32)
        etyf = sb("etyf", [P, C])
        wgt = sb("wgt", [P, C])
        idx_now = sb("idx_now", [P, 2, BIGB], i32)
        cont_now = sb("cont_now", [P, BIGB])
        negs_now = sb("negs_now", [P, BIGB])
        extra_now = sb("extra_now", [P, BIGB])
        q_now = sb("q_now", [P, BIGB], bf16)
        t_now = sb("t_now", [P, BIGB], bf16)
        onehot = sb("onehot", [P, BIGB, REL])
        qsel = sb("qsel", [P, BIGB, 4, REL])
        score = sb("score", [P, BIGB, 4])
        expo = sb("expo", [P, BIGB, 4])
        maxrun = sb("maxrun", [P, 4, 1 + BIGB])
        decay = sb("decay", [P, 4, BIGB])
        qlast = sb("qlast", [P, 32])
        QN = sb("QN", [P, T, 32])
        tab = sb("tab", [P, 2, REL * (F + 4)])
        XT = sb("XT", [P, 2, 512])
        ident = sb("ident", [P, P])
        upper = sb("upper", [P, P])
        realp = sb("realp", [P, P])
        contT = sb("contT", [P, P])
        negT = sb("negT", [P, P])
        cA = sb("cA", [P, P + 1])
        cB = sb("cB", [P, P])
        cC = sb("cC", [P, P])
        cD = sb("cD", [P, P + 1])
        before_c = sb("before_c", [P, PNA_W])
        fixed = sb("fixed", [P, PNA_W])
        fw = sb("fw", [P, 3, 4])
        deg = sb("deg", [P, T])
        has = sb("has", [P, T])
        hasnot = sb("hasnot", [P, T])
        rden = sb("rden", [P, T])
        amp = sb("amp", [P, T])
        att = sb("att", [P, T])
        s1 = sb("s1", [P, T])
        s2 = sb("s2", [P, T])
        s3 = sb("s3", [P, T])
        s4 = sb("s4", [P, T])
        hw1 = sb("hw1", [P, T, 4])
        end_i = sb("end_i", [P, T], i32)
        start_i = sb("start_i", [P, T], i32)
        dst0_i = sb("dst0_i", [P, 1], i32)
        end0_i = sb("end0_i", [P, 1], i32)
        fix_i = sb("fix_i", [P, 1], i32)
        col1 = sb("col1", [P, 1])
        col2 = sb("col2", [P, 1])
        col3 = sb("col3", [P, 1])
        tiny = sb("tiny", [P, 1])
        iota_i = sb("iota_i", [P, P], i32)
        iota_f = sb("iota_f", [P, P])
        part_i = sb("part_i", [P, 1], i32)
        first_node = sb("first_node", [P, 1])
        fa = sb("fa", [P, F])
        fb = sb("fb", [P, F])
        fc = sb("fc", [P, F])
        wrel = [sb(f"wrel{k}", [F, REL * F + F]) for k in range(3)]
        wgat = sb("wgat", [F, F + 2])
        agat = sb("agat", [F, 2])
        wk = sb("wk", [F, 2, REL, 8])
        wT = sb("wT", [F, F])
        wm = sb("wm", [P, LAYERS, 2, F])
        bm = sb("bm", [P, LAYERS * F])
        bm_now = sb("bm_now", [P, F])
        wu0 = sb("wu0", [F, F])
        wu = sb("wu", [P, 3, 3, F])
        wmix = sb("wmix", [P, F])
        par = sb("par", [P, 6, F])
        brow = sb("brow", [P, 3, F])

        dsti = nodes[:, 0:C].bitcast(i32)
        prevd = nodes[:, C:2 * C].bitcast(i32)
        dstf = nodes[:, 2 * C:3 * C]
        prevf = nodes[:, 3 * C:4 * C]
        qf = nodes[:, 4 * C:5 * C]
        tf = nodes[:, 5 * C:6 * C]
        HQ, HT = BIGB * P, BIGB * T
        oh_q = msgs[:, 0:HQ].bitcast(bf16).rearrange("p (h q j) -> p h q j", h=2, j=BIGB)
        oh_t = msgs[:, HQ:HQ + HT].bitcast(bf16).rearrange("p (h q j) -> p h q j", h=2, j=BIGB)
        at = HQ + HT
        iota_e = msgs[:, at:at + HQ // 2].bitcast(bf16).rearrange("p (q j) -> p q j", j=BIGB)
        at += HQ // 2
        qb = msgs[:, at:at + C // 2].bitcast(bf16)
        tb = msgs[:, at + C // 2:at + C].bitcast(bf16)
        at += C
        gat_rows = msgs[:, at:at + T * GAT.GW].rearrange("p (t w) -> p t w", t=T)
        ZN = C * RGAT.QW // 7
        zeros = rows[:, 0:ZN]
        feats = msgs[:, :].rearrange("p (t w) -> p t w", t=T)

        wT8 = msgs[0:F, 0:REL * F]

        def run_rows(w, b):
            return rows[:, 0:2 * b * w].rearrange("p (h j w) -> p h j w", h=2, j=b)

        def node_rows(w):
            return nodes[:, 0:T * w].rearrange("p (t w) -> p t w", t=T)

        def messages(w, b):
            return msgs[:, 0:2 * b * w].rearrange("p (h j w) -> p h j w", h=2, j=b)

        def dst_scores(qw):
            return qx[:, 0:2 * BIGB * qw].rearrange("p (h j w) -> p h j w", h=2, j=BIGB)

        wm_two = tab[:, :, :].rearrange("p k w -> p (k w)")[:, 2 * PICK * P:2 * PICK * P + 4 * F]
        wmix_two = onehot[:, :, :].rearrange("p j r -> p (j r)")[:, 0:2 * F]
        RW = REL * F + F
        w_even, w_odd = nodes[:, 0:RW], nodes[:, RW:2 * RW]
        spare = gath[:, :, :, :].rearrange("p h j w -> p (h j w)")
        PAIR = 2 * PICK * P
        near_src = spare[:, T * F:T * F + PAIR].bitcast(i32)
        near = spare[:, T * F + PAIR:T * F + PAIR + PAIR // 2].bitcast(bf16)
        tab_flat = tab[:, :, :].rearrange("p k w -> p (k w)")
        ring = [(qx if k < 3 else tab_flat)[:, k % 3 * PAIR // 2:(k % 3 + 1) * PAIR // 2].bitcast(bf16)
                for k in range(RING)]
        part_hm = Z[:, :, :].rearrange("p t f -> p (t f)").bitcast(bf16).rearrange("p (z t f) -> p z t f", z=2, t=T)
        part_l = QN[:, :, :].rearrange("p t f -> p (t f)").bitcast(bf16).rearrange("p (t f) -> p t f", t=T)
        parts = [part_hm[:, 0], part_hm[:, 1], part_l]
        qsel_flat = qsel[:, :, :, :].rearrange("p j k r -> p (j k r)")
        nothing = qsel_flat[:, 0:PICK * F].bitcast(bf16)
        landing = [x[:, 0:OWN * F].rearrange("p (j f) -> p j f", j=OWN)
                   for x in (qsel_flat[:, PICK * F:], XT[:, :, :].rearrange("p k n -> p (k n)"))]

        GEDGES = GPICK * P
        near_src_g = XT[:, :, :].rearrange("p k n -> p (k n)")[:, 0:GEDGES].bitcast(i32)
        near_g = qsel_flat[:, 0:GEDGES // 2].bitcast(bf16)
        nothing_g = qsel_flat[:, GEDGES // 2:GEDGES // 2 + P * 2].bitcast(bf16)[:, 0:GPICK * GAT.GW]
        ring_g = [(qx[:, 2 * BIGB:] if k < 3 else tab_flat)[:, k % 3 * GEDGES // 2:(k % 3 + 1) * GEDGES // 2].bitcast(bf16)
                  for k in range(RING)]
        parts_g = [x[:, :, :].rearrange("p t f -> p (t f)").bitcast(bf16)[:, 0:T * GAT.GW].rearrange(
            "p (t w) -> p t w", t=T) for x in (Bn, Y, Z)]

        psT = [ctx.enter_context(nc.psum_tensor(f"psT{k}", [P, 512], f32)) for k in range(2)]
        psO = [ctx.enter_context(nc.psum_tensor(f"psO{k}", [P, 512], f32)) for k in range(2)]
        psS = [ctx.enter_context(nc.psum_tensor(f"psS{k}", [P, 512], f32)) for k in range(2)]
        psR = ctx.enter_context(nc.psum_tensor("psR", [P, 512], f32))
        psH = ctx.enter_context(nc.psum_tensor("psH", [P, 512], f32))
        picked = psH[:, 0:2 * PICK * F].rearrange("p (h x) -> p h x", h=2)

        x_in = sem("x_in")
        loads_in = sem("loads_in")
        weights_in = sem("weights_in")
        zeros_stand = sem("zeros_stand")
        consts_stand = sem("consts_stand")
        transposed = sem("transposed")
        xt_ready = sem("xt_ready")
        product_done = sem("product_done")
        evacuated = sem("evacuated")
        base_ready = sem("base_ready")
        tab_stored = [sem("tab_stored0"), sem("tab_stored1")]
        rows_free = sem("rows_free")
        msgs_ready = sem("msgs_ready")
        scores_ready = sem("scores_ready")
        block_done = [sem("block_done0"), sem("block_done1")]
        runs_stored = [sem("runs_stored0"), sem("runs_stored1")]
        runs_free = [sem("runs_free0"), sem("runs_free1")]
        spread_in = [sem("spread_in0"), sem("spread_in1")]
        idx_ready = sem("idx_ready")
        table_ready = sem("table_ready")
        table_stored = sem("table_stored")
        starts_ready = sem("starts_ready")
        ends_stored = sem("ends_stored")
        fixed_ready = sem("fixed_ready")
        result_ready = sem("result_ready")
        sum_ready = sem("sum_ready")
        sum_done = sem("sum_done")
        operands_ready = sem("operands_ready")
        act_asked = sem("act_asked")
        act_done = sem("act_done")
        gathering = sem("gathering")
        oh_ready = sem("oh_ready")
        oh_used = sem("oh_used")
        stage_sems = [x_in, loads_in, weights_in, zeros_stand, consts_stand, transposed, xt_ready, product_done,
                      evacuated, base_ready, *tab_stored, rows_free, msgs_ready, scores_ready, *block_done, *runs_stored,
                      *runs_free, *spread_in, idx_ready, table_ready, table_stored, starts_ready, ends_stored,
                      fixed_ready, result_ready, sum_ready, sum_done, operands_ready, act_asked, act_done, gathering,
                      oh_ready, oh_used]
        near_in = sem("near_in")
        near_ready = sem("near_ready")
        onehot_ready = sem("onehot_ready")
        onehot_used = sem("onehot_used")
        parts_ready = sem("parts_ready")
        picked_done = sem("picked_done")
        picked_free = sem("picked_free")
        picked_in = sem("picked_in")
        msgs_free = sem("msgs_free")
        stage_sems += [picked_in, near_in, near_ready, onehot_ready, onehot_used, parts_ready, picked_done, picked_free, msgs_free]
        zero_rows = sem("zero_rows")
        zero_filled = sem("zero_filled")
        final_stored = sem("final_stored")
        names = ("gat", "pna", "rgat0", "rgat1", "rgcn")
        rows_in = {k: [sem(f"{k}_rows_in{h}") for h in range(2)] for k in names}
        nodes_in = {k: [sem(f"{k}_nodes_in{g}") for g in range(5 if k == "pna" else 1)] for k in names}
        fix_in = {k: sem(f"{k}_fix_in") for k in names}
        fix_out = {k: sem(f"{k}_fix_out") for k in names}
        spread_out = {k: sem(f"{k}_spread_out") for k in ("gat", "rgat0", "rgat1")}
        q_first_in = {k: sem(f"{k}_q_first_in") for k in ("gat", "rgat0", "rgat1")}
        end0_in = sem("end0_in")
        arrived = sem("arrived")
        go = {k: sem(f"go_{k}") for k in ("pe", "act", "dve", "pool")}
        dve_steps, pool_steps = sem("dve_steps"), sem("pool_steps")

        def meet(eng, who):
            eng.sem_inc(arrived, 1)
            eng.wait_ge(go[who], 1)
            eng.sem_clear(go[who])

        def meet_sp(sp):
            sp.wait_ge(arrived, 4)
            sp.sem_clear(arrived)
            for s in stage_sems:
                sp.sem_clear(s)
            for s in go.values():
                sp.sem_inc(s, 1)

        def cols(b, h, n):
            return bass.ds((b * 2 + h) * n, n)

        def bc(ap, shape):
            return ap.to_broadcast(shape)

        block = ctx.enter_context(nc.Block())

        @block.sync
        def _(sp):
            def load(dst, src, signal=loads_in):
                sp.dma_start(dst, src).then_inc(signal, 16)

            def edge_pass(w, n, spread=None, qw=0, key=None):
                if spread is not None:
                    sv, qv = spread.rearrange("(p c) w -> p c w", p=P), dst_scores(qw)
                    sp.wait_ge(spread_out[key], 16 * T)
                    for h in range(2):
                        sp.dma_start(qv[:, h], sv[:, h * n:h * n + n, :]).then_inc(spread_in[h], 16)
                for h in range(2):
                    sp.sem_inc(runs_free[h], 1)
                rv = runs[w][0:EP, :].rearrange("(p c) w -> p c w", p=P)
                with sp.Fori(0, pairs(n) - 1) as b:
                    for h in range(2):
                        sp.wait_ge(block_done[h], b + 1)
                        sp.dma_start(rv[:, cols(b, h, n), :], run_rows(w, n)[:, h]).then_inc(runs_stored[h], 16)
                        if spread is not None:
                            sp.dma_start(qv[:, h], sv[:, cols(b + 1, h, n), :]).then_inc(spread_in[h], 16)
                        sp.wait_ge(runs_stored[h], b * 16 + 16)
                        sp.sem_inc(runs_free[h], 1)
                for h in range(2):
                    sp.wait_ge(block_done[h], pairs(n))
                    sp.dma_start(rv[:, C - (2 - h) * n:C - (1 - h) * n, :], run_rows(w, n)[:, h]).then_inc(
                        runs_stored[h], 16)

            def odd_weights(k):
                load(w_odd[F:2 * F, :], wrel[k][:, :])

            def store_node_tables(table, w, bank_q=None, qw=0):
                tv = table.rearrange("(p t r) w -> p t (r w)", p=P, t=T)
                for s in range(T):
                    sp.wait_ge(evacuated, s + 1)
                    sp.dma_start(tv[:, s, :], tab[:, s % 2, 0:REL * w]).then_inc(tab_stored[s % 2], 16)
                if bank_q is not None:
                    sp.dma_start(bank_q.rearrange("(p t) w -> p t w", p=P), QN[:, :, 0:qw]).then_inc(table_stored, 16)

            load(X[:, :, :], t["x"].rearrange("(p t) f -> p t f", p=P), x_in)
            load(wgat[:, 0:F], t["L0_gnn_W"], x_in)
            for k in range(2):
                load(agat[:, k:k + 1], t["L0_gnn_a"][k * F:(k + 1) * F].unsqueeze(1), x_in)
            load(srci[:, :], t["src"], x_in)
            flat = t["dst"]
            load(dsti, flat[1:1 + EP].rearrange("(p c) -> p c", p=P))
            load(prevd, flat[0:EP].rearrange("(p c) -> p c", p=P))
            load(reli[:, :], t["edge_type_8"])
            load(wgt[:, :], t["edge_weight1"])
            sp.wait_ge(zeros_stand, 1)
            sp.dma_start(gat_spread.rearrange("(p c) w -> p (c w)", p=P), zeros[:, 0:C]).then_inc(zero_rows, 16)
            for w in runs:
                sp.dma_start(runs[w][EP:EP + 1, :], zeros[0:1, 0:w]).then_inc(zero_rows, 16)
            sp.wait_ge(table_ready, 1)
            sp.dma_start(gat_table.rearrange("(p t) w -> p t w", p=P), gat_rows).then_inc(table_stored, 16)
            sp.dma_start(gat_q.rearrange("(p t) w -> p (t w)", p=P), s4[:, :]).then_inc(table_stored, 16)
            zr = rgat_spread.rearrange("(p c) w -> p (c w)", p=P)
            for k in range(0, C * 32, ZN):
                sp.dma_start(zr[:, k:k + ZN], zeros).then_inc(zero_filled, 16)
            for l in range(LAYERS):
                for h in range(2):
                    load(wm[h * F:(h + 1) * F, l], t["L1_gnn_WM"][l].rearrange("(k f) n -> f k n", k=2), weights_in)
            load(bm[:, :], t["L1_gnn_bM"].rearrange("l f -> (l f)").partition_broadcast(P), weights_in)
            for k in range(2):
                n = str(k + 1)
                load(wrel[k][:, 0:REL * F].rearrange("f (r n) -> f r n", r=REL),
                     t["L2_gnn_W" + n].rearrange("r f n -> f r n"), weights_in)
                load(wk[:, k, :, 0:4], t["L2_gnn_K" + n].rearrange("r f n -> f r n"), weights_in)
                load(wk[:, k, :, 4:8], t["L2_gnn_Q" + n].rearrange("r f n -> f r n"), weights_in)
                load(brow[:, k, :], t["L2_gnn_b" + n].partition_broadcast(P), weights_in)
            load(wrel[2][:, 0:REL * F].rearrange("f (r n) -> f r n", r=REL),
                 t["L3_gnn_weight"].rearrange("r f n -> f r n"), weights_in)
            load(wrel[2][:, REL * F:], t["L3_gnn_loop_weight"], weights_in)
            load(brow[:, 2, :], t["L3_gnn_h_bias"].partition_broadcast(P), weights_in)
            sp.wait_ge(starts_ready, 1)
            sp.dma_start(end_table.rearrange("(p t) w -> p (t w)", p=P), end_i[:, :]).then_inc(ends_stored, 16)
            edge_pass(GAT.W, BIGB, gat_spread, GAT.QW, "gat")
            sp.wait_ge(zero_filled, 16 * 7)
            meet_sp(sp)

            with sp.Fori(0, LAYERS) as layer:
                one = bass.ds(layer, 1)
                wuv = t["L1_gnn_WU"][one, :, :].rearrange("l r n -> (l r) n")
                load(wu0[:, :], wuv[0:F, :])
                for g in range(3):
                    load(wu[:, :, g, :], wuv[F + g * 6 * F:F + (g + 1) * 6 * F, :].rearrange("(k p) n -> p k n", p=P))
                for h in range(2):
                    load(wmix[h * F:(h + 1) * F, :], t["L1_gnn_Wmix"][one, :, :].rearrange("l f n -> (l f) n"))
                for k, nm in enumerate(("bU", "gamma_t", "beta_t", "bmix", "gamma_o", "beta_o")):
                    load(par[:, k, :], t["L1_gnn_" + nm][one, :].rearrange("l f -> (l f)").partition_broadcast(P))
                sp.wait_ge(table_ready, 1)
                sp.dma_start(pna_table.rearrange("(p t) w -> p t w", p=P), Y[:, :, :]).then_inc(table_stored, 16)
                edge_pass(PNA_W, SMALLB)
                meet_sp(sp)

            for k in range(2):
                odd_weights(k)
                store_node_tables(rgat_table, RGAT.GW, rgat_q, RGAT.QW)
                edge_pass(RGAT.W, BIGB, rgat_spread, RGAT.QW, f"rgat{k}")
                meet_sp(sp)

            odd_weights(2)
            store_node_tables(rgcn_table, F)
            edge_pass(F, SMALLB)
            sp.wait_ge(result_ready, 1)
            sp.dma_start(t["out"].rearrange("(p t) f -> p t f", p=P), X[:, :, :]).then_inc(final_stored, 16)
            sp.wait_ge(final_stored, 16)

        @block.gpsimd
        def _(pool):
            steps = Steps(pool, pool_steps)

            def fetch(dst, table, idx, signal, bound):
                pool.indirect_dma_start(dst, None, table, bass.IndirectOffsetOnAxis(ap=idx, axis=0),
                                        bounds_check=bound, oob_is_err=False).then_inc(signal, 16)

            def put(table, src, idx, signal, bound):
                pool.indirect_dma_start(table, bass.IndirectOffsetOnAxis(ap=idx, axis=0), src, None,
                                        bounds_check=bound, oob_is_err=False).then_inc(signal, 16)

            def block_rows(table, idx, rows_of, landed, bound, n, own, b, h):
                nc.gpsimd.tensor_copy(idx_now[:, h, 0:own],
                                      idx[:, bass.ds((b * 2 + h) * n, own)]).then_inc(idx_ready, 1)
                pool.wait_ge(idx_ready, b * 2 + h + 1)
                pool.sem_inc(gathering, 1)
                for j in range(own):
                    fetch(rows_of(h, j), table, idx_now[:, h, j:j + 1], landed[h], bound)

            def first_pair(*a):
                for h in range(2):
                    block_rows(*a, 0, h)

            def other_pairs(*a):
                with pool.Fori(1, pairs(a[-2])) as b:
                    for h in range(2):
                        pool.wait_ge(rows_free, b * 2 + h - 1)
                        pool.sem_inc(gathering, 1)
                        block_rows(*a, b, h)

            def fix_chunks(w, n, key):
                for h in range(2):
                    pool.wait_ge(runs_stored[h], 16 * pairs(n))
                fetch(fixed[:, 0:w], runs[w], fix_i[:, 0:1], fix_in[key], EP - 1)
                pool.wait_ge(fixed_ready, 1)
                put(runs[w], fixed[:, 0:w], fix_i[:, 0:1], fix_out[key], EP - 1)

            def fetch_nodes(w, key):
                ns = node_rows(w)
                sems = nodes_in[key]
                for s in range(T):
                    fetch(ns[:, s, :], runs[w], end_i[:, s:s + 1], sems[s * len(sems) // T], EP)

            steps.do(nc.gpsimd.iota(iota_i[:, :], pattern=[[1, P]], base=0, channel_multiplier=0))
            steps.do(nc.gpsimd.iota(part_i[:, :], pattern=[[1, 1]], base=0, channel_multiplier=1))
            steps.do(nc.gpsimd.memset(ident[:, :], 0.0))
            steps.do(nc.gpsimd.affine_select(out=ident[:, :], in_=ident[:, :], compare_op=ALU.not_equal, fill=1.0,
                                             base=0, pattern=[[-1, P]], channel_multiplier=1))
            steps.do(nc.gpsimd.memset(upper[:, :], 1.0))
            steps.do(nc.gpsimd.affine_select(out=upper[:, :], in_=upper[:, :], compare_op=ALU.is_gt, fill=0.0,
                                             base=0, pattern=[[1, P]], channel_multiplier=-1))
            steps.do(nc.gpsimd.memset(realp[:, :], 1.0))
            steps.do(nc.gpsimd.affine_select(out=realp[:, :], in_=realp[:, :], compare_op=ALU.is_gt, fill=0.0,
                                             base=FULL, pattern=[[0, P]], channel_multiplier=-1))
            pool.sem_inc(consts_stand, 1)
            pool.wait_ge(x_in, 16 * 5)
            pool.wait_ge(table_stored, 32)
            a = (gat_table, srci, lambda h, j: gath[:, h, j, 0:GAT.GW], rows_in["gat"], NP - 1, BIGB, BIGB - GPICK)
            first_pair(*a)
            pool.wait_ge(starts_ready, 1)
            pool.wait_ge(zero_rows, 16 * (1 + len(runs)))
            for s in range(T):
                put(gat_spread, s4[:, s:s + 1], start_i[:, s:s + 1], spread_out["gat"], EP - 1)
            fetch(qlast[:, 0:1], gat_q, dst0_i[:, 0:1], q_first_in["gat"], NP - 1)
            pool.wait_ge(ends_stored, 16)
            fetch(end0_i[:, :], end_table, dst0_i[:, 0:1], end0_in, NP - 1)
            other_pairs(*a)
            fix_chunks(GAT.W, BIGB, "gat")
            pool.wait_ge(fix_out["gat"], 16)
            fetch_nodes(GAT.W, "gat")
            meet(pool, "pool")

            with pool.Fori(0, LAYERS) as layer:
                pool.wait_ge(table_stored, 16)
                a = (pna_table, srci, lambda h, j: landing[h][:, j, :], rows_in["pna"], NP - 1, SMALLB, OWN)
                first_pair(*a)
                other_pairs(*a)
                fix_chunks(PNA_W, SMALLB, "pna")
                pool.wait_ge(fix_out["pna"], layer * 16 + 16)
                pool.sem_inc(gathering, 1)
                fetch_nodes(PNA_W, "pna")
                meet(pool, "pool")

            for k in range(2):
                key = f"rgat{k}"
                for s in range(T):
                    pool.wait_ge(evacuated, s + 1)
                    put(rgat_spread, QN[:, s, :], start_i[:, s:s + 1], spread_out[key], EP - 1)
                for h in range(2):
                    pool.wait_ge(tab_stored[h], 16 * len(range(h, T, 2)))
                pool.wait_ge(table_stored, 16)
                fetch(qlast[:, :], rgat_q, dst0_i[:, 0:1], q_first_in[key], NP - 1)
                a = (rgat_table, reli, lambda h, j: gath[:, h, j, :], rows_in[key], NP * REL - 1, BIGB, BIGB)
                first_pair(*a)
                other_pairs(*a)
                fix_chunks(RGAT.W, BIGB, key)
                pool.wait_ge(fix_out[key], 16)
                fetch_nodes(RGAT.W, key)
                meet(pool, "pool")

            for h in range(2):
                pool.wait_ge(tab_stored[h], 16 * len(range(h, T, 2)))
            a = (rgcn_table, reli, lambda h, j: gath[:, h, j, 0:F], rows_in["rgcn"], NP * REL - 1, SMALLB, SMALLB)
            first_pair(*a)
            other_pairs(*a)
            fix_chunks(F, SMALLB, "rgcn")
            pool.wait_ge(fix_out["rgcn"], 16)
            fetch_nodes(F, "rgcn")

        @block.tensor
        def _(pe):
            def transposes(src, k, slots):
                if k >= 2:
                    pe.wait_ge(xt_ready, k - 1)
                for i, s in enumerate(slots):
                    last = nc.tensor.transpose(psT[k % 2][0:F, i * P:(i + 1) * P], src[:, s, :], ident[:, :])
                last.then_inc(transposed, 1)

            def group_products(src, rhs, n, k0):
                for g in range(len(GROUPS) + 1):
                    if g < len(GROUPS):
                        transposes(src, k0 + g, GROUPS[g])
                    if g >= 1:
                        k = k0 + g - 1
                        pe.wait_ge(xt_ready, k + 1)
                        if k >= 2:
                            pe.wait_ge(evacuated, k - 1)
                        for i, s in enumerate(GROUPS[g - 1]):
                            last = nc.tensor.matmul(psO[k % 2][:, i * n:(i + 1) * n], XT[0:F, k % 2, i * P:(i + 1) * P],
                                                    rhs, start=True, stop=True)
                        last.then_inc(product_done, 1)

            def pair_transposes(src, k, slots):
                if k >= 2:
                    pe.wait_ge(xt_ready, k - 1)
                for i, s in enumerate(slots[::2]):
                    w = min(2, T - s) * F
                    last = nc.tensor.transpose(psT[k % 2][0:w, i * P:(i + 1) * P],
                                               src[:, s:s + w // F, :].rearrange("p t f -> p (t f)"), ident[:, :])
                last.then_inc(transposed, 1)

            def pair_products(src, two, n, k0, groups):
                for g in range(len(groups) + 1):
                    if g < len(groups):
                        pair_transposes(src, k0 + g, groups[g])
                    if g >= 1:
                        k = k0 + g - 1
                        pe.wait_ge(xt_ready, k + 1)
                        if k >= 2:
                            pe.wait_ge(evacuated, k - 1)
                        for i, s in enumerate(groups[g - 1][::2]):
                            w = min(2, T - s)
                            last = nc.tensor.matmul(psO[k % 2][:, 2 * i * n:(2 * i + w) * n],
                                                    XT[0:w * F, k % 2, i * P:(i + 1) * P], two[0:w * F, 0:w * n],
                                                    start=True, stop=True)
                        last.then_inc(product_done, 1)

            def relation_products():
                pe.wait_ge(operands_ready, 1)
                pe.wait_ge(loads_in, 16)
                pair_transposes(Hn, 0, GROUPS[0])
                for g, slots in enumerate(GROUPS):
                    if g + 1 < len(GROUPS):
                        pair_transposes(Hn, g + 1, GROUPS[g + 1])
                    pe.wait_ge(xt_ready, g + 1)
                    for i, s in enumerate(slots):
                        if s >= 2:
                            pe.wait_ge(evacuated, s - 1)
                        rows_ = min(2, T - s + s % 2) * F
                        lhs = XT[0:rows_, g % 2, i // 2 * P:(i // 2 + 1) * P]
                        w = (w_even, w_odd)[s % 2][0:rows_, :]
                        nc.tensor.matmul(psO[s % 2][:, 0:REL * F], lhs, w[:, 0:REL * F], start=True, stop=True)
                        nc.tensor.matmul(psS[s % 2][:, 0:F], lhs, w[:, REL * F:], start=True, stop=True).then_inc(
                            product_done, 1)

            def pick_rows(units, n, w, hots, of, none):
                pe.wait_ge(parts_ready, 1)
                with pe.Fori(0, units) as b:
                    pe.wait_ge(picked_free, b + 1)
                    nc.tensor.matmul(psH[:, 0:n * w], none[:, 0:P], none, start=True, stop=False)
                    for s in range(T):
                        pe.wait_ge(onehot_ready, b * T + s + 1)
                        for c in range(n):
                            for part in of:
                                last = nc.tensor.matmul(psH[:, c * w:(c + 1) * w], hots[s % RING][:, c * P:(c + 1) * P],
                                                        part[:, s, :], start=False, stop=False)
                        last.then_inc(onehot_used, 1)
                    nc.tensor.matmul(psH[:, 0:n * w], none[:, 0:P], none, start=False, stop=True).then_inc(picked_done, 1)

            def total(k):
                pe.wait_ge(sum_ready, k)
                nc.tensor.matmul(psR[:, 0:F], realp[:, :], fa[:, :], start=True, stop=True).then_inc(sum_done, 1)

            def carry_attention(a, k):
                last = run_rows(a.W, BIGB)[:, 1, BIGB - 1, 0:a.A]
                pe.wait_ge(sum_ready, k + 1)
                nc.tensor.transpose(psT[0][0:a.A, 0:P], before_c[:, 0:a.A], ident[:, :])
                nc.tensor.transpose(psT[0][0:a.A, P:2 * P], last, ident[:, :]).then_inc(sum_done, 1)
                pe.wait_ge(sum_ready, k + 2)
                nc.tensor.transpose(psO[0][:, 0:a.A], cD[0:a.A, 0:P], ident[0:a.A, 0:a.A])
                nc.tensor.transpose(psO[0][:, P:P + a.A], cA[0:a.A, 0:P], ident[0:a.A, 0:a.A]).then_inc(sum_done, 1)

            pe.wait_ge(consts_stand, 1)
            pe.wait_ge(x_in, 16 * 5)
            nc.tensor.transpose(psR[0:F, 0:F], wgat[:, 0:F], ident[0:F, 0:F]).then_inc(sum_done, 1)
            pe.wait_ge(sum_ready, 1)
            nc.tensor.matmul(psR[0:F, F:F + 2], wT[:, :], agat[:, :], start=True, stop=True).then_inc(sum_done, 1)
            pe.wait_ge(operands_ready, 1)
            group_products(Hn, wgat[:, :], F + 2, 0)
            zl, zr = zeros[:, 0:P // 2].bitcast(bf16), zeros[:, 0:32].bitcast(bf16)[:, 0:T]
            nc.tensor.matmul(psH[:, 0:T], zl, zr, start=True, stop=False)
            with pe.Fori(0, pairs(BIGB)) as b:
                for h in range(2):
                    pe.wait_ge(oh_ready, b * 2 + h + 1)
                    for j in range(BIGB):
                        last = nc.tensor.matmul(psH[:, 0:T], oh_q[:, h, :, j], oh_t[:, h, :, j], start=False, stop=False)
                    last.then_inc(oh_used, 1)
            nc.tensor.matmul(psH[:, 0:T], zl, zr, start=False, stop=True).then_inc(sum_done, 1)
            pe.wait_ge(sum_ready, 2)
            nc.tensor.matmul(psS[0][:, 0:1], upper[:, :], col1[:, :], start=True, stop=True).then_inc(sum_done, 1)
            pe.wait_ge(sum_ready, 3)
            nc.tensor.matmul(psS[1][:, 0:P], cB[:, :], ident[:, :], start=True, stop=True).then_inc(sum_done, 1)
            for k in range(2):
                pe.wait_ge(sum_ready, 4 + 2 * k)
                for r in range(REL):
                    last = nc.tensor.transpose(psR[0:F, r * F:(r + 1) * F], wrel[k][:, r * F:(r + 1) * F], ident[0:F, 0:F])
                last.then_inc(sum_done, 1)
                pe.wait_ge(sum_ready, 5 + 2 * k)
                for r in range(REL):
                    last = nc.tensor.matmul(psS[0][0:F, 8 * r:8 * (r + 1)], wT8[:, r * F:(r + 1) * F], wk[:, k, r, :],
                                            start=True, stop=True)
                last.then_inc(sum_done, 1)
            pick_rows(pairs(BIGB) * 2, GPICK, GAT.GW, ring_g, parts_g, nothing_g)
            carry_attention(GAT, 7)
            meet(pe, "pe")

            NG = len(GROUPS)
            with pe.Fori(0, LAYERS) as layer:
                pe.wait_ge(operands_ready, 1)
                pair_products(Hn, wm_two, 2 * F, 0, GROUPS)
                pick_rows(pairs(SMALLB), 2 * PICK, F, ring, parts, nothing)
                pe.wait_ge(sum_ready, 1)
                last = run_rows(PNA_W, SMALLB)[:, 1, SMALLB - 1, :]
                nc.tensor.transpose(psT[0][:, 0:P], last[:, 0:P], ident[:, :])
                nc.tensor.transpose(psT[1][:, 0:P], last[:, P:2 * P], ident[:, :]).then_inc(sum_done, 1)
                pe.wait_ge(sum_ready, 2)
                nc.tensor.transpose(psO[0][:, 0:P], cA[:, 0:P], ident[:, :])
                nc.tensor.transpose(psO[0][:, P:2 * P], cD[:, 0:P], ident[:, :]).then_inc(sum_done, 1)
                for s in range(T + 1):
                    if s < T:
                        k = NG + s
                        if s % FIFTH == 0:
                            pe.wait_ge(act_done, s // FIFTH + 1)
                        pe.wait_ge(xt_ready, k - 1)
                        for i in range(3):
                            nc.tensor.transpose(psT[k % 2][:, i * P:(i + 1) * P], feats[:, s, i * P:(i + 1) * P], ident[:, :])
                        nc.tensor.transpose(psT[k % 2][0:F, 3 * P:4 * P], Hn[:, s, :], ident[:, :]).then_inc(transposed, 1)
                    if s >= 1:
                        k = NG + s - 1
                        pe.wait_ge(xt_ready, k + 1)
                        pe.wait_ge(evacuated, k - 1)
                        for i in range(3):
                            nc.tensor.matmul(psO[k % 2][:, 0:3 * F], XT[:, k % 2, i * P:(i + 1) * P],
                                             wu[:, i, :, :].rearrange("p g n -> p (g n)"), start=(i == 0), stop=False)
                        nc.tensor.matmul(psO[k % 2][:, 0:F], XT[0:F, k % 2, 3 * P:4 * P], wu0[:, :], start=False,
                                         stop=True).then_inc(product_done, 1)
                total(3)
                total(4)
                pe.wait_ge(operands_ready, 2)
                pair_products(Y, wmix_two, F, NG + T, BIG_GROUPS)
                total(5)
                total(6)
                meet(pe, "pe")

            for k in range(2):
                relation_products()
                carry_attention(RGAT, 0)
                meet(pe, "pe")

            relation_products()
            pe.wait_ge(sum_ready, 1)
            nc.tensor.transpose(psT[0][0:F, 0:P], run_rows(F, SMALLB)[:, 1, SMALLB - 1, :], ident[:, :]).then_inc(sum_done, 1)
            pe.wait_ge(sum_ready, 2)
            nc.tensor.transpose(psO[0][:, 0:F], cD[0:F, 0:P], ident[0:F, 0:F]).then_inc(sum_done, 1)

        @block.scalar
        def _(act):
            asked = [0]

            def func(out, in_, fn, **kw):
                asked[0] += 1
                act.wait_ge(act_asked, asked[0])
                nc.scalar.activation(out, in_, fn, **kw).then_inc(act_done, 1)

            def end():
                asked[0] = 0
                meet(act, "act")

            def group_copies(k0):
                for g, slots in enumerate(GROUPS):
                    k, n = k0 + g, len(slots) * P
                    act.wait_ge(transposed, k + 1)
                    if k >= 2:
                        act.wait_ge(product_done, k - 1)
                    nc.scalar.copy(XT[0:F, k % 2, 0:n], psT[k % 2][0:F, 0:n]).then_inc(xt_ready, 1)

            def pair_copies(k0, groups, per_slot=False):
                for g, slots in enumerate(groups):
                    k, n = k0 + g, len(slots) // 2 * P
                    act.wait_ge(transposed, k + 1)
                    if k >= 2:
                        act.wait_ge(product_done, G * (g - 1) if per_slot else k - 1)
                    if len(slots) % 2:
                        last = nc.scalar.copy(XT[0:F, k % 2, n:n + P], psT[k % 2][0:F, n:n + P])
                    if n:
                        last = nc.scalar.copy(XT[:, k % 2, 0:n], psT[k % 2][:, 0:n])
                    last.then_inc(xt_ready, 1)

            def layer_norm():
                func(s1[:, :], s2[:, :], ACT.Sqrt)

            def load_near(u, src, table):
                act.dma_start(src, t[table][bass.ds(u, 1), :].rearrange("b e -> (b e)").partition_broadcast(P)).then_inc(
                    near_in, 16)

            def next_near(u, out, src, table):
                act.wait_ge(near_in, u * 16 + 16)
                nc.scalar.activation(out, src, ACT.Identity, bias=first_node[:, 0:1]).then_inc(near_ready, 1)
                act.wait_ge(near_ready, u + 1)
                act.sem_inc(gathering, 1)
                load_near(u + 1, src, table)

            def edge_attention(a, picks=False):
                mv = messages(a.A, BIGB)
                near_of = (near_g, near_src_g, "gat_near")
                if picks:
                    act.wait_ge(parts_ready, 1)
                    load_near(0, *near_of[1:])
                    next_near(0, *near_of)
                    act.sem_inc(picked_free, 1)
                with act.Fori(0, pairs(BIGB)) as b:
                    for h in range(2):
                        if picks:
                            u = b * 2 + h
                            act.wait_ge(onehot_ready, u * T + T)
                            next_near(u + 1, *near_of)
                            act.wait_ge(picked_done, u + 1)
                            act.wait_ge(msgs_free, u + 1)
                            nc.scalar.copy(gath[:, h, BIGB - GPICK:, 0:GAT.GW], psH[:, 0:GPICK * GAT.GW].rearrange(
                                "p (j w) -> p j w", j=GPICK)).then_inc(picked_in, 1)
                            act.wait_ge(picked_in, u + 1)
                            act.sem_inc(picked_free, 1)
                        act.wait_ge(scores_ready, b * 2 + h + 1)
                        nc.scalar.activation(decay[:, 0:a.H, :], decay[:, 0:a.H, :], ACT.Exp).then_inc(msgs_ready, 1)
                        nc.scalar.activation(mv[:, h].rearrange("p j (k d) -> p j k d", k=a.H)[:, :, :, a.D],
                                             expo[:, :, 0:a.H], ACT.Exp).then_inc(msgs_ready, 1)
                if picks:
                    act.wait_ge(near_in, 16 * (2 * pairs(BIGB) + 2))
                func(cB[0:a.A, :], cB[0:a.A, :], ACT.Exp)
                func(cC[0:a.A, :], cC[0:a.A, :], ACT.Exp)
                func(fw[:, 0:2, 0:a.H], fw[:, 0:2, 0:a.H], ACT.Exp)

            layer_norm()
            group_copies(0)
            func(s2[:, :], s1[:, :], ACT.Ln)
            edge_attention(GAT, True)
            func(Z[:, :, :], Z[:, :, :], ACT.Exp)
            layer_norm()
            end()
            NG = len(GROUPS)
            with act.Fori(0, LAYERS) as layer:
                pair_copies(0, GROUPS)
                mv = messages(PNA_M, SMALLB)

                def messages_of(rows_, b, h, some):
                    nc.scalar.activation(mv[:, h, some, 0:F], rows_, ACT.Copy, scale=-1.0).then_inc(msgs_ready, 1)
                    nc.scalar.activation(mv[:, h, some, F:2 * F], rows_, ACT.Copy).then_inc(msgs_ready, 1)
                    nc.scalar.activation(mv[:, h, some, 2 * F:], rows_, ACT.Square).then_inc(msgs_ready, 1)

                def gathered_messages(b, h):
                    act.wait_ge(msgs_free, b * 2 + h + 1)
                    act.sem_inc(gathering, 1)
                    now = slice(h * SMALLB, (h + 1) * SMALLB)
                    nc.scalar.activation(cont_now[:, now], cont[:, cols(b, h, SMALLB)], ACT.Copy).then_inc(msgs_ready, 1)
                    nc.scalar.activation(negs_now[:, now], start[:, cols(b, h, SMALLB)], ACT.Copy,
                                         scale=-BIG).then_inc(msgs_ready, 1)
                    act.wait_ge(rows_in["pna"][h], (layer * pairs(SMALLB) + b + 1) * 16 * OWN)
                    messages_of(landing[h], b, h, slice(0, OWN))
                    act.wait_ge(msgs_ready, (b * 2 + h) * 8 + 5 + 3 * h)
                    act.sem_inc(rows_free, 1)

                def picked_messages(b, h):
                    messages_of(picked[:, h].rearrange("p (j f) -> p j f", j=PICK), b, h, slice(OWN, SMALLB))

                def pair_messages(b, more):
                    gathered_messages(b, 0)
                    if more:
                        act.wait_ge(onehot_ready, b * T + T)
                        next_near(b + 1, *near_of)
                    act.wait_ge(picked_done, b + 1)
                    picked_messages(b, 0)
                    act.wait_ge(msgs_free, b * 2 + 2)
                    picked_messages(b, 1)
                    act.wait_ge(msgs_ready, b * 16 + 11)
                    act.sem_inc(picked_free, 1)
                    gathered_messages(b, 1)

                near_of = (near, near_src, "pna_near")
                load_near(0, *near_of[1:])
                next_near(0, *near_of)
                act.sem_inc(picked_free, 1)
                last = pairs(SMALLB) - 1
                with act.Fori(0, last) as b:
                    pair_messages(b, True)
                pair_messages(last, False)
                act.wait_ge(near_in, 16 * (last + 2))
                for s in range(T + 1):
                    if s < T:
                        k = NG + s
                        if s == 0 or (s % FIFTH == FIFTH - 1 and s + 1 < T):
                            at = s + 1 if s else 0
                            some = slice(at, at + FIFTH)
                            func(feats[:, some, 3 * F:4 * F], feats[:, some, 4 * F:5 * F], ACT.Sqrt, bias=tiny[:, 0:1])
                        act.wait_ge(transposed, k + 1)
                        act.wait_ge(product_done, k - 1)
                        nc.scalar.copy(XT[:, k % 2, 0:3 * P], psT[k % 2][:, 0:3 * P])
                        nc.scalar.copy(XT[0:F, k % 2, 3 * P:], psT[k % 2][0:F, 3 * P:]).then_inc(xt_ready, 1)
                    if s >= 1:
                        act.wait_ge(product_done, NG + s)
                        nc.scalar.copy(Y[:, s - 1, :], psO[(NG + s - 1) % 2][:, 0:F]).then_inc(base_ready, 1)
                func(fb[:, :], fc[:, :], ACT.Sqrt)
                pair_copies(NG + T, BIG_GROUPS)
                func(fb[:, :], fc[:, :], ACT.Sqrt)
                end()
            for k in range(2):
                if k == 0:
                    layer_norm()
                pair_copies(0, GROUPS, per_slot=True)
                edge_attention(RGAT)
                if k:
                    layer_norm()
                end()
            pair_copies(0, GROUPS, per_slot=True)

        @block.vector
        def _(dve):
            st = Steps(dve, dve_steps)
            V = nc.vector
            asked, sums = [0], [0]

            def tt(out, a, b, op):
                st.do(V.tensor_tensor(out, a, b, op))

            def ts(out, a, x, op, y=None, op1=None):
                if y is None:
                    st.do(V.tensor_scalar(out, a, x, None, op))
                else:
                    st.do(V.tensor_scalar(out, a, x, y, op, op1))

            def copy(out, a):
                st.do(V.tensor_copy(out, a))

            def ask(wait=True):
                asked[0] += 1
                dve.sem_inc(act_asked, 1)
                if wait:
                    dve.wait_ge(act_done, asked[0])

            def ask_pe(wait=True):
                sums[0] += 1
                dve.sem_inc(sum_ready, 1)
                if wait:
                    dve.wait_ge(sum_done, sums[0])

            def end():
                st.reset()
                asked[0] = sums[0] = 0
                meet(dve, "dve")

            def over_t(x, w=F):
                return bc(x.unsqueeze(2), [P, x.shape[1], w])

            def over_f(x):
                return bc(x.unsqueeze(1), [P, T, F])

            def layer_norm():
                st.do(V.tensor_reduce(s3[:, :], X[:, :, :], AX.X, ALU.add))
                ts(s3[:, :], s3[:, :], 1.0 / F, ALU.mult)
                tt(Hn[:, :, :], X[:, :, :], over_t(s3[:, :]), ALU.subtract)
                tt(Z[:, :, :], Hn[:, :, :], Hn[:, :, :], ALU.mult)
                st.do(V.tensor_reduce(s2[:, :], Z[:, :, :], AX.X, ALU.add))
                ts(s2[:, :], s2[:, :], 1.0 / F, ALU.mult, 1e-5, ALU.add)
                ask()
                st.do(V.reciprocal(s3[:, :], s1[:, :]))
                tt(Hn[:, :, :], Hn[:, :, :], over_t(s3[:, :]), ALU.mult)
                ts(Hn[:, :, :], Hn[:, :, :], 0.0, ALU.max)

            def batch_norm(buf, squares, gamma, beta):
                def sum_of(of):
                    st.do(V.tensor_reduce(fa[:, :], of.rearrange("p t f -> p f t"), AX.X, ALU.add))
                    ask_pe()

                sum_of(buf)
                ts(fb[:, :], psR[:, 0:F], 1.0 / N, ALU.mult)
                tt(buf, buf, over_f(fb[:, :]), ALU.subtract)
                tt(squares, buf, buf, ALU.mult)
                sum_of(squares)
                ts(fc[:, :], psR[:, 0:F], 1.0 / N, ALU.mult, 1e-5, ALU.add)
                ask()
                st.do(V.reciprocal(fb[:, :], fb[:, :]))
                tt(fb[:, :], fb[:, :], gamma, ALU.mult)
                tt(buf, buf, over_f(fb[:, :]), ALU.mult)
                tt(buf, buf, over_f(beta), ALU.add)

            def block_masks(b, h, n, extra=None):
                st.add(V.tensor_copy(cont_now[:, 0:n], cont[:, cols(b, h, n)]))
                st.add(V.tensor_scalar(negs_now[:, 0:n], start[:, cols(b, h, n)], -BIG, None, ALU.mult))
                if extra is not None:
                    st.add(V.tensor_copy(extra_now[:, 0:n], extra[:, cols(b, h, n)]))
                st.wait()

            def finish_block(h):
                st.wait()
                dve.sem_inc(block_done[h], 1)
                st.reset()

            def one_hot(hots, of, u, s):
                dve.wait_ge(onehot_used, u * T + s + 1)
                V.tensor_scalar(hots[s % RING], of, float(s), None, ALU.is_equal).then_inc(onehot_ready, 1)

            def split(of, table, rest):
                copy(of[0], table)
                tt(rest, table, of[0], ALU.subtract)
                copy(of[1], rest)
                tt(rest, rest, of[1], ALU.subtract)
                copy(of[2], rest)

            def scan(out, data0, data1, initial, op0, op1):
                return V.tensor_tensor_scan(out, data0, data1, initial, op0, op1)

            def evacuate(k0, n, take, groups=GROUPS):
                for g, slots in enumerate(groups):
                    k = k0 + g
                    dve.wait_ge(product_done, k + 1)
                    take(slice(slots[0], slots[-1] + 1), psO[k % 2][:, 0:len(slots) * n].rearrange(
                        "p (s n) -> p s n", n=n))
                    st.wait()
                    dve.sem_inc(evacuated, 1)

            def edge_attention(a, key, picks=0):
                n = BIGB
                landed = rows_in[key]
                rv, mv, qv = run_rows(a.W, n), messages(a.A, n), dst_scores(a.QW)
                st.do(V.memset(rv[:, 1, n - 1, :], 0.0))
                st.do(V.memset(maxrun[:, :, :], -BIG))
                if picks:
                    dve.wait_ge(near_ready, 1)
                    for s in range(T):
                        one_hot(ring_g, near_g, 0, s)
                dve.wait_ge(q_first_in[key], 16)
                st.reset()
                def attend(b, h, hots=False):
                    u = b * 2 + h + 1
                    block_masks(b, h, n, etyf if a.R > 1 else None)
                    dve.wait_ge(spread_in[h], b * 16 + 16)
                    for c in range(a.QW):
                        st.add(scan(qv[:, h, :, c], cont_now[:, :], qv[:, h, :, c], qlast[:, c:c + 1], ALU.mult, ALU.add))
                    st.wait()
                    if a.R == 1:
                        q = qv[:, h]
                    else:
                        tt(onehot[:, :, :], bc(iota_f[:, 0:REL].unsqueeze(1), [P, n, REL]),
                           bc(extra_now[:, :].unsqueeze(2), [P, n, REL]), ALU.is_equal)
                        tt(qsel[:, :, :, :], qv[:, h].rearrange("p j (k r) -> p j k r", k=a.H),
                           bc(onehot[:, :, :].unsqueeze(2), [P, n, a.H, REL]), ALU.mult)
                        st.do(V.tensor_reduce(expo[:, :, :], qsel[:, :, :, :], AX.X, ALU.add))
                        q = expo[:, :, 0:a.H]
                    copy(qlast[:, 0:a.QW], qv[:, h, n - 1, :])
                    if hots:
                        dve.wait_ge(near_ready, u + 1)
                        for s in range(3):
                            one_hot(ring_g, near_g, u, s)
                    dve.wait_ge(landed[h], (b + 1) * 16 * (n - picks))
                    dve.sem_inc(gathering, 1)
                    if picks:
                        dve.wait_ge(picked_in, u)
                    tt(score[:, :, 0:a.H], q, gath[:, h, :, F:F + a.H], ALU.add)
                    st.do(V.scalar_tensor_tensor(score[:, :, 0:a.H], score[:, :, 0:a.H], 0.2, score[:, :, 0:a.H],
                                                 ALU.mult, ALU.max))
                    for k in range(a.H):
                        st.add(scan(maxrun[:, k, 1:], negs_now[:, :], score[:, :, k], maxrun[:, k, 0:1],
                                    ALU.add, ALU.max))
                    st.wait()
                    st.add(V.tensor_tensor(expo[:, :, 0:a.H], score[:, :, 0:a.H],
                                           maxrun[:, 0:a.H, 1:].rearrange("p k j -> p j k"), ALU.subtract))
                    tt(decay[:, 0:a.H, :], maxrun[:, 0:a.H, 0:n], maxrun[:, 0:a.H, 1:], ALU.subtract)
                    ts(decay[:, 0:a.H, :], decay[:, 0:a.H, :], 0.0, ALU.min)
                    dve.sem_inc(scores_ready, 1)
                    dve.wait_ge(runs_free[h], b + 1)
                    st.add(V.tensor_copy(rv[:, h, :, a.A:], maxrun[:, 0:a.H, 1:].rearrange("p k j -> p j k")))
                    copy(maxrun[:, 0:a.H, 0:1], maxrun[:, 0:a.H, n:])
                    dve.wait_ge(msgs_ready, (b * 2 + h) * 2 + 2)
                    m4 = mv[:, h].rearrange("p j (k d) -> p j k d", k=a.H)
                    st.add(V.tensor_tensor(decay[:, 0:a.H, :], decay[:, 0:a.H, :],
                                           bc(cont_now[:, :].unsqueeze(1), [P, a.H, n]), ALU.mult))
                    tt(m4[:, :, :, 0:a.D], gath[:, h, :, 0:F].rearrange("p j (k d) -> p j k d", k=a.H),
                       bc(m4[:, :, :, a.D:], [P, n, a.H, a.D]), ALU.mult)
                    dve.sem_inc(rows_free, 1)
                    if picks:
                        dve.sem_inc(msgs_free, 1)
                    if a.H == 1:
                        for j in range(n):
                            before = rv[:, h, j - 1, :] if j else rv[:, 1 - h, n - 1, :]
                            st.add(V.scalar_tensor_tensor(rv[:, h, j, 0:a.A], before[:, 0:a.A], decay[:, 0, j:j + 1],
                                                          mv[:, h, j, :], ALU.mult, ALU.add))
                            if hots and 3 + j < T:
                                one_hot(ring_g, near_g, u, 3 + j)
                            st.wait()
                    else:
                        for c in range(a.A):
                            st.add(scan(rv[:, h, :, c], decay[:, c // a.D1, :], mv[:, h, :, c],
                                        rv[:, 1 - h, n - 1, c:c + 1], ALU.mult, ALU.add))
                    finish_block(h)

                last = pairs(n) - 1
                with dve.Fori(0, last) as b:
                    for h in range(2):
                        attend(b, h, picks > 0)
                attend(last, 0, picks > 0)
                attend(last, 1)
                last = rv[:, 1, n - 1, :]
                copy(before_c[:, 0:a.A].rearrange("p (k d) -> p k d", k=a.H),
                     bc(last[:, a.A:].unsqueeze(2), [P, a.H, a.D1]))
                st.add(V.memset(cA[:, 0:1], -BIG))
                st.do(V.memset(cD[:, 0:1], 0.0))
                ask_pe()
                maxT, lastT = psT[0][0:a.A, 0:P], psT[0][0:a.A, P:2 * P]
                st.do(scan(cA[0:a.A, 1:], negT[0:a.A, :], maxT, -BIG, ALU.add, ALU.max))
                tt(cB[0:a.A, :], cA[0:a.A, 0:P], cA[0:a.A, 1:], ALU.subtract)
                ts(cB[0:a.A, :], cB[0:a.A, :], 0.0, ALU.min)
                ask(False)
                tt(cC[0:a.A, :], maxT, cA[0:a.A, 1:], ALU.subtract)
                ask()
                st.add(V.tensor_tensor(cB[0:a.A, :], cB[0:a.A, :], contT[0:a.A, :], ALU.mult))
                tt(cC[0:a.A, :], lastT, cC[0:a.A, :], ALU.mult)
                st.do(scan(cD[0:a.A, 1:], cB[0:a.A, :], cC[0:a.A, :], 0.0, ALU.mult, ALU.add))
                ask_pe()
                st.add(V.tensor_copy(before_c[:, 0:a.A], psO[0][:, 0:a.A]))
                copy(before_c[:, a.A:a.W], psO[0][:, P:P + a.A].rearrange("p (k d) -> p k d", k=a.H)[:, :, 0])
                dve.wait_ge(fix_in[key], 16)
                mf, mb = fixed[:, a.A:a.W], before_c[:, a.A:a.W]
                tt(fw[:, 2, 0:a.H], mf, mb, ALU.max)
                st.add(V.tensor_tensor(fw[:, 0, 0:a.H], mf, fw[:, 2, 0:a.H], ALU.subtract))
                tt(fw[:, 1, 0:a.H], mb, fw[:, 2, 0:a.H], ALU.subtract)
                ask()
                f3 = fixed[:, 0:a.A].rearrange("p (k d) -> p k d", k=a.H)
                b3 = before_c[:, 0:a.A].rearrange("p (k d) -> p k d", k=a.H)
                st.add(V.tensor_tensor(f3, f3, bc(fw[:, 0, 0:a.H].unsqueeze(2), [P, a.H, a.D1]), ALU.mult))
                tt(b3, b3, bc(fw[:, 1, 0:a.H].unsqueeze(2), [P, a.H, a.D1]), ALU.mult)
                tt(f3, f3, b3, ALU.add)
                dve.sem_inc(fixed_ready, 1)
                dve.wait_ge(nodes_in[key][0], 16 * T)
                n4 = node_rows(a.W)[:, :, 0:a.A].rearrange("p t (k d) -> p t k d", k=a.H)
                if a.R > 1:
                    ts(n4[:, :, :, a.D], n4[:, :, :, a.D], 1e-16, ALU.add)
                tt(hw1[:, :, 0:a.H], n4[:, :, :, a.D], over_t(hasnot[:, :], a.H), ALU.add)
                st.do(V.reciprocal(hw1[:, :, 0:a.H], hw1[:, :, 0:a.H]))
                tt(Z[:, :, :].rearrange("p t (k d) -> p t k d", k=a.H), n4[:, :, :, 0:a.D],
                   bc(hw1[:, :, 0:a.H].unsqueeze(3), [P, T, a.H, a.D]), ALU.mult)

            st.add(V.memset(zeros, 0.0))
            st.add(V.memset(fixed[:, :], 0.0))
            st.do(V.memset(tiny[:, :], 1e-30))
            dve.sem_inc(zeros_stand, 1)
            dve.wait_ge(x_in, 16 * 5)
            layer_norm()
            dve.wait_ge(sum_done, 1)
            copy(wT[:, :], psR[0:F, 0:F])
            sums[0] = 1
            ask_pe()
            copy(wgat[:, F:F + 2], psR[0:F, F:F + 2])
            dve.sem_inc(operands_ready, 1)

            def take_gat(sl, ps):
                st.add(V.tensor_copy(gat_rows[:, sl, :], ps[:, :, 0:GAT.GW]))
                st.add(V.tensor_copy(s4[:, sl], ps[:, :, GAT.GW]))

            evacuate(0, F + 2, take_gat)
            dve.sem_inc(table_ready, 1)
            dve.wait_ge(consts_stand, 1)
            copy(iota_f[:, :], iota_i[:, :])
            copy(iota_e, bc(iota_i[:, :].unsqueeze(2), [P, P, BIGB]))
            dve.wait_ge(loads_in, 16 * 4)
            copy(dstf, dsti)
            copy(dst0_i[:, :], dsti[:, 0:1])
            copy(prevf, prevd)
            tt(start[:, :], dstf, prevf, ALU.not_equal)
            ts(cont[:, :], start[:, :], -1.0, ALU.mult, 1.0, ALU.add)
            copy(etyf[:, :], reli[:, :])
            copy(prevf, srci[:, :])
            st.do(V.scalar_tensor_tensor(prevf, prevf, float(REL), etyf[:, :], ALU.mult, ALU.add))
            copy(reli[:, :], prevf)

            def floor_of(x, step):
                ts(x, x, 0.5, ALU.add, 1.0 / step, ALU.mult)
                ts(x, x, -0.5, ALU.add)
                ts(x, x, ROUND, ALU.add)
                ts(x, x, -ROUND, ALU.add)

            copy(qf, dstf)
            floor_of(qf, T)
            st.do(V.scalar_tensor_tensor(tf, qf, -float(T), dstf, ALU.mult, ALU.add))
            copy(qb, qf)
            copy(tb, tf)
            st.reset()
            dve.sem_inc(oh_used, 2)
            with dve.Fori(0, pairs(BIGB)) as b:
                for h in range(2):
                    st.add(V.tensor_copy(q_now[:, :], qb[:, cols(b, h, BIGB)]))
                    st.add(V.tensor_copy(t_now[:, :], tb[:, cols(b, h, BIGB)]))
                    st.wait()
                    dve.wait_ge(oh_used, b * 2 + h + 1)
                    st.add(V.tensor_tensor(oh_q[:, h], iota_e, bc(q_now[:, :].unsqueeze(1), [P, P, BIGB]), ALU.is_equal))
                    st.add(V.tensor_tensor(oh_t[:, h], iota_e[:, 0:T, :], bc(t_now[:, :].unsqueeze(1), [P, T, BIGB]),
                                           ALU.is_equal))
                    st.wait()
                    dve.sem_inc(oh_ready, 1)
                    st.reset()
            dve.wait_ge(sum_done, 3)
            sums[0] = 3 - 1
            copy(deg[:, :], psH[:, 0:T])
            ts(has[:, :], deg[:, :], 0.0, ALU.is_gt)
            ts(hasnot[:, :], has[:, :], -1.0, ALU.mult, 1.0, ALU.add)
            st.do(V.memset(s1[:, :], 1.0))
            st.do(scan(s2[:, :], s1[:, :], deg[:, :], 0.0, ALU.mult, ALU.add))
            copy(col1[:, :], s2[:, T - 1:T])
            dve.sem_inc(sum_ready, 1)
            dve.wait_ge(sum_done, 4)
            copy(col2[:, :], psS[0][:, 0:1])
            ts(s2[:, :], s2[:, :], col2[:, 0:1], ALU.add)
            tt(s1[:, :], s2[:, :], deg[:, :], ALU.subtract)
            ts(s2[:, :], s2[:, :], -1.0, ALU.add)
            st.do(V.scalar_tensor_tensor(s1[:, :], hasnot[:, :], float(NO_EDGE), s1[:, :], ALU.mult, ALU.add))
            copy(start_i[:, :], s1[:, :])
            tt(s2[:, :], s2[:, :], has[:, :], ALU.mult)
            st.do(V.scalar_tensor_tensor(s2[:, :], hasnot[:, :], float(EP), s2[:, :], ALU.mult, ALU.add))
            copy(end_i[:, :], s2[:, :])
            dve.sem_inc(starts_ready, 1)
            st.do(V.tensor_reduce(col1[:, :], start[:, :], AX.X, ALU.max))
            ts(col1[:, :], col1[:, :], -1.0, ALU.mult, 1.0, ALU.add)
            copy(cB[:, :], bc(col1[:, :], [P, P]))
            dve.sem_inc(sum_ready, 1)
            dve.wait_ge(sum_done, 5)
            copy(contT[:, :], psS[1][:, 0:P])
            ts(negT[:, :], contT[:, :], -1.0, ALU.add, BIG, ALU.mult)
            ts(s3[:, :], deg[:, :], 1.0, ALU.max)
            st.do(V.reciprocal(rden[:, :], s3[:, :]))
            ts(s1[:, :], deg[:, :], 1.0, ALU.add)
            ask()
            ts(amp[:, :], s2[:, :], 1.0 / 2.5, ALU.mult)
            tt(s3[:, :], hasnot[:, :], s2[:, :], ALU.add)
            st.do(V.reciprocal(s3[:, :], s3[:, :]))
            ts(s3[:, :], s3[:, :], 2.5, ALU.mult)
            tt(att[:, :], s3[:, :], has[:, :], ALU.mult)
            dve.wait_ge(end0_in, 16)
            copy(col1[:, :], end0_i[:, :])
            copy(col2[:, :], col1[:, :])
            floor_of(col2[:, :], C)
            copy(col3[:, :], part_i[:, :])
            tt(col2[:, :], col2[:, :], col3[:, :], ALU.is_equal)
            tt(col2[:, :], col2[:, :], cont[:, 0:1], ALU.mult)
            ts(col3[:, :], col2[:, :], -float(NO_EDGE), ALU.mult, float(NO_EDGE), ALU.add)
            tt(col3[:, :], col3[:, :], col1[:, :], ALU.add)
            copy(fix_i[:, :], col3[:, :])
            copy(first_node[:, :], part_i[:, :])
            ts(first_node[:, :], first_node[:, :], -float(T), ALU.mult)
            st.do(V.memset(nothing_g, 0.0))
            split(parts_g, gat_rows, nodes[:, 6 * C:6 * C + T * GAT.GW].rearrange("p (t w) -> p t w", t=T))
            dve.sem_inc(parts_ready, 1)
            dve.sem_inc(onehot_used, RING)
            dve.sem_inc(msgs_free, 2)
            dve.wait_ge(weights_in, 16 * (2 * LAYERS + 1 + 8 + 3))
            sums[0] = 5
            for k in range(2):
                ask_pe()
                copy(wT8, psR[0:F, :])
                ask_pe()
                small = psS[0][0:F, 0:8 * REL].rearrange("f (r w) -> f r w", r=REL)
                st.add(V.tensor_copy(wrel[k][:, REL * F:REL * F + 32].rearrange("f (r w) -> f r w", r=REL),
                                     small[:, :, 0:4]))
                copy(wrel[k][:, REL * F + 32:].rearrange("f (k r) -> f k r", r=REL),
                     small[:, :, 4:8].rearrange("f r k -> f k r"))
            dve.wait_ge(zero_filled, 16 * 7)
            edge_attention(GAT, "gat", GPICK)
            ts(Y[:, :, :], Z[:, :, :], 0.0, ALU.max)
            ts(Z[:, :, :], Z[:, :, :], 0.0, ALU.min)
            ask()
            st.do(V.scalar_tensor_tensor(Y[:, :, :], Z[:, :, :], -1.0, Y[:, :, :], ALU.add, ALU.add))
            tt(X[:, :, :], X[:, :, :], Y[:, :, :], ALU.add)
            layer_norm()
            end()

            NG = len(GROUPS)
            with dve.Fori(0, LAYERS) as layer:
                st.add(V.tensor_copy(bm_now[:, :], bm[:, bass.ds(layer * F, F)]))
                st.do(V.memset(wm_two, 0.0))
                for h in range(2):
                    half = slice(h * F, (h + 1) * F)
                    copy(wm_two[half, 2 * F * h:2 * F * (h + 1)].rearrange("f (k n) -> f k n", k=2),
                         wm[half, bass.ds(layer, 1), :, :].rearrange("f l k n -> f (l k) n"))
                dve.sem_inc(operands_ready, 1)

                def take_pna(sl, ps):
                    n = sl.stop - sl.start
                    st.add(V.tensor_copy(Y[:, sl, :], ps[:, :, 0:F]))
                    tt(Bn[:, sl, :], ps[:, :, F:2 * F], bc(bm_now[:, :].unsqueeze(1), [P, n, F]), ALU.add)

                evacuate(0, 2 * F, take_pna)
                dve.sem_inc(table_ready, 1)
                st.do(V.memset(nothing, 0.0))
                split(parts, Y[:, :, :], nodes[:, 0:T * F].rearrange("p (t f) -> p t f", t=T))
                dve.sem_inc(parts_ready, 1)
                dve.sem_inc(onehot_used, RING)
                dve.sem_inc(msgs_free, 2)

                dve.wait_ge(near_ready, 1)
                for s in range(T):
                    one_hot(ring, near, 0, s)
                tt(Bn[:, :, :], Bn[:, :, :], over_t(has[:, :]), ALU.mult)
                tt(Bd[:, :, :], Bn[:, :, :], over_t(deg[:, :]), ALU.mult)
                n = SMALLB
                rv, mv = run_rows(PNA_W, n), messages(PNA_M, n)
                st.do(V.memset(rv[:, 1, n - 1, 0:2 * F], -BIG))
                st.do(V.memset(rv[:, 1, n - 1, 2 * F:], 0.0))
                st.reset()

                def block_pair(b, one_hots):
                    if one_hots:
                        dve.wait_ge(near_ready, b + 2)
                    s = 0
                    for h in range(2):
                        dve.wait_ge(msgs_ready, (b * 2 + h) * 8 + 8)
                        dve.sem_inc(gathering, 1)
                        dve.wait_ge(runs_free[h], b + 1)
                        for j in range(n):
                            before = rv[:, h, j - 1, :] if j else rv[:, 1 - h, n - 1, :]
                            if j:
                                st.wait(st.n - 1)
                            st.add(V.scalar_tensor_tensor(rv[:, h, j, 0:2 * F], before[:, 0:2 * F],
                                                          negs_now[:, h * n + j:h * n + j + 1], mv[:, h, j, 0:2 * F], ALU.add, ALU.max))
                            if j:
                                st.wait(st.n - 1)
                            st.add(V.scalar_tensor_tensor(rv[:, h, j, 2 * F:], before[:, 2 * F:],
                                                          cont_now[:, h * n + j:h * n + j + 1], mv[:, h, j, F:], ALU.mult, ALU.add))
                            for _ in range((2 if j < 5 and not h else 1) if one_hots and s < T else 0):
                                one_hot(ring, near, b + 1, s)
                                s += 1
                        finish_block(h)
                        dve.sem_inc(msgs_free, 1)

                with dve.Fori(0, pairs(n) - 1) as b:
                    block_pair(b, True)
                block_pair(pairs(n) - 1, False)
                st.add(V.memset(cA[:, 0:1], -BIG))
                st.do(V.memset(cD[:, 0:1], 0.0))
                ask_pe()
                st.add(scan(cA[:, 1:], negT[:, :], psT[0][:, 0:P], -BIG, ALU.add, ALU.max))
                st.do(scan(cD[:, 1:], contT[:, :], psT[1][:, 0:P], 0.0, ALU.mult, ALU.add))
                ask_pe()
                dve.wait_ge(fix_in["pna"], layer * 16 + 16)
                st.add(V.tensor_tensor(fixed[:, 0:2 * F], psO[0][:, 0:P], fixed[:, 0:2 * F], ALU.max))
                tt(fixed[:, 2 * F:], psO[0][:, P:2 * P], fixed[:, 2 * F:], ALU.add)
                dve.sem_inc(fixed_ready, 1)
                dve.wait_ge(loads_in, 16 * 12)
                ts(par[:, 0, :], par[:, 0, :], 1.0 / float(N) ** 0.5, ALU.mult)
                st.do(V.memset(wmix_two, 0.0))
                for h in range(2):
                    half = slice(h * F, (h + 1) * F)
                    copy(wmix_two[half, half], wmix[half, :])

                def aggregates(g, part):
                    sl = slice(g * FIFTH, (g + 1) * FIFTH)
                    nmax, amax, asum, asq = (node_rows(PNA_W)[:, sl, k * F:(k + 1) * F] for k in range(4))
                    mean, mx, mn, _, var, s_ = (feats[:, sl, k * F:(k + 1) * F] for k in range(6))
                    if part == 0:
                        dve.wait_ge(nodes_in["pna"][g], (layer + 1) * 16 * FIFTH)
                        st.add(V.tensor_tensor(Z[:, sl, :], asum, over_t(rden[:, sl]), ALU.mult))
                        st.add(V.tensor_tensor(var, asq, over_t(rden[:, sl]), ALU.mult))
                    elif part == 1:
                        st.wait()
                        tt(Z[:, sl, :], Z[:, sl, :], Z[:, sl, :], ALU.mult)
                        st.add(V.tensor_tensor(s_, asum, Bd[:, sl, :], ALU.add))
                    elif part == 2:
                        st.add(V.tensor_tensor(var, var, Z[:, sl, :], ALU.subtract))
                        st.add(V.tensor_tensor(mx, amax, Bn[:, sl, :], ALU.add))
                    else:
                        st.wait()
                        st.add(V.tensor_scalar(var, var, 0.0, None, ALU.max))
                        st.add(V.tensor_tensor(mn, Bn[:, sl, :], nmax, ALU.subtract))
                        tt(mean, s_, over_t(rden[:, sl]), ALU.mult)
                        ask(False)

                for part in range(4):
                    aggregates(0, part)
                for g in range(5):
                    for s in range(g * FIFTH, (g + 1) * FIFTH):
                        ps = psO[(NG + s) % 2]
                        dve.wait_ge(base_ready, s + 1)
                        st.do(V.scalar_tensor_tensor(Y[:, s, :], ps[:, F:2 * F], amp[:, s:s + 1], Y[:, s, :],
                                                     ALU.mult, ALU.add))
                        st.do(V.scalar_tensor_tensor(Y[:, s, :], ps[:, 2 * F:3 * F], att[:, s:s + 1], Y[:, s, :],
                                                     ALU.mult, ALU.add))
                        dve.sem_inc(evacuated, 1)
                        if s < 2:
                            aggregates(1, 2 * s)
                            aggregates(1, 2 * s + 1)
                        elif 4 <= s < 16:
                            aggregates(s // 4 + 1, s % 4)
                    sl = slice(g * FIFTH, (g + 1) * FIFTH)
                    st.add(V.scalar_tensor_tensor(Y[:, sl, :], Y[:, sl, :], 1.0 / float(N) ** 0.5,
                                                  bc(par[:, 0, :].unsqueeze(1), [P, FIFTH, F]), ALU.mult, ALU.add))
                st.wait()
                batch_norm(Y[:, :, :], Z[:, :, :], par[:, 1, :], par[:, 2, :])
                dve.sem_inc(operands_ready, 1)

                def take_mix(sl, ps):
                    tt(Bn[:, sl, :], ps, bc(par[:, 3, :].unsqueeze(1), [P, sl.stop - sl.start, F]), ALU.add)
                    st.do(V.scalar_tensor_tensor(Bn[:, sl, :], Bn[:, sl, :], 0.01, Bn[:, sl, :], ALU.mult, ALU.max))
                    st.add(V.tensor_tensor(Z[:, sl, :], Bn[:, sl, :], Hn[:, sl, :], ALU.add))

                evacuate(NG + T, F, take_mix, BIG_GROUPS)
                batch_norm(Z[:, :, :], Y[:, :, :], par[:, 4, :], par[:, 5, :])
                st.do(V.scalar_tensor_tensor(Hn[:, :, :], Z[:, :, :], 0.0, Hn[:, :, :], ALU.max, ALU.add))
                end()

            def even_weights(k):
                st.add(V.memset(w_even[F:2 * F, :], 0.0))
                st.add(V.memset(w_odd[0:F, :], 0.0))
                copy(w_even[0:F, :], wrel[k][:, :])

            def evacuate_relations(w, take):
                for s in range(T):
                    tv = tab[:, s % 2, 0:REL * w].rearrange("p (r w) -> p r w", r=REL)
                    dve.wait_ge(product_done, s + 1)
                    if s >= 2:
                        dve.wait_ge(tab_stored[s % 2], 16 * (s // 2))
                    take(s, tv, psO[s % 2][:, :].rearrange("p (r w) -> p r w", r=REL), psS[s % 2])
                    st.wait()
                    dve.sem_inc(evacuated, 1)

            def take_rgat(s, tv, ps, small):
                st.add(V.tensor_copy(tv[:, :, 0:F], ps))
                st.add(V.tensor_copy(tv[:, :, F:], small[:, 0:32].rearrange("p (r w) -> p r w", r=REL)))
                st.add(V.tensor_copy(QN[:, s, :], small[:, 32:64]))

            for k in range(2):
                if k == 0:
                    tt(X[:, :, :], X[:, :, :], Hn[:, :, :], ALU.add)
                    layer_norm()
                even_weights(k)
                dve.sem_inc(operands_ready, 1)
                evacuate_relations(RGAT.GW, take_rgat)
                edge_attention(RGAT, f"rgat{k}")
                tt(Z[:, :, :], Z[:, :, :], over_f(brow[:, k, :]), ALU.add)
                if k == 0:
                    ts(Hn[:, :, :], Z[:, :, :], 0.0, ALU.max)
                else:
                    tt(X[:, :, :], X[:, :, :], Z[:, :, :], ALU.add)
                    layer_norm()
                end()

            def take_rgcn(s, tv, ps, small):
                st.add(V.tensor_tensor(tv, ps, bc(brow[:, 2, :].unsqueeze(1), [P, REL, F]), ALU.add))
                st.add(V.tensor_copy(Bn[:, s, :], small[:, 0:F]))

            even_weights(2)
            dve.sem_inc(operands_ready, 1)
            evacuate_relations(F, take_rgcn)
            n = SMALLB
            rv, mv = run_rows(F, n), messages(F, n)
            st.do(V.memset(rv[:, 1, n - 1, :], 0.0))
            st.reset()
            with dve.Fori(0, pairs(n)) as b:
                for h in range(2):
                    block_masks(b, h, n, wgt)
                    dve.wait_ge(rows_in["rgcn"][h], (b + 1) * 16 * n)
                    tt(mv[:, h], gath[:, h, 0:n, 0:F], bc(extra_now[:, 0:n].unsqueeze(2), [P, n, F]), ALU.mult)
                    dve.sem_inc(rows_free, 1)
                    dve.wait_ge(runs_free[h], b + 1)
                    for j in range(n):
                        before = rv[:, h, j - 1, :] if j else rv[:, 1 - h, n - 1, :]
                        st.do(V.scalar_tensor_tensor(rv[:, h, j, :], before, cont_now[:, j:j + 1], mv[:, h, j, :],
                                                     ALU.mult, ALU.add))
                    finish_block(h)
            st.do(V.memset(cD[:, 0:1], 0.0))
            ask_pe()
            st.do(scan(cD[0:F, 1:], contT[0:F, :], psT[0][0:F, 0:P], 0.0, ALU.mult, ALU.add))
            ask_pe()
            dve.wait_ge(fix_in["rgcn"], 16)
            tt(fixed[:, 0:F], psO[0][:, 0:F], fixed[:, 0:F], ALU.add)
            dve.sem_inc(fixed_ready, 1)
            dve.wait_ge(nodes_in["rgcn"][0], 16 * T)
            tt(Z[:, :, :], node_rows(F), Bn[:, :, :], ALU.add)
            tt(X[:, :, :], X[:, :, :], Z[:, :, :], ALU.add)
            dve.sem_inc(result_ready, 1)


_WEIGHTS = ("L0_gnn_W", "L0_gnn_a", "L1_gnn_WM", "L1_gnn_bM", "L1_gnn_WU", "L1_gnn_bU", "L1_gnn_gamma_t",
            "L1_gnn_beta_t", "L1_gnn_Wmix", "L1_gnn_bmix", "L1_gnn_gamma_o", "L1_gnn_beta_o", "L2_gnn_W1",
            "L2_gnn_Q1", "L2_gnn_K1", "L2_gnn_b1", "L2_gnn_W2", "L2_gnn_Q2", "L2_gnn_K2", "L2_gnn_b2",
            "L3_gnn_weight", "L3_gnn_h_bias", "L3_gnn_loop_weight")


def kernel(**inputs):
    import numpy as np
    import concourse.bacc as bacc
    from concourse import mybir as mb
    from concourse.bass_utils import run_bass_kernel_spmd

    def padded(a, n, fill=0):
        a = np.asarray(a)
        return np.concatenate([a, np.full((n - a.shape[0],) + a.shape[1:], fill, a.dtype)])

    def near_sources(n, pick):
        a = arrays["src"].reshape(P, C // n, n)[:, :, n - pick:]
        return padded(np.ascontiguousarray(a.transpose(1, 2, 0)).reshape(2 * pairs(BIGB), -1), 2 * pairs(BIGB) + 2)

    arrays = {
        "x": padded(inputs["x"], NP),
        "src": padded(inputs["src"], EP).reshape(P, C),
        "dst": np.concatenate([np.full((1,), -1, np.int32), padded(inputs["dst"], EP, N)]),
        "edge_type_8": padded(inputs["edge_type_8"], EP).reshape(P, C),
        "edge_weight1": padded(inputs["edge_weight1"], EP).reshape(P, C),
    }
    arrays["pna_near"] = near_sources(SMALLB, PICK)
    arrays["gat_near"] = near_sources(BIGB, GPICK)
    for name in _WEIGHTS:
        arrays[name] = np.ascontiguousarray(inputs[name])
    nc = bacc.Bacc("TRN2", target_bir_lowering=False, num_devices=1)
    t = {k: nc.dram_tensor(f"in_{k}", a.shape, mb.dt.from_np(a.dtype), kind="ExternalInput").ap()
         for k, a in arrays.items()}
    t["out"] = nc.dram_tensor("out_x", (NP, F), mb.dt.float32, kind="ExternalOutput").ap()
    gnn(nc, t)
    r = run_bass_kernel_spmd(nc, [{f"in_{k}": a for k, a in arrays.items()}], core_ids=[0])
    return r.results[0]["out_x"][0:N]
```
